# Optimizing a Trainium2 kernel written in Bass

```python
import numpy as np
import jax
import jax.numpy as jnp

def _softmax(x, axis=-1):
    return jax.nn.softmax(x, axis=axis)

def _gelu(x):
    return jax.nn.gelu(x, approximate=True)

def _silu(x):
    return jax.nn.silu(x)

def _sigmoid(x):
    return jax.nn.sigmoid(x)

def _layernorm(x, axis=-1, eps=1e-05):
    m = jnp.mean(x, axis=axis, keepdims=True)
    v = jnp.var(x, axis=axis, keepdims=True)
    return (x - m) / jnp.sqrt(v + eps)

def _scatter_add(tgt, idx, src, axis=0):
    return tgt.at[idx].add(src)

def _segment_sum(src, seg, n):
    return jax.ops.segment_sum(src, seg, n)
kernel_name = 'mk_xattn_ffn_d2_seqx_r8_90decf'

def setup_inputs(seed: int=0):
    np.random.seed(seed)
    _w = jnp.asarray

    def _rec_inputs():
        import jax
        import jax.numpy as jnp
        _rk = jax.random.key(seed)
        x = 7.22e-05 + 1 * jax.random.normal(jax.random.fold_in(_rk, 1), (8, 128, 128), jnp.float32)
        _lenS = 128 - jax.random.randint(jax.random.fold_in(_rk, 7), (8,), 0, max(1, 128 // 4) + 1, jnp.int32)
        _lenS2 = 77 - jax.random.randint(jax.random.fold_in(_rk, 8), (8,), 0, max(1, 77 // 4) + 1, jnp.int32)
        _ctx_1024P = jax.random.normal(jax.random.fold_in(_rk, 11), (8, 16, 128), jnp.float32)
        _ctx_1024c = jax.random.dirichlet(jax.random.fold_in(_rk, 511), 0.3 * jnp.ones((16,), jnp.float32), (8, 77))
        _ctx_1024t = jnp.einsum('bsk,bkd->bsd', _ctx_1024c, _ctx_1024P)
        _ctx_1024t = _ctx_1024t * jax.lax.rsqrt(jnp.mean(jnp.square(_ctx_1024t)) + 1e-12) * 0.953939
        ctx_1024 = 4.13588e-05 + 0.999923 * (_ctx_1024t + 0.3 * jax.random.normal(jax.random.fold_in(_rk, 611), (8, 77, 128), jnp.float32))
        _validS = jnp.arange(128)[None, :] < _lenS[:, None]
        _validS2 = jnp.arange(77)[None, :] < _lenS2[:, None]
        _causal = jnp.tril(jnp.ones((128, 128), dtype=bool))
        mask_Bx1xSxS2_bk1 = jnp.broadcast_to(_validS2[:, None, None, :], (8, 1, 128, 77))
        return (x, ctx_1024, mask_Bx1xSxS2_bk1)
    x, ctx_1024, mask_Bx1xSxS2_bk1 = _rec_inputs()

    def _L0_xattn_setup():
        import jax, jax.numpy as jnp
        import numpy as np
        B, S, D, H = (4, 256, 128, 16)
        HD = D // H
        key = jax.random.key(seed)
        ks = jax.random.split(key, 12)
        scale = 1.0 / np.sqrt(D)
        inp = {'queries': jax.random.normal(ks[0], (B, S, D), jnp.float32), 'keys': jax.random.normal(ks[1], (B, S, D), jnp.float32), 'values': jax.random.normal(ks[2], (B, S, D), jnp.float32), 'mask': jax.random.randint(ks[3], (B, 1, S, S), 0, 2).astype(bool), 'Wq': jax.random.normal(ks[4], (D, D), jnp.float32) * scale, 'bq': jnp.zeros((D,), jnp.float32), 'Wk': jax.random.normal(ks[5], (D, D), jnp.float32) * scale, 'bk': jnp.zeros((D,), jnp.float32), 'Wv': jax.random.normal(ks[6], (D, D), jnp.float32) * scale, 'bv': jnp.zeros((D,), jnp.float32), 'Wo': jax.random.normal(ks[7], (D, D), jnp.float32) * scale, 'bo': jnp.zeros((D,), jnp.float32)}
        return inp
    _L0_xattn_all = _L0_xattn_setup()
    _L0_xattn_in = {k: v for k, v in _L0_xattn_all.items() if k in ('Wq', 'bq', 'Wk', 'bk', 'Wv', 'bv', 'Wo', 'bo')}
    del _L0_xattn_all

    def _L0_ffn_setup():
        import jax, jax.numpy as jnp
        import numpy as np
        TOP_K = 2
        EPS = 1e-09
        key = jax.random.key(seed)
        ks = jax.random.split(key, 6)
        B, T, D, H, E = (4, 256, 128, 256, 8)
        x = jax.random.normal(ks[0], (B, T, D), dtype=jnp.float32)
        Wg = jax.random.normal(ks[1], (E, D), dtype=jnp.float32) * 0.02
        W1 = jax.random.normal(ks[2], (E, 2 * H, D), dtype=jnp.float32) * 0.02
        b1 = jax.random.normal(ks[3], (E, 2 * H), dtype=jnp.float32) * 0.02
        Wo = jax.random.normal(ks[4], (D, H), dtype=jnp.float32) * 0.02
        bo = jax.random.normal(ks[5], (D,), dtype=jnp.float32) * 0.02
        return {'x': x, 'Wg': Wg, 'W1': W1, 'b1': b1, 'Wo': Wo, 'bo': bo}
    _L0_ffn_all = _L0_ffn_setup()
    _L0_ffn_in = {k: v for k, v in _L0_ffn_all.items() if k in ('Wg', 'W1', 'b1', 'Wo', 'bo')}
    del _L0_ffn_all

    def _L1_xattn_setup():
        import jax, jax.numpy as jnp
        import numpy as np
        DIM = 128
        NUM_HEADS = 16
        DIM_HEAD = 64
        INNER = NUM_HEADS * DIM_HEAD
        SCALE = DIM_HEAD ** (-0.5)

        def _layernorm(x, gamma, beta, eps=1e-05):
            mu = jnp.mean(x, axis=-1, keepdims=True)
            var = jnp.mean(jnp.square(x - mu), axis=-1, keepdims=True)
            return (x - mu) * jax.lax.rsqrt(var + eps) * gamma + beta
        key = jax.random.key(seed)
        ks = jax.random.split(key, 8)
        B, SQ, SK = (2, 256, 512)
        x = jax.random.normal(ks[0], (B, SQ, DIM), dtype=jnp.float32)
        context = jax.random.normal(ks[1], (B, SK, DIM), dtype=jnp.float32)
        ln_gamma = jnp.ones((DIM,), jnp.float32)
        ln_beta = jnp.zeros((DIM,), jnp.float32)
        w_q = jax.random.normal(ks[2], (DIM, INNER), dtype=jnp.float32) / np.sqrt(DIM)
        w_kv = jax.random.normal(ks[3], (DIM, 2 * INNER), dtype=jnp.float32) / np.sqrt(DIM)
        w_out = jax.random.normal(ks[4], (INNER, DIM), dtype=jnp.float32) / np.sqrt(INNER)
        b_out = jnp.zeros((DIM,), jnp.float32)
        gate = jnp.array([0.5], jnp.float32)
        return {'x': x, 'context': context, 'ln_gamma': ln_gamma, 'ln_beta': ln_beta, 'w_q': w_q, 'w_kv': w_kv, 'w_out': w_out, 'b_out': b_out, 'gate': gate}
    _L1_xattn_all = _L1_xattn_setup()
    _L1_xattn_in = {k: v for k, v in _L1_xattn_all.items() if k in ('ln_gamma', 'ln_beta', 'w_q', 'w_kv', 'w_out', 'b_out', 'gate')}
    del _L1_xattn_all

    def _L1_ffn_setup():
        import jax, jax.numpy as jnp
        import numpy as np
        B, S, H = (2, 256, 128)
        E, K, F_EXP, F_SHARED = (16, 2, 64, 128)
        key = jax.random.key(seed)
        ks = jax.random.split(key, 9)
        sc = 1.0 / np.sqrt(H)
        scf = 1.0 / np.sqrt(F_EXP)
        scfs = 1.0 / np.sqrt(F_SHARED)
        return {'x': jax.random.normal(ks[0], (B, S, H), dtype=jnp.float32), 'router_w': jax.random.normal(ks[1], (H, E), dtype=jnp.float32) * sc, 'gate_w': jax.random.normal(ks[2], (E, H, F_EXP), dtype=jnp.float32) * sc, 'up_w': jax.random.normal(ks[3], (E, H, F_EXP), dtype=jnp.float32) * sc, 'down_w': jax.random.normal(ks[4], (E, F_EXP, H), dtype=jnp.float32) * scf, 'shared_gate_w': jax.random.normal(ks[5], (H, F_SHARED), dtype=jnp.float32) * sc, 'shared_up_w': jax.random.normal(ks[6], (H, F_SHARED), dtype=jnp.float32) * sc, 'shared_down_w': jax.random.normal(ks[7], (F_SHARED, H), dtype=jnp.float32) * scfs}
    _L1_ffn_all = _L1_ffn_setup()
    _L1_ffn_in = {k: v for k, v in _L1_ffn_all.items() if k in ('router_w', 'gate_w', 'up_w', 'down_w', 'shared_gate_w', 'shared_up_w', 'shared_down_w')}
    del _L1_ffn_all
    return {'x': x, 'ctx_1024': ctx_1024, 'mask_Bx1xSxS2_bk1': mask_Bx1xSxS2_bk1, 'L0_xattn_Wq': _L0_xattn_in['Wq'], 'L0_xattn_bq': _L0_xattn_in['bq'], 'L0_xattn_Wk': _L0_xattn_in['Wk'], 'L0_xattn_bk': _L0_xattn_in['bk'], 'L0_xattn_Wv': _L0_xattn_in['Wv'], 'L0_xattn_bv': _L0_xattn_in['bv'], 'L0_xattn_Wo': _L0_xattn_in['Wo'], 'L0_xattn_bo': _L0_xattn_in['bo'], 'L0_ffn_Wg': _L0_ffn_in['Wg'], 'L0_ffn_W1': _L0_ffn_in['W1'], 'L0_ffn_b1': _L0_ffn_in['b1'], 'L0_ffn_Wo': _L0_ffn_in['Wo'], 'L0_ffn_bo': _L0_ffn_in['bo'], 'L1_xattn_ln_gamma': _L1_xattn_in['ln_gamma'], 'L1_xattn_ln_beta': _L1_xattn_in['ln_beta'], 'L1_xattn_w_q': _L1_xattn_in['w_q'], 'L1_xattn_w_kv': _L1_xattn_in['w_kv'], 'L1_xattn_w_out': _L1_xattn_in['w_out'], 'L1_xattn_b_out': _L1_xattn_in['b_out'], 'L1_xattn_gate': _L1_xattn_in['gate'], 'L1_ffn_router_w': _L1_ffn_in['router_w'], 'L1_ffn_gate_w': _L1_ffn_in['gate_w'], 'L1_ffn_up_w': _L1_ffn_in['up_w'], 'L1_ffn_down_w': _L1_ffn_in['down_w'], 'L1_ffn_shared_gate_w': _L1_ffn_in['shared_gate_w'], 'L1_ffn_shared_up_w': _L1_ffn_in['shared_up_w'], 'L1_ffn_shared_down_w': _L1_ffn_in['shared_down_w']}

def reference(x, ctx_1024, mask_Bx1xSxS2_bk1, L0_xattn_Wq, L0_xattn_bq, L0_xattn_Wk, L0_xattn_bk, L0_xattn_Wv, L0_xattn_bv, L0_xattn_Wo, L0_xattn_bo, L0_ffn_Wg, L0_ffn_W1, L0_ffn_b1, L0_ffn_Wo, L0_ffn_bo, L1_xattn_ln_gamma, L1_xattn_ln_beta, L1_xattn_w_q, L1_xattn_w_kv, L1_xattn_w_out, L1_xattn_b_out, L1_xattn_gate, L1_ffn_router_w, L1_ffn_gate_w, L1_ffn_up_w, L1_ffn_down_w, L1_ffn_shared_gate_w, L1_ffn_shared_up_w, L1_ffn_shared_down_w):
    import jax
    import jax.numpy as jnp

    def _L0_xattn_ref(queries, keys, values, mask, Wq, bq, Wk, bk, Wv, bv, Wo, bo):
        import jax, jax.numpy as jnp
        import numpy as np
        B, S, D, H = (4, 256, 128, 16)
        HD = D // H
        b, sq, d = queries.shape

        def split_heads(x):
            return x.reshape(b, x.shape[1], H, HD).transpose(0, 2, 1, 3)
        q = split_heads(queries @ Wq + bq)
        k = split_heads(keys @ Wk + bk)
        v = split_heads(values @ Wv + bv)
        scores = jnp.einsum('bhqd,bhkd->bhqk', q, k) / jnp.sqrt(jnp.float32(HD))
        scores = jnp.where(mask, jnp.float32(-1000000000000000.0), scores)
        attn = jax.nn.softmax(scores, axis=-1)
        ctx = jnp.einsum('bhqk,bhkd->bhqd', attn, v)
        ctx = ctx.transpose(0, 2, 1, 3).reshape(b, sq, d)
        return ctx @ Wo + bo

    def _L0_ffn_ref(x, Wg, W1, b1, Wo, bo):
        import jax, jax.numpy as jnp
        import numpy as np
        TOP_K = 2
        EPS = 1e-09
        E = Wg.shape[0]
        gate_logits = jnp.einsum('btd,ed->bte', x, Wg)
        gate_scores = jax.nn.softmax(gate_logits, axis=-1)
        topk_val, topk_idx = jax.lax.top_k(gate_scores, TOP_K)
        topk_val = topk_val / (topk_val.sum(axis=-1, keepdims=True) + EPS)
        comb = (jax.nn.one_hot(topk_idx, E, dtype=x.dtype) * topk_val[..., None]).sum(axis=-2)
        out = jnp.zeros_like(x)
        for e in range(E):
            h = jnp.einsum('btd,hd->bth', x, W1[e]) + b1[e]
            a, b = jnp.split(h, 2, axis=-1)
            g = a * jax.nn.sigmoid(b)
            eo = jnp.einsum('bth,dh->btd', g, Wo) + bo
            out = out + eo * comb[..., e:e + 1]
        return out

    def _L1_xattn_ref(x, context, ln_gamma, ln_beta, w_q, w_kv, w_out, b_out, gate):
        import jax, jax.numpy as jnp
        import numpy as np
        DIM = 128
        NUM_HEADS = 16
        DIM_HEAD = 64
        INNER = NUM_HEADS * DIM_HEAD
        SCALE = DIM_HEAD ** (-0.5)

        def _layernorm(x, gamma, beta, eps=1e-05):
            mu = jnp.mean(x, axis=-1, keepdims=True)
            var = jnp.mean(jnp.square(x - mu), axis=-1, keepdims=True)
            return (x - mu) * jax.lax.rsqrt(var + eps) * gamma + beta
        B, SQ, _ = x.shape
        SK = context.shape[1]
        xn = _layernorm(x, ln_gamma, ln_beta)
        q = (xn @ w_q).reshape(B, SQ, NUM_HEADS, DIM_HEAD)
        kv = context @ w_kv
        k, v = jnp.split(kv, 2, axis=-1)
        k = k.reshape(B, SK, NUM_HEADS, DIM_HEAD)
        v = v.reshape(B, SK, NUM_HEADS, DIM_HEAD)
        scores = jnp.einsum('bqhd,bkhd->bhqk', q * SCALE, k)
        attn = jax.nn.softmax(scores, axis=-1)
        out = jnp.einsum('bhqk,bkhd->bqhd', attn, v).reshape(B, SQ, INNER)
        out = out @ w_out + b_out
        return out * jnp.tanh(gate[0])

    def _L1_ffn_ref(x, router_w, gate_w, up_w, down_w, shared_gate_w, shared_up_w, shared_down_w):
        import jax, jax.numpy as jnp
        import numpy as np
        B, S, H = (2, 256, 128)
        E, K, F_EXP, F_SHARED = (16, 2, 64, 128)
        b, s, h = x.shape
        T = b * s
        x_flat = x.reshape(T, h)
        shared_out = jax.nn.silu(x @ shared_gate_w) * (x @ shared_up_w) @ shared_down_w
        router_probs = jax.nn.softmax(x_flat @ router_w, axis=-1)
        topk_probs, topk_idx = jax.lax.top_k(router_probs, K)
        coeff = jnp.einsum('tk,tke->te', topk_probs, jax.nn.one_hot(topk_idx, E, dtype=x.dtype))

        def expert_step(acc, ws):
            g, u, d, c = ws
            inter = jax.nn.silu(x_flat @ g) * (x_flat @ u)
            return (acc + inter @ d * c[:, None], None)
        routed, _ = jax.lax.scan(expert_step, jnp.zeros((T, h), dtype=x.dtype), (gate_w, up_w, down_w, coeff.T))
        return routed.reshape(b, s, h) + shared_out
    x = x + _L0_xattn_ref(_layernorm(x, axis=-1), ctx_1024, ctx_1024, mask_Bx1xSxS2_bk1, L0_xattn_Wq, L0_xattn_bq, L0_xattn_Wk, L0_xattn_bk, L0_xattn_Wv, L0_xattn_bv, L0_xattn_Wo, L0_xattn_bo)
    x = x + _L0_ffn_ref(_layernorm(x, axis=-1), L0_ffn_Wg, L0_ffn_W1, L0_ffn_b1, L0_ffn_Wo, L0_ffn_bo)
    x = x + _L1_xattn_ref(_layernorm(x, axis=-1), ctx_1024, L1_xattn_ln_gamma, L1_xattn_ln_beta, L1_xattn_w_q, L1_xattn_w_kv, L1_xattn_w_out, L1_xattn_b_out, L1_xattn_gate)
    x = x + _L1_ffn_ref(_layernorm(x, axis=-1), L1_ffn_router_w, L1_ffn_gate_w, L1_ffn_up_w, L1_ffn_down_w, L1_ffn_shared_gate_w, L1_ffn_shared_up_w, L1_ffn_shared_down_w)
    return x

_drawn_inputs = setup_inputs


def setup_inputs(seed=0):
    import zlib

    import numpy as np

    out = dict(_drawn_inputs(seed))
    spreads = {'L0_xattn_bq': (0.0, 0.1),
     'L0_xattn_bk': (0.0, 2.0),
     'L0_xattn_bv': (0.0, 0.1),
     'L0_xattn_bo': (0.0, 0.1),
     'L1_xattn_ln_gamma': (1.0, 0.6),
     'L1_xattn_ln_beta': (0.0, 0.55),
     'L1_xattn_b_out': (0.0, 0.1)}
    factors = {'L0_ffn_b1': 21.721}
    for name, (base, spread) in spreads.items():
        noise = np.random.default_rng([zlib.crc32(name.encode()), seed]).standard_normal(out[name].shape)
        drawn = base * np.exp(spread * noise) if base else spread * noise
        out[name] = jnp.asarray(drawn.astype(out[name].dtype))
    for name, factor in factors.items():
        out[name] = (out[name] * factor).astype(out[name].dtype)
    return out
```

```python
from contextlib import ExitStack

import concourse.bass as bass
from concourse import mybir

B, S, D, K, H = 8, 128, 128, 77, 16
HK = H * K
KC = (HK + 127) // 128
KLAST = HK - 128 * (KC - 1)
HD = D // H
OW = HD + 1
NK = B * K
NKH = NK // 2
E0, F0 = 8, 256
EP = 4
E1, F1, FS = 16, 64, 128
EI = E1 * F1
IC = (EI + FS) // 128
HEADS = [(0, 5), (5, 10), (10, 16)]
CHUNKS = [(0, 4), (4, 8), (8, 10)]
ICHUNKS = [(0, 4), (4, 8), (8, 9)]
EPS, EPS_TOP = 1e-5, 1e-9
MASKED = -1e15
BIG = 3.0e38


def rows_of(c):
    return 128 if c < KC - 1 else KLAST


class Tile:

    def __init__(self, n, odd):
        self.n, self.odd = n, odd

    def back(self, k):
        return Tile(self.n - k, (self.odd + k) % 2)

    def pairs(self, per):
        return (self.n - self.odd) * (per // 2)

    def live(self):
        return not isinstance(self.n, int) or 0 <= self.n < B


def steps(eng, lag, step):
    for n in range(2):
        step(Tile(n, n % 2))
    with eng.Fori(0, (B - 2) // 2) as i:
        for odd in range(2):
            step(Tile(i * 2 + (2 + odd), odd))
    for n in range(B, B + lag):
        step(Tile(n, n % 2))


def wait(eng, sem, value):
    if not isinstance(value, int) or value > 0:
        eng.wait_ge(sem, value)


class Chain:

    def __init__(self, eng, sem, per):
        self.eng, self.sem, self.per, self.t, self.k = eng, sem, per, None, 0

    def start(self, t):
        assert self.t is None or self.k == self.per
        self.t, self.k = t, 0

    def link(self, ins):
        self.k += 1
        ins.then_inc(self.sem, 1)
        self.eng.wait_ge(self.sem, self.t.n * self.per + self.k)


def settle(eng, ins=None):
    eng.drain()


def build(nc, x, ctx_t, mask, w0, cols, rows, w1, b1, wg, wo0, wq, wk, wv, wout, gate, gu, rsh, down,
          ident, hmask, vmask, out):
    f32, f32r, bf16, u8 = mybir.dt.float32, mybir.dt.float32r, mybir.dt.bfloat16, mybir.dt.uint8
    ALU, ACT, AX = mybir.AluOpType, mybir.ActivationFunctionType, mybir.AxisListType
    vw_dram = nc.dram_tensor("vw_scratch", [B, HK, D], f32, kind="Internal").ap()

    with ExitStack() as stack:
        def sb(name, shape, dt=f32, on=stack):
            return on.enter_context(nc.sbuf_tensor(name, shape, dt))

        def sem(name):
            return stack.enter_context(nc.semaphore(name))

        bank = [stack.enter_context(nc.psum_tensor(f"bank{i}", [128, 512], f32)) for i in range(8)]

        xr = sb("xr", [128, B, D])
        rows_s = sb("rows_s", [128, 3, D])
        w0_s = sb("w0_s", [128, 4, D])
        wo0_s = sb("wo0_s", [128, 2, D])
        id_s = sb("id_s", [128, 2, 128])
        idb = sb("idb", [128, 128], bf16)
        hmask_s = sb("hmask_s", [128, H])
        vmask_s = sb("vmask_s", [128, KC, D], u8)
        maskneg = sb("maskneg", [128, B, K], bf16)
        k_t = sb("k_t", [128, NK])
        v_t = sb("v_t", [128, NK])
        q_t = sb("q_t", [128, B * S])
        xn_t = sb("xn_t", [128, B * S])
        wgt = sb("wgt", [128, E0])
        tanh_g = sb("tanh_g", [128, 1])
        b_all = sb("b_all", [128, B, HK])
        w1_hi, w1_lo = sb("w1_hi", [128, E0, 512], f32r), sb("w1_lo", [128, E0, 512], f32r)
        lhs = sb("lhs", [128, 2, 128])
        lhs_hi, lhs_lo = sb("lhs_hi", [128, 2, 128], f32r), sb("lhs_lo", [128, 2, 128], f32r)
        mx, rs = sb("mx", [128, 2, H]), sb("rs", [128, 2, H])
        rinv = sb("rinv", [128, 2, H])
        o_n = sb("o_n", [128, 2, H, HD])
        ot = sb("ot", [128, 2, 256])
        xh = sb("xh", [128, 2, D])
        st, ag = sb("st", [128, 2, 6]), sb("ag", [128, 2, 2])
        var, scale = sb("var", [128, 2]), sb("scale", [128, 2])
        ag8, var8, scale8 = sb("ag8", [128, B, 2]), sb("var8", [128, B]), sb("scale8", [128, B])
        one = sb("one", [1, 128])
        root = sb("root", [128, B])
        lg, lr = sb("lg", [128, 24]), sb("lr", [128, 24])
        top, mark = sb("top", [128, 8]), sb("mark", [128, 8])
        ee, es, sel = sb("ee", [128, 2, E1]), sb("es", [128, E1]), sb("sel", [128, E1])
        neg, ssum, s2 = sb("neg", [128, 2]), sb("ssum", [128, 2]), sb("s2", [128, 4])
        comb, csum = sb("comb", [128, 2, E1]), sb("csum", [128, 2])
        yb = sb("yb", [128, 2, D])

        with ExitStack() as early:
            ctx_s = sb("ctx_s", [128, NK], on=early)
            mask_s = sb("mask_s", [128, B, K], u8, on=early)
            cols_s = sb("cols_s", [128, 5], on=early)
            w1_s = sb("w1_s", [128, 32, D], on=early)
            w1f = sb("w1f", [128, 2, 4, D], on=early)
            w127 = sb("w127", [E0, 1], on=early)
            b1_s = sb("b1_s", [128, 32], on=early)
            wg_s = sb("wg_s", [E0, D], on=early)
            wq_s = sb("wq_s", [128, H * 64], on=early)
            wk_s = sb("wk_s", [128, 8, D], on=early)
            wv_s = sb("wv_s", [128, 8, D], on=early)
            wout_s = sb("wout_s", [128, 8, D], on=early)
            gate_s = sb("gate_s", [128, 1], on=early)
            tt = sb("tt", [128, D], on=early)
            ctx_hi, ctx_lo = sb("ctx_hi", [128, NK], f32r, early), sb("ctx_lo", [128, NK], f32r, early)
            cb_hi, cb_lo = sb("cb_hi", [128, 2, K], f32r, early), sb("cb_lo", [128, 2, K], f32r, early)
            m_hi, m_lo = sb("m_hi", [128, H * D], f32r, early), sb("m_lo", [128, H * D], f32r, early)
            with ExitStack() as first:
                pair_q = sb("pair_q", [128, 8, 2, D], on=first)
                pair_o = sb("pair_o", [128, 8, 2, D], on=first)
                xh0 = sb("xh0", [128, B, D], on=first)
                a_hi, a_lo = sb("a_hi", [128, H * D], f32r, first), sb("a_lo", [128, H * D], f32r, first)
            vws = sb("vws", [K, 2, 4, 512], on=early)
        p = sb("p", [128, 2, HK])
        pt = sb("pt", [128, 2, KC, 128])
        vw = sb("vw", [128, 2, KC, D])
        gu_s = sb("gu_s", [128, 2 * EI])
        rsh_s = sb("rsh_s", [128, 2 * FS + E1])
        down_s = sb("down_s", [128, IC, D])
        wide_hi = sb("wide_hi", [128, 2 * EI + 2 * FS + E1], f32r)
        wide_lo = sb("wide_lo", [128, 2 * EI + 2 * FS + E1], f32r)
        with ExitStack() as phase_a:
            vbd = sb("vbd", [128, 2, KC, H * OW], on=phase_a)
            kbd = sb("kbd", [128, 2, HK], on=phase_a)
            vper = sb("vper", [128, 2, 3, K], on=phase_a)
        with ExitStack() as phase_b:
            th = sb("th", [128, 4, F0], on=phase_b)
            ub = sb("ub", [128, E0, F0], on=phase_b)
            gb = sb("gb", [128, 2, F0], on=phase_b)
            part = sb("part", [128, EP, F0], on=phase_b)
        tg = sb("tg", [128, 3, 512])
        z1 = sb("z1", [128, 3, 512])
        z2 = sb("z2", [128, 2, 512])
        inter = sb("inter", [128, 2, EI + FS])
        it = pt

        names = ("ctx", "w0", "cols", "x", "ident", "wq", "wout", "gate", "wk", "wv", "wg", "rows", "mask",
                 "hmask", "w1", "b1", "vmask", "wo0", "gu", "rsh", "down")
        load = {n: sem("load_" + n) for n in names}

        def loaded(eng, *which):
            for n in which:
                eng.wait_ge(load[n], 16)

        first_ready = [sem(f"first_ready{i}") for i in range(8)]
        first_done = [sem(f"first_done{i}") for i in range(8)]
        hi_done = sem("hi_done")
        dve_first, act_first, pool_first = sem("dve_first"), sem("act_first"), sem("pool_first")
        tt_done, ctx_split, xh0_done, wg_done = sem("tt_done"), sem("ctx_split"), sem("xh0_done"), sem("wg_done")
        bd_zero, w1_done, consts_done, tanh_done = sem("bd_zero"), sem("w1_done"), sem("consts_done"), sem("tanh_done")
        outw_done, bias0_done = sem("outw_done"), sem("bias0_done")
        cb_done, vw_ready, vw_act, vw_dve, vw_stored = (
            sem("cb_done"), sem("vw_ready"), sem("vw_act"), sem("vw_dve"), [sem("vw_stored0"), sem("vw_stored1")])
        w1t_ready, w1t_hi, w1t_done = sem("w1t_ready"), sem("w1t_hi"), sem("w1t_done")
        ones_done = sem("ones_done")
        a_prep, a_sub, a_exp, a_scores = sem("a_prep"), sem("a_sub"), sem("a_exp"), sem("a_scores")
        a_ready = {i: sem(f"a_ready{i}") for i in range(3, 8)}
        a_done = {i: sem(f"a_done{i}") for i in range(3, 8)}
        a_norm, a_xh = sem("a_norm"), sem("a_xh")
        a_chain, a_chain_y = sem("a_chain"), sem("a_chain_y")
        b_prep_hi, b_prep = sem("b_prep_hi"), sem("b_prep")
        b_lg, b_lg_done, b_h, b_tanh, b_u, b_acc = (
            sem("b_lg"), sem("b_lg_done"), sem("b_h"), sem("b_tanh"), sem("b_u"), sem("b_acc"))
        b_neg, b_exp, b_comb = sem("b_neg"), sem("b_exp"), sem("b_comb")
        b_part, b_sum = sem("b_part"), sem("b_sum")
        var8_done, scale8_done = sem("var8_done"), sem("scale8_done")
        a_var, a_scale, b_var, b_scale, c_var, c_scale = (
            sem("a_var"), sem("a_scale"), sem("b_var"), sem("b_scale"), sem("c_var"), sem("c_scale"))
        b_gt, b_gt_done, b_y, b_y_done, b_xh, b_xt, b_xt_done = (
            sem("b_gt"), sem("b_gt_done"), sem("b_y"), sem("b_y_done"), sem("b_xh"), sem("b_xt"), sem("b_xt_done"))
        b_chain, b_chain_y = sem("b_chain"), sem("b_chain_y")
        wide_act, wide_done = sem("wide_act"), sem("wide_done")
        c_prep, c_scores, c_sub, c_exp, c_rs, c_norm = (
            sem("c_prep"), sem("c_scores"), sem("c_sub"), sem("c_exp"), sem("c_rs"), sem("c_norm"))
        c_vw = [sem("c_vw0"), sem("c_vw1")]
        c_bias0 = sem("c_bias0")
        c_pt3, c_pt4, c_pt3_done, c_pt4_done = sem("c_pt3"), sem("c_pt4"), sem("c_pt3_done"), sem("c_pt4_done")
        c_y, c_y_done, c_xh, c_xt, c_xt_done = sem("c_y"), sem("c_y_done"), sem("c_xh"), sem("c_xt"), sem("c_xt_done")
        c_chain, c_chain_y = sem("c_chain"), sem("c_chain_y")
        d_prep_hi, d_prep = sem("d_prep_hi"), sem("d_prep")
        d_sh, d_gu, d_tanh, d_tanh_sh, d_z, d_sh_done, d_mul = (
            sem("d_sh"), sem("d_gu"), sem("d_tanh"), sem("d_tanh_sh"), sem("d_z"), sem("d_sh_done"), sem("d_mul"))
        d_neg, d_exp, d_comb = sem("d_neg"), sem("d_exp"), sem("d_comb")
        d_it5, d_it6, d_it5_done, d_it6_done = sem("d_it5"), sem("d_it6"), sem("d_it5_done"), sem("d_it6_done")
        scores_max, d_lg_done, d_z1 = sem("scores_max"), sem("d_lg_done"), sem("d_z1")
        d_y, d_y_done, d_out, d_chain = sem("d_y"), sem("d_y_done"), [sem("d_out0"), sem("d_out1")], sem("d_chain")

        G_K, G_V, G_WQ, G_A, G_M, G_XT, G_Q, G_WG, G_B = 0, 2, 4, 6, 10, 14, 16, 18, 19
        N_B = 2 * H
        N_FIRST = G_B + N_B

        def columns(tensor, t, width):
            return tensor[:, bass.ds(t.n * width, width)]

        def tile_of(tensor, t):
            if isinstance(t.n, int):
                return tensor[:, t.n, :]
            return tensor[:, bass.ds(t.n, 1), :].rearrange("p o d -> p (o d)")

        block = stack.enter_context(nc.Block())

        @block.sync
        def _(sp):
            srcs = {"ctx": (ctx_s[:, :], ctx_t), "w0": (w0_s[:, :, :], w0), "cols": (cols_s[:, :], cols),
                    "ident": (id_s[:, :, :], ident), "wq": (wq_s[:, :], wq), "wk": (wk_s[:, :, :], wk),
                    "gate": (gate_s[:, :], gate.broadcast_to([128, 1])), "wout": (wout_s[:, :, :], wout),
                    "wv": (wv_s[:, :, :], wv),
                    "wg": (wg_s[:, :], wg), "w1": (w1_s[:, :, :], w1), "b1": (b1_s[:, :], b1)}
            for n, (dst, src) in srcs.items():
                sp.dma_start(dst, src).then_inc(load[n], 16)

            def store(t):
                sp.wait_ge(vw_act, t.n * 2 + 2)
                sp.wait_ge(vw_dve, t.n * 2 + 2)
                dst = vw_dram[bass.ds(t.n, 1), :, :].rearrange("o (h k) d -> k (o h) d", h=H)
                sp.dma_start(dst, vws[:, t.odd, :, :].rearrange("k a (h d) -> k (a h) d", h=4)).then_inc(vw_stored[t.odd], 16)

            steps(sp, 0, store)

            for stored in vw_stored:
                sp.wait_ge(stored, 16 * (B // 2))
            sp.wait_ge(w1t_ready, B)
            sp.wait_ge(w1t_done, B)
            sp.dma_start(gu_s[:, :], gu).then_inc(load["gu"], 16)
            sp.dma_start(rsh_s[:, :], rsh).then_inc(load["rsh"], 16)
            sp.dma_start(down_s[:, :, :], down).then_inc(load["down"], 16)

            def fetch(t):
                wait(sp, c_y, t.n - 1)
                src = vw_dram[bass.ds(t.n, 1), :, :]
                sp.dma_start(vw[:, t.odd, 0:KC - 1, :],
                             src[:, 0:128 * (KC - 1), :].rearrange("o (c p) d -> p (o c) d", p=128)
                             ).then_inc(c_vw[t.odd], 16)
                sp.dma_start(vw[0:KLAST, t.odd, KC - 1, :],
                             src[:, 128 * (KC - 1):HK, :].rearrange("o p d -> p (o d)")
                             ).then_inc(c_vw[t.odd], 16)

            steps(sp, 0, fetch)

            def result(t):
                sp.wait_ge(d_y_done, t.n + 1)
                sp.dma_start(out[bass.ds(t.n, 1), :, :].rearrange("o s d -> s (o d)"),
                             yb[:, t.odd, :]).then_inc(d_out[t.odd], 16)

            steps(sp, 0, result)
            for s in d_out:
                sp.wait_ge(s, 16 * (B // 2))

        @block.gpsimd
        def _(pool):
            ps = nc.gpsimd
            own = [0]

            def link(ins):
                own[0] += 1
                ins.then_inc(pool_first, 1)
                pool.wait_ge(pool_first, own[0])

            for buf in (pair_q, pair_o):
                ps.memset(buf[:, :, :, :], 0.0).then_inc(bd_zero, 1)
            link(ps.memset(root[:, :], -0.5))

            def inverse_root(t, var_sem, scale_sem):
                pool.wait_ge(var_sem, t.n + 1)
                u = slice(t.odd, t.odd + 1)
                ps.tensor_tensor(scale[:, u], var[:, u], root[:, 0:1], ALU.pow).then_inc(scale_sem, 1)

            pool.wait_ge(var8_done, 1)
            ps.tensor_tensor(scale8[:, :], var8[:, :], root[:, :], ALU.pow).then_inc(scale8_done, 1)
            loaded(pool, "wg")
            link(ps.tensor_copy(w127[:, 0:1], wg_s[:, D - 1:D]))
            link(ps.tensor_tensor(wg_s[:, 0:D - 1], wg_s[:, 0:D - 1],
                                  w127[:, 0:1].broadcast_to([E0, D - 1]), ALU.subtract))
            ps.memset(wg_s[:, D - 1:D], 0.0).then_inc(wg_done, 1)
            loaded(pool, "rows")
            pool.wait_ge(xh0_done, B)
            ps.tensor_tensor(xr[:, :, :], xr[:, :, :], rows_s[:, 0:1, :].broadcast_to([128, B, D]),
                             ALU.add).then_inc(bias0_done, 1)

            pool.wait_ge(ctx_split, 2)

            def context(t):
                wait(pool, vw_ready, (t.n - 1) * 4)
                ps.tensor_copy(cb_hi[:, t.odd, :], columns(ctx_hi, t, K))
                ps.tensor_copy(cb_lo[:, t.odd, :], columns(ctx_lo, t, K)).then_inc(cb_done, 1)
                wait(pool, w1t_ready, t.n - 1)
                rows4 = w1_s[:, bass.ds(t.n * 4, 4), :]
                ps.tensor_tensor(w1f[:, t.odd, :, 0:D - 1], rows4[:, :, 0:D - 1],
                                 rows4[:, :, D - 1:D].broadcast_to([128, 4, D - 1]), ALU.subtract)
                ps.tensor_copy(w1f[:, t.odd, :, D - 1], b1_s[:, bass.ds(t.n * 4, 4)]).then_inc(w1_done, 1)

            loaded(pool, "w1", "b1")
            steps(pool, 0, context)

            pool.wait_ge(w1t_ready, B)
            pool.wait_ge(w1t_done, B)
            for stored in vw_stored:
                pool.wait_ge(stored, 16 * (B // 2))
            pool.wait_ge(first_done[(G_Q + 1) % 8], (G_Q + 1) // 8 + 1)
            pool.wait_ge(first_done[G_Q % 8], G_Q // 8 + 1)
            loaded(pool, "hmask")

            def step_a(t):
                if t.live():
                    prep_a(t)
                if t.back(2).live():
                    inverse_root(t.back(2), a_var, a_scale)

            def prep_a(t):
                wait(pool, a_ready[5], (t.n - 1) * 2)
                ps.tensor_copy(lhs[:, t.odd, :], columns(q_t, t, S))
                ps.tensor_tensor(kbd[:, t.odd, :].rearrange("p (h k) -> p h k", h=H),
                                 columns(k_t, t, K).unsqueeze(1).broadcast_to([128, H, K]),
                                 hmask_s[:, :].unsqueeze(2).broadcast_to([128, H, K]), ALU.mult)
                ps.tensor_copy(vper[:, t.odd, :, :],
                               columns(v_t, t, K).unsqueeze(1).broadcast_to([128, 3, K])).then_inc(a_prep, 1)

            steps(pool, 2, step_a)

            def step_b(t):
                if t.live():
                    pool.wait_ge(b_u, t.n * E0 + EP)
                    pool.wait_ge(b_comb, t.n + 1)
                    ps.tensor_tensor(part[:, :, :], ub[:, 0:EP, :],
                                     comb[:, t.odd, 0:EP].unsqueeze(2).broadcast_to([128, EP, F0]),
                                     ALU.mult).then_inc(b_part, 1)
                    pool.wait_ge(b_part, t.n * 2 + 1)
                    ps.tensor_tensor(part[:, 0:2, :], part[:, 0:2, :], part[:, 2:4, :], ALU.add).then_inc(b_part, 1)
                    pool.wait_ge(b_part, t.n * 2 + 2)
                    wait(pool, b_gt, t.n - 1)
                    ps.tensor_tensor(gb[:, t.odd, :], part[:, 0, :], part[:, 1, :], ALU.add).then_inc(b_acc, 1)
                if t.back(1).live():
                    inverse_root(t.back(1), b_var, b_scale)

            steps(pool, 1, step_b)

            loaded(pool, "gu", "rsh")
            pool.wait_ge(wide_act, 2)
            ps.tensor_tensor(wide_lo[:, 0:2 * EI], gu_s[:, :], wide_hi[:, 0:2 * EI].bitcast(f32),
                             ALU.subtract)
            ps.tensor_tensor(wide_lo[:, 2 * EI:], rsh_s[:, :], wide_hi[:, 2 * EI:].bitcast(f32),
                             ALU.subtract).then_inc(wide_done, 1)
            pool.wait_ge(tanh_done, 1)
            ps.memset(one[0:1, :], 1.0)
            ps.tensor_scalar(rows_s[:, 2, :], rows_s[:, 2, :], tanh_g[:, 0:1], None, ALU.mult).then_inc(c_bias0, 1)

            def step_c(t):
                if t.live():
                    pool.wait_ge(b_xt_done, t.n + 1)
                    wait(pool, c_scores, (t.n - 1) * 3)
                    ps.tensor_copy(lhs[:, t.odd, :], columns(xn_t, t, S)).then_inc(c_prep, 1)
                if t.back(1).live():
                    q = t.back(1)
                    pool.wait_ge(c_rs, q.n + 1)
                    pq = p[:, q.odd, :].rearrange("p (h k) -> p h k", h=H)
                    ps.tensor_tensor(pq, pq, rinv[:, q.odd, :].unsqueeze(2).broadcast_to([128, H, K]),
                                     ALU.mult).then_inc(c_norm, 1)
                if t.back(2).live():
                    inverse_root(t.back(2), c_var, c_scale)

            steps(pool, 2, step_c)

            def weigh(t, half):
                pool.wait_ge(d_z, t.n * 2 + half + 1)
                pool.wait_ge(d_comb, t.n + 1)
                if half == 0:
                    wait(pool, d_it6, t.n - 1)
                    wait(pool, d_it5, (t.n - 1) * 2)
                ps.tensor_tensor(
                    inter[:, t.odd, half * 512:(half + 1) * 512].rearrange("p (e f) -> p e f", f=F1),
                    z2[:, half, :].rearrange("p (e f) -> p e f", f=F1),
                    comb[:, t.odd, half * 8:half * 8 + 8].unsqueeze(2).broadcast_to([128, 8, F1]),
                    ALU.mult).then_inc(d_mul, 1)

            def step_d(t):
                if t.back(1).live():
                    weigh(t.back(1), 1)
                if t.live():
                    weigh(t, 0)

            steps(pool, 1, step_d)

        @block.scalar
        def _(act):
            ac = nc.scalar
            srcs = {"x": (xr[:, :, :], x), "rows": (rows_s[:, :, :], rows.unsqueeze(0).broadcast_to([128, 3, D])),
                    "mask": (mask_s[:, :, :], mask), "hmask": (hmask_s[:, :], hmask),
                    "vmask": (vmask_s[:, :, :], vmask), "wo0": (wo0_s[:, :, :], wo0)}
            for n, (dst, src) in srcs.items():
                act.dma_start(dst, src).then_inc(load[n], 16)

            def group(g):
                act.wait_ge(first_ready[g % 8], g // 8 + 1)
                return bank[g % 8]

            loaded(act, "ctx")
            ac.activation(ctx_hi[:, :], ctx_s[:, :], ACT.Copy).then_inc(ctx_split, 1)
            loaded(act, "cols")
            for i in range(2):
                g = G_K + i
                ac.activation(k_t[:, i * NKH:(i + 1) * NKH], group(g)[:, 0:NKH], ACT.Identity,
                              bias=cols_s[:, 1:2]).then_inc(first_done[g % 8], 1)
            for i in range(2):
                g = G_V + i
                ac.activation(v_t[:, i * NKH:(i + 1) * NKH], group(g)[:, 0:NKH], ACT.Identity,
                              bias=cols_s[:, 2:3]).then_inc(first_done[g % 8], 1)
            loaded(act, "ident")
            ac.activation(idb[:, :], id_s[:, 0, :], ACT.Copy).then_inc(consts_done, 1)
            loaded(act, "gate", "wout")
            ac.activation(tanh_g[:, :], gate_s[:, :], ACT.Tanh).then_inc(tanh_done, 1)
            act.wait_ge(tanh_done, 1)
            act.wait_ge(bd_zero, 2)
            for h in range(2):
                half = slice(64 * h, 64 * h + 64)
                ac.activation(pair_o[half, :, h, :], wout_s[half, :, :], ACT.Copy,
                              scale=tanh_g[half, 0:1]).then_inc(outw_done, 1)

            def wq_group(i):
                g = G_WQ + i
                src = group(g)[:, :].rearrange("p (c d) -> p c d", c=4)
                for h in range(2):
                    half = slice(64 * h, 64 * h + 64)
                    last = ac.activation(pair_q[half, 4 * i:4 * i + 4, h, :], src[half, :, :], ACT.Copy)
                last.then_inc(first_done[g % 8], 1)

            for i in range(2):
                wq_group(i)
            for g0, hi in ((G_A, a_hi), (G_M, m_hi)):
                for i in range(4):
                    ac.activation(hi[:, i * 512:(i + 1) * 512], group(g0 + i)[:, :], ACT.Copy).then_inc(hi_done, 1)
            for i in range(2):
                g = G_XT + i
                ac.activation(xn_t[:, i * 512:(i + 1) * 512], group(g)[:, :], ACT.Copy).then_inc(first_done[g % 8], 1)
            for i in range(2):
                g = G_Q + i
                ac.activation(q_t[:, i * 512:(i + 1) * 512], group(g)[:, :], ACT.Identity,
                              bias=cols_s[:, 0:1]).then_inc(first_done[g % 8], 1)
            g = G_WG
            ac.activation(wgt[:, :], group(g)[:, 0:E0], ACT.Copy).then_inc(first_done[g % 8], 1)
            for i in range(0, N_B, 2):
                g = G_B + i
                ac.activation(b_all[:, 0:4, (i // 2) * K:(i // 2) * K + K],
                              group(g)[:, 0:NKH].rearrange("p (b k) -> p b k", k=K),
                              ACT.Copy).then_inc(first_done[g % 8], 1)

            def step_w(t):
                wait(act, vw_stored[t.odd], t.pairs(16))
                for c in (0, 2):
                    act.wait_ge(vw_ready, t.n * 4 + c + 1)
                    ac.activation(vws[:, t.odd, c, :], bank[c][0:K, :], ACT.Copy).then_inc(vw_act, 1)
                act.wait_ge(w1t_ready, t.n + 1)
                ac.activation(w1_hi[:, bass.ds(t.n, 1), :].rearrange("p o f -> p (o f)"), bank[4 + t.odd][:, :],
                              ACT.Copy).then_inc(w1t_hi, 1)

            act.wait_ge(first_ready[(N_FIRST - 1) % 8], (N_FIRST - 1) // 8 + 1)
            steps(act, 0, step_w)

            for stored in vw_stored:
                act.wait_ge(stored, 16 * (B // 2))

            def step_a(t):
                if t.back(2).live():
                    q = t.back(2)
                    act.wait_ge(a_ready[7], q.n * 3 + 1)
                    ac.activation(ot[:, q.odd, 0:128], bank[7][:, 0:128], ACT.Copy).then_inc(a_done[7], 1)
                if t.back(1).live():
                    q = t.back(1)
                    wait(act, a_ready[6], (q.n - 1) * 2)
                    for c, (c0, c1) in enumerate(CHUNKS):
                        b = 3 if c != 1 else 4
                        act.wait_ge(a_ready[b], q.n * 2 + c // 2 + 1 if b == 3 else q.n + 1)
                        src = bank[b][:, 0:(c1 - c0) * 128].rearrange("p (c q) -> p c q", q=128)
                        if c < 2:
                            ins = ac.activation(pt[:, q.odd, c0:c1, :], src, ACT.Copy)
                        else:
                            ac.activation(pt[:, q.odd, c0:c0 + 1, :], src[:, 0:1, :], ACT.Copy)
                            ins = ac.activation(pt[0:KLAST, q.odd, c0 + 1, :], src[0:KLAST, 1, :], ACT.Copy)
                        ins.then_inc(a_done[b], 1)
                if t.back(2).live():
                    q = t.back(2)
                    act.wait_ge(a_ready[7], q.n * 3 + 3)
                    ac.activation(columns(xn_t, q, S), bank[7][:, 256:384], ACT.Copy).then_inc(a_done[7], 1)
                if t.live():
                    for g, (h0, h1) in enumerate(HEADS):
                        act.wait_ge(a_sub, t.n * 3 + g + 1)
                        cut = p[:, t.odd, h0 * K:h1 * K]
                        ac.activation(cut, cut, ACT.Exp, scale=HD ** -0.5).then_inc(a_exp, 1)

            steps(act, 2, step_a)

            def router_exp(t, n, neg_sem, exp_sem):
                act.wait_ge(neg_sem, t.n + 1)
                ac.activation(ee[:, t.odd, 0:n], lg[:, 0:n], ACT.Exp, bias=neg[:, t.odd:t.odd + 1],
                              accum_out=ssum[:, t.odd:t.odd + 1]).then_inc(exp_sem, 1)

            def halves(t, there, n, used, m, hi_sem):
                act.wait_ge(there, n)
                wait(act, used, m)
                ac.activation(lhs_hi[:, t.odd, :], columns(xn_t, t, S), ACT.Copy).then_inc(hi_sem, 1)

            def tanh_b(t, e):
                act.wait_ge(b_h, t.n * E0 + e + 1)
                ac.activation(th[:, e % 4, :], bank[e % 4][:, F0:2 * F0], ACT.Tanh, scale=0.5).then_inc(b_tanh, 1)

            def step_b(t):
                q1, q2 = t.back(1), t.back(2)
                if t.live():
                    halves(t, a_done[7], t.n * 3 + 3, b_h, (t.n - 1) * E0, b_prep_hi)
                if q1.live():
                    tanh_b(q1, 6)
                    tanh_b(q1, 7)
                if t.live():
                    tanh_b(t, 0)
                    router_exp(t, E0, b_neg, b_exp)
                    tanh_b(t, 1)
                    tanh_b(t, 2)
                    tanh_b(t, 3)
                if q1.live():
                    act.wait_ge(b_gt, q1.n + 1)
                    wait(act, b_y, q1.n - 1)
                    ac.activation(ot[:, q1.odd, :], bank[5][:, 0:256], ACT.Copy).then_inc(b_gt_done, 1)
                if t.live():
                    tanh_b(t, 4)
                    tanh_b(t, 5)
                if q2.live():
                    act.wait_ge(b_xt, q2.n + 1)
                    ac.activation(columns(xn_t, q2, S), bank[7][:, 0:128], ACT.Copy).then_inc(b_xt_done, 1)

            steps(act, 2, step_b)
            loaded(act, "gu", "rsh")
            ac.activation(wide_hi[:, 0:2 * EI], gu_s[:, :], ACT.Copy).then_inc(wide_act, 1)
            ac.activation(wide_hi[:, 2 * EI:], rsh_s[:, :], ACT.Copy).then_inc(wide_act, 1)

            def step_c(t):
                if t.back(1).live():
                    q = t.back(1)
                    wait(act, c_y, q.n - 1)
                    for c, (c0, c1) in enumerate(CHUNKS):
                        b = 3 if c != 1 else 4
                        if b == 3:
                            act.wait_ge(c_pt3, q.n * 2 + c // 2 + 1)
                        else:
                            act.wait_ge(c_pt4, q.n + 1)
                        src = bank[b][:, 0:(c1 - c0) * 128].rearrange("p (c q) -> p c q", q=128)
                        if c < 2:
                            ins = ac.activation(pt[:, q.odd, c0:c1, :], src, ACT.Copy)
                        else:
                            ac.activation(pt[:, q.odd, c0:c0 + 1, :], src[:, 0:1, :], ACT.Copy)
                            ins = ac.activation(pt[0:KLAST, q.odd, c0 + 1, :], src[0:KLAST, 1, :], ACT.Copy)
                        ins.then_inc(c_pt3_done if b == 3 else c_pt4_done, 1)
                if t.back(2).live():
                    q = t.back(2)
                    act.wait_ge(c_xt, q.n + 1)
                    ac.activation(columns(xn_t, q, S), bank[6][:, 0:128], ACT.Copy).then_inc(c_xt_done, 1)
                if t.live():
                    for g, (h0, h1) in enumerate(HEADS):
                        act.wait_ge(c_sub, t.n * 3 + g + 1)
                        cut = p[:, t.odd, h0 * K:h1 * K]
                        ac.activation(cut, cut, ACT.Exp, scale=64 ** -0.5).then_inc(c_exp, 1)

            steps(act, 2, step_c)

            def tanh_d(t, h):
                act.wait_ge(d_gu, t.n * 2 + h + 1)
                ac.activation(tg[:, h, :], bank[2 * h][:, :], ACT.Tanh, scale=0.5).then_inc(d_tanh, 1)

            def step_d(t):
                q = t.back(1)
                if t.live():
                    halves(t, c_xt_done, t.n + 1, d_gu, (t.n - 1) * 2, d_prep_hi)
                if q.live():
                    tanh_d(q, 1)
                if t.live():
                    router_exp(t, E1, d_neg, d_exp)
                    ac.activation(tg[:, 2, 0:FS], bank[4][:, 0:FS], ACT.Tanh, scale=0.5).then_inc(d_tanh_sh, 1)
                    tanh_d(t, 0)
                if q.live():
                    wait(act, d_y, q.n - 1)
                    act.wait_ge(d_it5, q.n * 2 + 1)
                    ac.activation(it[:, q.odd, 0:4, :], bank[5][:, :].rearrange("p (c q) -> p c q", q=128),
                                  ACT.Copy).then_inc(d_it5_done, 1)
                    act.wait_ge(d_it6, q.n + 1)
                    ac.activation(it[:, q.odd, 4:8, :], bank[6][:, :].rearrange("p (c q) -> p c q", q=128),
                                  ACT.Copy).then_inc(d_it6_done, 1)
                    act.wait_ge(d_it5, q.n * 2 + 2)
                    ac.activation(it[:, q.odd, 8, :], bank[5][:, 0:128], ACT.Copy).then_inc(d_it5_done, 1)

            steps(act, 1, step_d)

        @block.vector
        def _(dve):
            ve = nc.vector
            own = [0]

            def link(ins):
                own[0] += 1
                ins.then_inc(dve_first, 1)
                dve.wait_ge(dve_first, own[0])

            def group(g):
                dve.wait_ge(first_ready[g % 8], g // 8 + 1)
                return bank[g % 8]

            def spread(chain, row, t, var_sem, twice=False):
                u = t.odd
                chain.start(t)
                settle(dve, ve.bn_stats(out=st[:, u, :], in_=row))
                chain.link(ve.bn_aggr(out=ag[:, u, :], in_=st[:, u, :]))
                ve.tensor_scalar(var[:, u:u + 1], ag[:, u, 1:2], 1.0 + EPS if twice else 1.0,
                                 EPS * EPS if twice else EPS, ALU.mult, ALU.add).then_inc(var_sem, 1)

            def normed(row, t, scale_sem, xh_sem, last=None):
                u = t.odd
                dve.wait_ge(scale_sem, t.n + 1)
                n = D if last is None else D - 1
                if last is not None:
                    ve.memset(xh[:, u, D - 1:D], last)
                ve.tensor_scalar(xh[:, u, 0:n], row[:, 0:n], ag[:, u, 0:1], scale[:, u:u + 1],
                                 ALU.subtract, ALU.mult).then_inc(xh_sem, 1)

            loaded(dve, "cols", "ident")
            link(ve.tensor_scalar(tt[:, :], id_s[:, 1, :], cols_s[:, 3:4], None, ALU.mult))
            ve.tensor_copy(tt[:, D - 1:D], cols_s[:, 4:5]).then_inc(tt_done, 1)
            dve.wait_ge(ctx_split, 1)
            loaded(dve, "ctx")
            ve.tensor_tensor(ctx_lo[:, :], ctx_s[:, :], ctx_hi[:, :].bitcast(f32), ALU.subtract).then_inc(ctx_split, 1)
            loaded(dve, "x")
            for b in range(B):
                link(ve.bn_stats(out=st[:, b % 2, :], in_=xr[:, b, :]))
                link(ve.bn_aggr(out=ag8[:, b, :], in_=st[:, b % 2, :]))
            ve.tensor_scalar(var8[:, :], ag8[:, :, 1], EPS, None, ALU.add).then_inc(var8_done, 1)
            dve.wait_ge(scale8_done, 1)
            for b in range(B):
                ve.tensor_scalar(xh0[:, b, :], xr[:, b, :], ag8[:, b, 0:1], scale8[:, b:b + 1],
                                 ALU.subtract, ALU.mult).then_inc(xh0_done, 1)
            loaded(dve, "mask")
            ve.tensor_scalar(maskneg[:, :, :], mask_s[:, :, :], MASKED, None, ALU.mult).then_inc(consts_done, 1)
            link(ve.memset(mark[:, :], BIG))
            link(ve.memset(lg[:, :], BIG))
            n_hi = 0
            for g0, hi, lo in ((G_A, a_hi, a_lo), (G_M, m_hi, m_lo)):
                for i in range(4):
                    n_hi += 1
                    g, cut = g0 + i, slice(i * 512, (i + 1) * 512)
                    src = group(g)
                    dve.wait_ge(hi_done, n_hi)
                    ve.tensor_tensor(lo[:, cut], src[:, :], hi[:, cut].bitcast(f32),
                                     ALU.subtract).then_inc(first_done[g % 8], 1)
            for i in range(1, N_B, 2):
                g = G_B + i
                ve.tensor_copy(b_all[:, 4:8, (i // 2) * K:(i // 2) * K + K],
                               group(g)[:, 0:NKH].rearrange("p (b k) -> p b k", k=K)).then_inc(first_done[g % 8], 1)

            def step_w(t):
                wait(dve, vw_stored[t.odd], t.pairs(16))
                for c in (1, 3):
                    dve.wait_ge(vw_ready, t.n * 4 + c + 1)
                    ve.tensor_copy(vws[:, t.odd, c, :], bank[c][0:K, :]).then_inc(vw_dve, 1)
                dve.wait_ge(w1t_hi, t.n + 1)
                e = bass.ds(t.n, 1)
                ve.tensor_tensor(w1_lo[:, e, :].rearrange("p o f -> p (o f)"), bank[4 + t.odd][:, :],
                                 w1_hi[:, e, :].rearrange("p o f -> p (o f)").bitcast(f32),
                                 ALU.subtract).then_inc(w1t_done, 1)

            steps(dve, 0, step_w)

            for stored in vw_stored:
                dve.wait_ge(stored, 16 * (B // 2))
            dve.wait_ge(w1t_done, B)
            loaded(dve, "vmask")
            dve.wait_ge(bias0_done, 1)
            for u in range(2):
                ve.tensor_copy(vbd[:, u, :, :].rearrange("p c (h o) -> p c h o", o=OW)[:, :, :, HD],
                               vmask_s[:, :, :].rearrange("p c (h o) -> p c h o", o=HD)[:, :, :, 0]).then_inc(ones_done, 1)

            def maxima(t, scores):
                for g, (h0, h1) in enumerate(HEADS):
                    dve.wait_ge(scores, t.n * 3 + g + 1)
                    ins = ve.tensor_reduce(mx[:, t.odd, h0:h1],
                                           bank[g][:, 0:(h1 - h0) * K].rearrange("p (h k) -> p h k", k=K),
                                           AX.X, ALU.max)
                    ins.then_inc(scores_max, 1)

            def minus_max(t, first, sub):
                for g, (h0, h1) in enumerate(HEADS):
                    dve.wait_ge(scores_max, (first + t.n) * 3 + g + 1)
                    ve.tensor_tensor(p[:, t.odd, h0 * K:h1 * K].rearrange("p (h k) -> p h k", k=K),
                                     bank[g][:, 0:(h1 - h0) * K].rearrange("p (h k) -> p h k", k=K),
                                     mx[:, t.odd, h0:h1].unsqueeze(2).broadcast_to([128, h1 - h0, K]),
                                     ALU.subtract).then_inc(sub, 1)

            chain_o, chain_y = Chain(dve, a_chain, 1), Chain(dve, a_chain_y, 1)

            def values(q, c):
                c0, c1 = CHUNKS[c]
                b = 5 if c != 1 else 6
                if c == 0:
                    wait(dve, a_ready[6], (q.n - 1) * 2)
                dve.wait_ge(a_ready[b], q.n * 2 + c // 2 + 1 if b == 5 else q.n * 2 + 1)
                src = bank[b][:, 0:(c1 - c0) * 128].rearrange("p (c h o) -> p c h o", h=H, o=HD)
                msk = vmask_s[:, c0:c1, :].rearrange("p c (h o) -> p c h o", o=HD)
                dst = vbd[:, q.odd, c0:c1, :].rearrange("p c (h o) -> p c h o", o=OW)[:, :, :, 0:HD]
                if c < 2:
                    ins = ve.tensor_tensor(dst, src, msk, ALU.mult)
                else:
                    ve.tensor_tensor(dst[:, 0], src[:, 0], msk[:, 0], ALU.mult)
                    ins = ve.tensor_tensor(dst[0:KLAST, 1], src[0:KLAST, 1], msk[0:KLAST, 1], ALU.mult)
                ins.then_inc(a_done[b], 1)

            def step_a(t):
                if t.back(1).live():
                    values(t.back(1), 0)
                    values(t.back(1), 1)
                if t.back(2).live():
                    q = t.back(2)
                    dve.wait_ge(a_ready[7], q.n * 3 + 2)
                    row = tile_of(xr, q)
                    ve.tensor_tensor(row, bank[7][:, 128:256], row, ALU.add).then_inc(a_done[7], 1)
                    settle(dve)
                    spread(chain_y, row, q, a_var)
                if t.live():
                    maxima(t, a_scores)
                if t.back(2).live():
                    q = t.back(2)
                    normed(tile_of(xr, q), q, a_scale, a_xh, 1.0)
                if t.back(1).live():
                    values(t.back(1), 2)
                if t.live():
                    wait(dve, a_ready[3], (t.n - 1) * 2)
                    minus_max(t, 0, a_sub)
                if t.back(1).live():
                    q = t.back(1)
                    dve.wait_ge(a_ready[6], q.n * 2 + 2)
                    heads = bank[6][:, 0:H * OW].rearrange("p (h o) -> p h o", o=OW)
                    chain_o.start(q)
                    chain_o.link(ve.reciprocal(rinv[:, q.odd, :], heads[:, :, HD]))
                    wait(dve, a_ready[7], (q.n - 1) * 3)
                    ve.tensor_tensor(o_n[:, q.odd, :, :], heads[:, :, 0:HD],
                                     rinv[:, q.odd, :].unsqueeze(2).broadcast_to([128, H, HD]),
                                     ALU.mult).then_inc(a_done[6], 1)

            steps(dve, 2, step_a)

            def choose(chain, t, n, logits, logits_done, neg_sem):
                settle(dve, ve.tensor_copy(lg[:, 0:n], logits))
                chain.link(ve.max(out=top[:, :], in_=lg[:, 0:n]))
                ve.tensor_scalar(neg[:, t.odd:t.odd + 1], top[:, 0:1], -1.0, None, ALU.mult).then_inc(neg_sem, 1)
                settle(dve, ve.tensor_copy(mark[:, 0:2], top[:, 0:2]))
                chain.link(ve.match_replace(out=lr[:, 0:n + 6], in_to_replace=mark[:, :],
                                            in_values=lg[:, 0:n + 6], imm_value=-BIG))
                ve.tensor_tensor(sel[:, 0:n], lr[:, 0:n], lg[:, 0:n], ALU.is_lt).then_inc(logits_done, 1)
                dve.wait_ge(logits_done, t.n + 1)

            def pick(chain, t, n, exp_sem):
                dve.wait_ge(exp_sem, t.n + 1)
                chain.link(ve.tensor_tensor(es[:, 0:n], ee[:, t.odd, 0:n], sel[:, 0:n], ALU.mult))
                chain.link(ve.tensor_reduce(s2[:, 0:1], es[:, 0:n], AX.X, ALU.add))

            chain_r, chain_y = Chain(dve, b_chain, 8), Chain(dve, b_chain_y, 1)

            def low_half(t, hi_sem, done_sem):
                dve.wait_ge(hi_sem, t.n + 1)
                ve.tensor_tensor(lhs_lo[:, t.odd, :], columns(xn_t, t, S), lhs_hi[:, t.odd, :].bitcast(f32),
                                 ALU.subtract).then_inc(done_sem, 1)

            def gated(t, e):
                dve.wait_ge(b_tanh, t.n * E0 + e + 1)
                if e < EP:
                    wait(dve, b_part, (t.n - 1) * 2 + 1)
                ve.scalar_tensor_tensor(out=ub[:, e, :], in0=th[:, e % 4, :], scalar=1.0,
                                        in1=bank[e % 4][:, 0:F0], op0=ALU.add, op1=ALU.mult).then_inc(b_u, 1)

            def step_b(t):
                q1, q2 = t.back(1), t.back(2)
                if t.live():
                    low_half(t, b_prep_hi, b_prep)
                if q1.live():
                    gated(q1, 6)
                    gated(q1, 7)
                if t.live():
                    chain_r.start(t)
                    dve.wait_ge(b_lg, t.n + 1)
                    choose(chain_r, t, E0, bank[4][:, 0:E0], b_lg_done, b_neg)
                    gated(t, 0)
                    pick(chain_r, t, E0, b_exp)
                    chain_r.link(ve.scalar_tensor_tensor(out=s2[:, 1:2], in0=ssum[:, t.odd:t.odd + 1],
                                                         scalar=EPS_TOP, in1=s2[:, 0:1],
                                                         op0=ALU.mult, op1=ALU.add))
                    chain_r.link(ve.reciprocal(s2[:, 2:3], s2[:, 1:2]))
                    ve.tensor_scalar(comb[:, t.odd, 0:E0], es[:, 0:E0], s2[:, 2:3], 0.5,
                                     ALU.mult, ALU.mult).then_inc(b_comb, 1)
                    chain_r.link(ve.tensor_tensor(csum[:, t.odd:t.odd + 1], s2[:, 0:1], s2[:, 2:3], ALU.mult))
                    row = tile_of(xr, t)
                    chain_r.link(ve.scalar_tensor_tensor(out=row, in0=rows_s[:, 1, :],
                                                         scalar=csum[:, t.odd:t.odd + 1], in1=row,
                                                         op0=ALU.mult, op1=ALU.add))
                if q1.live():
                    dve.wait_ge(b_acc, q1.n + 1)
                    dve.wait_ge(b_u, q1.n * E0 + E0)
                    for k in range(E0 - EP):
                        wait(dve, b_sum, q1.n * (E0 - EP) + k)
                        ve.scalar_tensor_tensor(out=gb[:, q1.odd, :], in0=ub[:, EP + k, :],
                                                scalar=comb[:, q1.odd, EP + k:EP + k + 1], in1=gb[:, q1.odd, :],
                                                op0=ALU.mult, op1=ALU.add).then_inc(b_sum, 1)
                if t.live():
                    gated(t, 1)
                    gated(t, 2)
                if q2.live():
                    normed(tile_of(xr, q2), q2, b_scale, b_xh, 1.0)
                if t.live():
                    gated(t, 3)
                    gated(t, 4)
                if q1.live():
                    dve.wait_ge(b_y, q1.n + 1)
                    row = tile_of(xr, q1)
                    ve.tensor_tensor(row, bank[6][:, 0:D], row, ALU.add).then_inc(b_y_done, 1)
                    settle(dve)
                    spread(chain_y, row, q1, b_var, True)
                if t.live():
                    gated(t, 5)

            steps(dve, 2, step_b)

            chain_y = Chain(dve, c_chain_y, 1)

            def step_c(t):
                if t.live():
                    maxima(t, c_scores)
                if t.back(2).live():
                    q = t.back(2)
                    dve.wait_ge(c_y, q.n + 1)
                    row = tile_of(xr, q)
                    ve.tensor_tensor(row, bank[5][:, 0:D], row, ALU.add).then_inc(c_y_done, 1)
                    settle(dve)
                    spread(chain_y, row, q, c_var)
                if t.live():
                    wait(dve, c_pt3, (t.n - 1) * 2)
                    minus_max(t, B, c_sub)
                if t.back(2).live():
                    q = t.back(2)
                    normed(tile_of(xr, q), q, c_scale, c_xh)
                if t.live():
                    dve.wait_ge(c_exp, t.n * 3 + 3)
                    ve.tensor_reduce(rs[:, t.odd, :], p[:, t.odd, :].rearrange("p (h k) -> p h k", k=K),
                                     AX.X, ALU.add).then_inc(c_chain, 1)
                    dve.wait_ge(c_chain, t.n + 1)
                    wait(dve, c_norm, t.n - 1)
                    ve.reciprocal(rinv[:, t.odd, :], rs[:, t.odd, :]).then_inc(c_rs, 1)

            steps(dve, 2, step_c)

            chain_r = Chain(dve, d_chain, 6)
            dve.wait_ge(c_rs, B)
            link(ve.memset(lg[:, E1:24], BIG))

            def half(t, h):
                dve.wait_ge(d_tanh, t.n * 2 + h + 1)
                ve.scalar_tensor_tensor(out=z1[:, h, :], in0=tg[:, h, :], scalar=1.0, in1=bank[2 * h][:, :],
                                        op0=ALU.add, op1=ALU.mult).then_inc(d_z1, 1)
                dve.wait_ge(d_z1, t.n * 2 + h + 1)
                wait(dve, d_mul, (t.n - 1) * 2 + h + 1)
                ve.tensor_tensor(z2[:, h, :], z1[:, h, :], bank[2 * h + 1][:, :], ALU.mult).then_inc(d_z, 1)

            def step_d(t):
                if t.live():
                    low_half(t, d_prep_hi, d_prep)
                if t.back(1).live():
                    half(t.back(1), 1)
                if t.live():
                    chain_r.start(t)
                    dve.wait_ge(d_sh, t.n + 1)
                    choose(chain_r, t, E1, bank[4][:, 2 * FS:2 * FS + E1], d_lg_done, d_neg)
                    dve.wait_ge(d_tanh_sh, t.n + 1)
                    chain_r.link(ve.scalar_tensor_tensor(out=z1[:, 2, 0:FS], in0=tg[:, 2, 0:FS], scalar=1.0,
                                                         in1=bank[4][:, 0:FS], op0=ALU.add, op1=ALU.mult))
                    wait(dve, d_it5, (t.n - 1) * 2)
                    ve.scalar_tensor_tensor(out=inter[:, t.odd, EI:EI + FS], in0=z1[:, 2, 0:FS], scalar=0.5,
                                            in1=bank[4][:, FS:2 * FS], op0=ALU.mult,
                                            op1=ALU.mult).then_inc(d_sh_done, 1)
                    pick(chain_r, t, E1, d_exp)
                    chain_r.link(ve.reciprocal(s2[:, 2:3], ssum[:, t.odd:t.odd + 1]))
                    wait(dve, d_mul, (t.n - 1) * 2)
                    ve.tensor_scalar(comb[:, t.odd, :], es[:, :], s2[:, 2:3], 0.5,
                                     ALU.mult, ALU.mult).then_inc(d_comb, 1)
                    half(t, 0)
                if t.back(1).live():
                    q = t.back(1)
                    wait(dve, d_out[q.odd], q.pairs(16))
                    dve.wait_ge(d_y, q.n + 1)
                    ve.tensor_tensor(yb[:, q.odd, :], bank[7][:, 0:D], tile_of(xr, q), ALU.add).then_inc(d_y_done, 1)

            steps(dve, 1, step_d)

        @block.tensor
        def _(pe):
            te = nc.tensor

            def mm3(dst, a_hi_, a_lo_, b_hi_, b_lo_):
                te.matmul(dst, a_hi_, b_hi_, start=True, stop=False)
                te.matmul(dst, a_hi_, b_lo_, start=False, stop=False)
                return te.matmul(dst, a_lo_, b_hi_, start=False, stop=True)

            def group(g):
                if g >= 8:
                    pe.wait_ge(first_done[g % 8], g // 8)
                return bank[g % 8]

            def ready(ins, g):
                ins.then_inc(first_ready[g % 8], 1)

            loaded(pe, "ctx", "w0")
            for g0, w in ((G_K, 1), (G_V, 2)):
                for i in range(2):
                    ready(te.matmul(group(g0 + i)[:, 0:NKH], w0_s[:, w, :], ctx_s[:, i * NKH:(i + 1) * NKH],
                                    start=True, stop=True), g0 + i)
            loaded(pe, "wq")
            pe.wait_ge(tt_done, 1)
            for i in range(2):
                dst = group(G_WQ + i)
                for c in range(4):
                    j = 4 * i + c
                    last = te.matmul(dst[:, c * 128:(c + 1) * 128], wq_s[:, j * 128:(j + 1) * 128], tt[:, :],
                                     start=True, stop=True)
                ready(last, G_WQ + i)
            pe.wait_ge(bd_zero, 2)
            loaded(pe, "wk")
            for i in range(2):
                pe.wait_ge(first_done[(G_WQ + i) % 8], (G_WQ + i) // 8 + 1)
            for g0, lhs_w, rhs_w in ((G_A, wk_s, pair_q), (G_M, wv_s, pair_o)):
                if g0 == G_M:
                    loaded(pe, "wv")
                    pe.wait_ge(outw_done, 2)
                for i in range(4):
                    dst = group(g0 + i)
                    for c in range(2):
                        j = 2 * i + c
                        last = te.matmul(dst[:, c * 256:(c + 1) * 256], lhs_w[:, j, :],
                                         rhs_w[:, j, :, :].rearrange("p h d -> p (h d)"), start=True, stop=True)
                    ready(last, g0 + i)
            loaded(pe, "ident")
            for i in range(2):
                dst = group(G_XT + i)
                for c in range(4):
                    pe.wait_ge(xh0_done, 4 * i + c + 1)
                    last = te.transpose(dst[:, c * 128:(c + 1) * 128], xh0[:, 4 * i + c, :], id_s[:, 0, :])
                ready(last, G_XT + i)
            for i in range(2):
                dst = group(G_Q + i)
                pe.wait_ge(first_done[(G_XT + i) % 8], (G_XT + i) // 8 + 1)
                ready(te.matmul(dst[:, :], w0_s[:, 0, :], xn_t[:, i * 512:(i + 1) * 512], start=True, stop=True),
                      G_Q + i)
            pe.wait_ge(wg_done, 1)
            ready(te.transpose(group(G_WG)[:, 0:E0], wg_s[:, :], id_s[0:E0, 0, 0:E0]), G_WG)
            pe.wait_ge(ctx_split, 2)
            for i in range(4):
                pe.wait_ge(first_done[(G_A + i) % 8], (G_A + i) // 8 + 1)
            for h in range(H):
                for i in range(2):
                    g = G_B + 2 * h + i
                    cut = slice(h * D, h * D + D)
                    ready(mm3(group(g)[:, 0:NKH], a_hi[:, cut], a_lo[:, cut],
                              ctx_hi[:, i * NKH:(i + 1) * NKH], ctx_lo[:, i * NKH:(i + 1) * NKH]), g)
            for i in range(8):
                n = len([g for g in range(N_FIRST) if g % 8 == i])
                pe.wait_ge(first_done[i], n)

            def step_w(t):
                pe.wait_ge(cb_done, t.n + 1)
                for c in range(4):
                    wait(pe, vw_act if c % 2 == 0 else vw_dve, (t.n - 1) * 2 + c // 2 + 1)
                    cut = slice(c * 512, (c + 1) * 512)
                    mm3(bank[c][0:K, :], cb_hi[:, t.odd, :], cb_lo[:, t.odd, :], m_hi[:, cut],
                        m_lo[:, cut]).then_inc(vw_ready, 1)
                wait(pe, w1t_done, t.n - 1)
                pe.wait_ge(w1_done, t.n + 1)
                for c in range(4):
                    last = te.transpose(bank[4 + t.odd][:, c * 128:(c + 1) * 128], w1f[:, t.odd, c, :],
                                        id_s[:, 0, :])
                last.then_inc(w1t_ready, 1)

            steps(pe, 0, step_w)

            for i in range(0, 4):
                pe.wait_ge(vw_act if i % 2 == 0 else vw_dve, B * 2)
            pe.wait_ge(w1t_done, B)
            pe.wait_ge(consts_done, 2)
            pe.wait_ge(ones_done, 2)

            def scores_a(t, g):
                h0, h1 = HEADS[g]
                dst = bank[g][:, 0:(h1 - h0) * K]
                wait(pe, a_sub, (t.n - 1) * 3 + g + 1)
                te.matmul(dst, lhs[:, t.odd, :], kbd[:, t.odd, h0 * K:h1 * K], start=True, stop=False)
                te.matmul(dst.rearrange("p (h k) -> p h k", k=K), idb[:, :],
                          maskneg[:, bass.ds(t.n, 1), :].broadcast_to([128, h1 - h0, K]),
                          start=False, stop=True).then_inc(a_scores, 1)

            def probs(q, c, b, ready, done, n, count):
                c0, c1 = CHUNKS[c]
                wait(pe, done, n)
                for j in range(c0, c1):
                    m = rows_of(j)
                    last = te.transpose(bank[b][0:m, (j - c0) * 128:(j - c0 + 1) * 128],
                                        p[:, q.odd, j * 128:j * 128 + m], id_s[:, 0, :])
                last.then_inc(ready, 1)

            def values_a(q, c, b, n):
                c0, c1 = CHUNKS[c]
                wait(pe, a_done[b], n)
                flat = vper[:, q.odd, :, :].rearrange("p a k -> p (a k)")
                for j in range(c0, c1):
                    m, at = rows_of(j), (j * 128) % K
                    last = te.transpose(bank[b][0:m, (j - c0) * 128:(j - c0 + 1) * 128],
                                        flat[:, at:at + m], id_s[:, 0, :])
                last.then_inc(a_ready[b], 1)

            def step_a(t):
                q1, q2 = t.back(1), t.back(2)
                if q1.live():
                    values_a(q1, 0, 5, q1.n * 2)
                    values_a(q1, 1, 6, q1.n * 2)
                if q2.live():
                    pe.wait_ge(a_done[6], q2.n * 2 + 2)
                    wait(pe, a_done[7], q2.n * 3)
                    te.transpose(bank[7][:, 0:128], o_n[:, q2.odd, :, :].rearrange("p h o -> p (h o)"),
                                 id_s[:, 0, :]).then_inc(a_ready[7], 1)
                if t.live():
                    pe.wait_ge(a_prep, t.n + 1)
                    scores_a(t, 0)
                if q2.live():
                    pe.wait_ge(a_done[7], q2.n * 3 + 1)
                    te.matmul(bank[7][:, 128:256], ot[:, q2.odd, 0:128], w0_s[:, 3, :],
                              start=True, stop=True).then_inc(a_ready[7], 1)
                if t.live():
                    scores_a(t, 1)
                    scores_a(t, 2)
                if q1.live():
                    pe.wait_ge(a_exp, q1.n * 3 + 3)
                    probs(q1, 0, 3, a_ready[3], a_done[3], q1.n * 2, None)
                    probs(q1, 1, 4, a_ready[4], a_done[4], q1.n, None)
                    values_a(q1, 2, 5, q1.n * 2 + 1)
                    probs(q1, 2, 3, a_ready[3], a_done[3], q1.n * 2 + 1, None)
                if q2.live():
                    pe.wait_ge(a_xh, q2.n + 1)
                    wait(pe, a_done[7], q2.n * 3 + 2)
                    te.transpose(bank[7][:, 256:384], xh[:, q2.odd, :], id_s[:, 0, :]).then_inc(a_ready[7], 1)
                if q1.live():
                    pe.wait_ge(a_done[3], q1.n * 2 + 2)
                    pe.wait_ge(a_done[4], q1.n + 1)
                    pe.wait_ge(a_done[5], q1.n * 2 + 2)
                    pe.wait_ge(a_done[6], q1.n * 2 + 1)
                    for j in range(KC):
                        m = rows_of(j)
                        last = te.matmul(bank[6][:, 0:H * OW], pt[0:m, q1.odd, j, :], vbd[0:m, q1.odd, j, :],
                                         start=(j == 0), stop=(j == KC - 1))
                    last.then_inc(a_ready[6], 1)

            steps(pe, 2, step_a)
            pe.wait_ge(a_done[7], B * 3)
            pe.wait_ge(first_done[G_WG % 8], G_WG // 8 + 1)
            loaded(pe, "wo0")

            def experts(t, e0, e1):
                for e in range(e0, e1):
                    wait(pe, b_u, t.n * E0 + e - 3)
                    mm3(bank[e % 4][:, :], lhs_hi[:, t.odd, :], lhs_lo[:, t.odd, :], w1_hi[:, e, :],
                        w1_lo[:, e, :]).then_inc(b_h, 1)

            def step_b(t):
                q1, q2 = t.back(1), t.back(2)
                if t.live():
                    pe.wait_ge(b_prep, t.n + 1)
                    wait(pe, b_lg_done, t.n)
                    te.matmul(bank[4][:, 0:E0], lhs_hi[:, t.odd, :].bitcast(f32), wgt[:, :], start=True, stop=False)
                    te.matmul(bank[4][:, 0:E0], lhs_lo[:, t.odd, :].bitcast(f32), wgt[:, :], start=False,
                              stop=True).then_inc(b_lg, 1)
                    experts(t, 0, 4)
                if q1.live():
                    pe.wait_ge(b_sum, (q1.n + 1) * (E0 - EP))
                    wait(pe, b_gt_done, q1.n)
                    for c in range(2):
                        last = te.transpose(bank[5][:, c * 128:(c + 1) * 128],
                                            gb[:, q1.odd, c * 128:(c + 1) * 128], id_s[:, 0, :])
                    last.then_inc(b_gt, 1)
                if t.live():
                    experts(t, 4, 5)
                if q1.live():
                    pe.wait_ge(b_gt_done, q1.n + 1)
                    wait(pe, b_y_done, q1.n)
                    te.matmul(bank[6][:, 0:D], ot[:, q1.odd, 0:128], wo0_s[:, 0, :], start=True, stop=False)
                    te.matmul(bank[6][:, 0:D], ot[:, q1.odd, 128:256], wo0_s[:, 1, :], start=False,
                              stop=True).then_inc(b_y, 1)
                if q2.live():
                    pe.wait_ge(b_xh, q2.n + 1)
                    wait(pe, b_xt_done, q2.n)
                    te.transpose(bank[7][:, 0:128], xh[:, q2.odd, :], id_s[:, 0, :]).then_inc(b_xt, 1)
                if t.live():
                    experts(t, 5, E0)

            steps(pe, 2, step_b)

            pe.wait_ge(b_u, B * E0)
            pe.wait_ge(b_xt_done, B)
            pe.wait_ge(c_bias0, 1)

            def step_c(t):
                q1, q2 = t.back(1), t.back(2)
                if t.live():
                    pe.wait_ge(c_prep, t.n + 1)
                    for g, (h0, h1) in enumerate(HEADS):
                        wait(pe, c_sub, (t.n - 1) * 3 + g + 1)
                        te.matmul(bank[g][:, 0:(h1 - h0) * K], lhs[:, t.odd, :],
                                  b_all[:, bass.ds(t.n, 1), h0 * K:h1 * K].rearrange("p o k -> p (o k)"),
                                  start=True, stop=True).then_inc(c_scores, 1)
                if q1.live():
                    pe.wait_ge(c_norm, q1.n + 1)
                    probs(q1, 0, 3, c_pt3, c_pt3_done, q1.n * 2, None)
                    probs(q1, 1, 4, c_pt4, c_pt4_done, q1.n, None)
                    probs(q1, 2, 3, c_pt3, c_pt3_done, q1.n * 2 + 1, None)
                    pe.wait_ge(c_pt3_done, q1.n * 2 + 2)
                    pe.wait_ge(c_pt4_done, q1.n + 1)
                    pe.wait_ge(c_vw[q1.odd], q1.pairs(32) + 32)
                    wait(pe, c_y_done, q1.n)
                    for j in range(KC):
                        m = rows_of(j)
                        te.matmul(bank[5][:, 0:D], pt[0:m, q1.odd, j, :], vw[0:m, q1.odd, j, :],
                                  start=(j == 0), stop=False)
                    te.matmul(bank[5][:, 0:D], one[0:1, :], rows_s[0:1, 2, :], start=False,
                              stop=True).then_inc(c_y, 1)
                if q2.live():
                    pe.wait_ge(c_xh, q2.n + 1)
                    wait(pe, c_xt_done, q2.n)
                    te.transpose(bank[6][:, 0:128], xh[:, q2.odd, :], id_s[:, 0, :]).then_inc(c_xt, 1)

            steps(pe, 2, step_c)

            pe.wait_ge(wide_done, 1)
            pe.wait_ge(wide_act, 2)
            pe.wait_ge(c_xt_done, B)
            loaded(pe, "down")

            def wide(t, dst, at, n):
                return mm3(dst, lhs_hi[:, t.odd, :], lhs_lo[:, t.odd, :], wide_hi[:, at:at + n], wide_lo[:, at:at + n])

            def step_d(t):
                q = t.back(1)

                def inner(c, b, ready, done, n):
                    c0, c1 = ICHUNKS[c]
                    wait(pe, done, n)
                    for j in range(c0, c1):
                        last = te.transpose(bank[b][:, (j - c0) * 128:(j - c0 + 1) * 128],
                                            inter[:, q.odd, j * 128:(j + 1) * 128], id_s[:, 0, :])
                    last.then_inc(ready, 1)

                def gate_up(h):
                    wait(pe, d_z, (t.n - 1) * 2 + h + 1)
                    wide(t, bank[2 * h][:, :], h * 512, 512)
                    wide(t, bank[2 * h + 1][:, :], EI + h * 512, 512).then_inc(d_gu, 1)

                if t.live():
                    pe.wait_ge(d_prep, t.n + 1)
                    wait(pe, d_lg_done, t.n)
                    wait(pe, d_sh_done, t.n)
                    wide(t, bank[4][:, 0:2 * FS + E1], 2 * EI, 2 * FS + E1).then_inc(d_sh, 1)
                    gate_up(0)
                if q.live():
                    pe.wait_ge(d_mul, q.n * 2 + 2)
                    pe.wait_ge(d_sh_done, q.n + 1)
                    inner(0, 5, d_it5, d_it5_done, q.n * 2)
                    inner(1, 6, d_it6, d_it6_done, q.n)
                if t.live():
                    gate_up(1)
                if q.live():
                    inner(2, 5, d_it5, d_it5_done, q.n * 2 + 1)
                    pe.wait_ge(d_it5_done, q.n * 2 + 2)
                    pe.wait_ge(d_it6_done, q.n + 1)
                    wait(pe, d_y_done, q.n)
                    for j in range(IC):
                        last = te.matmul(bank[7][:, 0:D], it[:, q.odd, j, :], down_s[:, j, :],
                                         start=(j == 0), stop=(j == IC - 1))
                    last.then_inc(d_y, 1)

            steps(pe, 1, step_d)


def kernel(x, ctx_1024, mask_Bx1xSxS2_bk1, L0_xattn_Wq, L0_xattn_bq, L0_xattn_Wk, L0_xattn_bk, L0_xattn_Wv,
           L0_xattn_bv, L0_xattn_Wo, L0_xattn_bo, L0_ffn_Wg, L0_ffn_W1, L0_ffn_b1, L0_ffn_Wo, L0_ffn_bo,
           L1_xattn_ln_gamma, L1_xattn_ln_beta, L1_xattn_w_q, L1_xattn_w_kv, L1_xattn_w_out, L1_xattn_b_out,
           L1_xattn_gate, L1_ffn_router_w, L1_ffn_gate_w, L1_ffn_up_w, L1_ffn_down_w, L1_ffn_shared_gate_w,
           L1_ffn_shared_up_w, L1_ffn_shared_down_w):
    import concourse.bacc as bacc
    import numpy as np
    from concourse.bass_utils import run_bass_kernel_spmd

    inner = H * 64
    pairs = lambda w: w.reshape(8, 128, D).transpose(1, 0, 2)
    eye = np.eye(128, dtype=np.float32)
    less_last = eye.copy()
    less_last[127, :] -= 1.0
    row_head = np.arange(KC * 128) // K
    arrays = {
        "x": x.transpose(1, 0, 2),
        "ctx_t": ctx_1024.reshape(NK, D).T,
        "mask": mask_Bx1xSxS2_bk1[:, 0].transpose(1, 0, 2),
        "w0": np.stack([L0_xattn_Wq, L0_xattn_Wk, L0_xattn_Wv, L0_xattn_Wo], axis=1),
        "cols": np.stack([L0_xattn_bq, L0_xattn_bk, L0_xattn_bv, L1_xattn_ln_gamma, L1_xattn_ln_beta], axis=1),
        "rows": np.stack([L0_xattn_bo, L0_ffn_bo, L1_xattn_b_out]),
        "w1": L0_ffn_W1.reshape(32, 128, D).transpose(1, 0, 2),
        "b1": L0_ffn_b1.reshape(32, 128).T,
        "wg": L0_ffn_Wg,
        "wo0": L0_ffn_Wo.T.reshape(2, 128, D).transpose(1, 0, 2),
        "wq": L1_xattn_w_q,
        "wk": pairs(L1_xattn_w_kv[:, :inner].T),
        "wv": pairs(L1_xattn_w_kv[:, inner:].T),
        "wout": pairs(L1_xattn_w_out),
        "gate": L1_xattn_gate.reshape(1, 1),
        "gu": np.concatenate([L1_ffn_gate_w.transpose(1, 0, 2).reshape(D, EI),
                              L1_ffn_up_w.transpose(1, 0, 2).reshape(D, EI)], axis=1),
        "rsh": np.concatenate([L1_ffn_shared_gate_w, L1_ffn_shared_up_w, L1_ffn_router_w], axis=1),
        "down": np.concatenate([L1_ffn_down_w.reshape(EI, D), L1_ffn_shared_down_w]).reshape(IC, 128, D)
                .transpose(1, 0, 2),
        "ident": np.stack([eye, less_last], axis=1),
        "hmask": (np.arange(D)[:, None] // HD == np.arange(H)[None, :]).astype(np.float32),
        "vmask": row_head.reshape(KC, 128).T[:, :, None] == np.arange(D)[None, None, :] // HD,
    }
    nc = bacc.Bacc("TRN2", target_bir_lowering=False, num_devices=1)
    feeds, args = {}, {}
    for name, a in arrays.items():
        a = np.ascontiguousarray(a)
        feeds[name + "_in"] = a
        args[name] = nc.dram_tensor(name + "_in", a.shape, mybir.dt.from_np(a.dtype), kind="ExternalInput").ap()
    args["out"] = nc.dram_tensor("out_0", (B, S, D), mybir.dt.float32, kind="ExternalOutput").ap()
    build(nc, **args)
    return run_bass_kernel_spmd(nc, [feeds], core_ids=[0]).results[0]["out_0"]
```

```python
from contextlib import ExitStack

import concourse.bass as bass
from concourse import mybir

B, S, D, K, H = 8, 128, 128, 77, 16
HK = H * K
KC = (HK + 127) // 128
KLAST = HK - 128 * (KC - 1)
HD = D // H
OW = HD + 1
NK = B * K
NKH = NK // 2
E0, F0 = 8, 256
EP = 4
E1, F1, FS = 16, 64, 128
EI = E1 * F1
IC = (EI + FS) // 128
HEADS = [(0, 5), (5, 10), (10, 16)]
CHUNKS = [(0, 4), (4, 8), (8, 10)]
PT_BANKS = (3, 4, 7)
ICHUNKS = [(0, 4), (4, 8), (8, 9)]
EPS, EPS_TOP = 1e-5, 1e-9
MASKED = -1e15
BIG = 3.0e38


def rows_of(c):
    return 128 if c < KC - 1 else KLAST


class Tile:

    def __init__(self, n, odd):
        self.n, self.odd = n, odd

    def back(self, k):
        return Tile(self.n - k, (self.odd + k) % 2)

    def pairs(self, per):
        return (self.n - self.odd) * (per // 2)

    def live(self):
        return not isinstance(self.n, int) or 0 <= self.n < B


def steps(eng, lag, step):
    first = max(2, lag + lag % 2)
    for n in range(first):
        step(Tile(n, n % 2))
    with eng.Fori(0, (B - first) // 2) as i:
        for odd in range(2):
            step(Tile(i * 2 + (first + odd), odd))
    for n in range(B, B + lag):
        step(Tile(n, n % 2))


def wait(eng, sem, value):
    if not isinstance(value, int) or value > 0:
        eng.wait_ge(sem, value)


class Chain:

    def __init__(self, eng, sem, per):
        self.eng, self.sem, self.per = eng, sem, per

    def made(self, ins):
        ins.then_inc(self.sem, 1)

    def need(self, t, k):
        self.eng.wait_ge(self.sem, t.n * self.per + k)


def build(nc, x, ctx_t, mask, w0, cols, rows, w1, b1, wg, wo0, wq, wk, wv, wout, gate, gu, rsh, down,
          ident, hmask, vmask, out):
    f32, f32r, bf16, u8 = mybir.dt.float32, mybir.dt.float32r, mybir.dt.bfloat16, mybir.dt.uint8
    ALU, ACT, AX = mybir.AluOpType, mybir.ActivationFunctionType, mybir.AxisListType
    vw_dram = nc.dram_tensor("vw_scratch", [B, HK, D], f32, kind="Internal").ap()

    with ExitStack() as stack:
        def sb(name, shape, dt=f32, on=stack):
            return on.enter_context(nc.sbuf_tensor(name, shape, dt))

        def sem(name):
            return stack.enter_context(nc.semaphore(name))

        bank = [stack.enter_context(nc.psum_tensor(f"bank{i}", [128, 512], f32)) for i in range(8)]

        xr = sb("xr", [128, B, D])
        rows_s = sb("rows_s", [128, 3, D])
        w0_s = sb("w0_s", [128, 4, D])
        wo0_s = sb("wo0_s", [128, 2, D])
        id_s = sb("id_s", [128, 2, 128])
        idb = sb("idb", [128, 128], bf16)
        hmask_s = sb("hmask_s", [128, H])
        vmask_s = sb("vmask_s", [128, KC, D], u8)
        maskneg = sb("maskneg", [128, B, K], bf16)
        k_t = sb("k_t", [128, NK])
        v_t = sb("v_t", [128, NK])
        q_t = sb("q_t", [128, B * S])
        xn_t = sb("xn_t", [128, B * S])
        wgt = sb("wgt", [128, E0])
        tanh_g = sb("tanh_g", [128, 1])
        b_all = sb("b_all", [128, B, HK])
        w1_hi, w1_lo = sb("w1_hi", [128, E0, 512], f32r), sb("w1_lo", [128, E0, 512], f32r)
        lhs = sb("lhs", [128, 2, 128])
        lhs_hi, lhs_lo = sb("lhs_hi", [128, 2, 128], f32r), sb("lhs_lo", [128, 2, 128], f32r)
        mx, rs = sb("mx", [128, 2, H]), sb("rs", [128, 2, H])
        rinv = sb("rinv", [128, 2, H])
        o_n = sb("o_n", [128, 2, H, HD])
        ot = sb("ot", [128, 2, 256])
        xh = sb("xh", [128, 2, D])
        st, ag = sb("st", [128, 2, 6]), sb("ag", [128, 2, 2])
        var, scale = sb("var", [128, 2]), sb("scale", [128, 2])
        ag8, var8, scale8 = sb("ag8", [128, B, 2]), sb("var8", [128, B]), sb("scale8", [128, B])
        one = sb("one", [1, 128])
        root = sb("root", [128, B])
        lg, lr = sb("lg", [128, 24]), sb("lr", [128, 24])
        top, mark = sb("top", [128, 8]), sb("mark", [128, 8])
        ee, es, sel = sb("ee", [128, 2, E1]), sb("es", [128, E1]), sb("sel", [128, E1])
        neg, ssum, s2 = sb("neg", [128, 2]), sb("ssum", [128, 2]), sb("s2", [128, 4])
        comb, csum = sb("comb", [128, 2, E1]), sb("csum", [128, 2])
        yb = sb("yb", [128, 2, D])

        with ExitStack() as early:
            ctx_s = sb("ctx_s", [128, NK], on=early)
            mask_s = sb("mask_s", [128, B, K], u8, on=early)
            cols_s = sb("cols_s", [128, 5], on=early)
            w1_s = sb("w1_s", [128, 32, D], on=early)
            w1f = sb("w1f", [128, 2, 4, D], on=early)
            w127 = sb("w127", [E0, 1], on=early)
            b1_s = sb("b1_s", [128, 32], on=early)
            wg_s = sb("wg_s", [E0, D], on=early)
            wq_s = sb("wq_s", [128, H * 64], on=early)
            wk_s = sb("wk_s", [128, 8, D], on=early)
            wv_s = sb("wv_s", [128, 8, D], on=early)
            wout_s = sb("wout_s", [128, 8, D], on=early)
            gate_s = sb("gate_s", [128, 1], on=early)
            tt = sb("tt", [128, D], on=early)
            ctx_hi, ctx_lo = sb("ctx_hi", [128, NK], f32r, early), sb("ctx_lo", [128, NK], f32r, early)
            cb_hi, cb_lo = sb("cb_hi", [128, 2, K], f32r, early), sb("cb_lo", [128, 2, K], f32r, early)
            m_hi, m_lo = sb("m_hi", [128, H * D], f32r, early), sb("m_lo", [128, H * D], f32r, early)
            with ExitStack() as first:
                pair_q = sb("pair_q", [128, 8, 2, D], on=first)
                pair_o = sb("pair_o", [128, 8, 2, D], on=first)
                xh0 = sb("xh0", [128, B, D], on=first)
                a_hi, a_lo = sb("a_hi", [128, H * D], f32r, first), sb("a_lo", [128, H * D], f32r, first)
            vws = sb("vws", [K, 2, 4, 512], on=early)
        p = sb("p", [128, 2, HK])
        pt = sb("pt", [128, 2, KC, 128])
        vw = sb("vw", [128, 2, KC, D])
        gu_s = sb("gu_s", [128, 2 * EI])
        rsh_s = sb("rsh_s", [128, 2 * FS + E1])
        down_s = sb("down_s", [128, IC, D])
        wide_hi = sb("wide_hi", [128, 2 * EI + 2 * FS + E1], f32r)
        wide_lo = sb("wide_lo", [128, 2 * EI + 2 * FS + E1], f32r)
        with ExitStack() as phase_a:
            vbd = sb("vbd", [128, 2, KC, H * OW], on=phase_a)
            kbd = sb("kbd", [128, 2, HK], on=phase_a)
            vper = sb("vper", [128, 2, 3, K], on=phase_a)
        with ExitStack() as phase_b:
            th = sb("th", [128, 4, F0], on=phase_b)
            ub = sb("ub", [128, E0, F0], on=phase_b)
            gb = sb("gb", [128, 2, F0], on=phase_b)
            part = sb("part", [128, EP, F0], on=phase_b)
        tg = sb("tg", [128, 3, 512])
        z1 = sb("z1", [128, 3, 512])
        z2 = sb("z2", [128, 2, 512])
        inter = sb("inter", [128, 2, EI + FS])
        it = pt

        names = ("ctx", "w0", "cols", "x", "ident", "wq", "wout", "gate", "wk", "wv", "wg", "rows", "mask",
                 "hmask", "w1", "b1", "vmask", "wo0", "gu", "rsh", "down")
        load = {n: sem("load_" + n) for n in names}

        def loaded(eng, *which):
            for n in which:
                eng.wait_ge(load[n], 16)

        first_ready = [sem(f"first_ready{i}") for i in range(8)]
        first_done = [sem(f"first_done{i}") for i in range(8)]
        hi_done = sem("hi_done")
        dve_first, pool_first = sem("dve_first"), sem("pool_first")
        tt_done, ctx_split, xh0_done, wg_done = sem("tt_done"), sem("ctx_split"), sem("xh0_done"), sem("wg_done")
        bd_zero, w1_done, consts_done, tanh_done = sem("bd_zero"), sem("w1_done"), sem("consts_done"), sem("tanh_done")
        outw_done, bias0_done = sem("outw_done"), sem("bias0_done")
        cb_done, vw_ready, vw_act, vw_dve, vw_stored = (
            sem("cb_done"), sem("vw_ready"), sem("vw_act"), sem("vw_dve"), [sem("vw_stored0"), sem("vw_stored1")])
        w1t_ready, w1t_hi, w1t_done = sem("w1t_ready"), sem("w1t_hi"), sem("w1t_done")
        ones_done = sem("ones_done")
        a_prep, a_vper = sem("a_prep"), sem("a_vper")
        a_sub, a_exp, a_scores = sem("a_sub"), sem("a_exp"), sem("a_scores")
        a_ready = {i: sem(f"a_ready{i}") for i in range(3, 8)}
        a_done = {i: sem(f"a_done{i}") for i in range(3, 8)}
        a_xh = sem("a_xh")
        a_chain, a_chain_y = sem("a_chain"), sem("a_chain_y")
        b_prep_hi, b_prep = sem("b_prep_hi"), sem("b_prep")
        b_lg, b_lg_done, b_h, b_tanh, b_u, b_acc = (
            sem("b_lg"), sem("b_lg_done"), sem("b_h"), sem("b_tanh"), sem("b_u"), sem("b_acc"))
        b_neg, b_exp, b_comb = sem("b_neg"), sem("b_exp"), sem("b_comb")
        b_part, b_sum = sem("b_part"), sem("b_sum")
        var8_done, scale8_done = sem("var8_done"), sem("scale8_done")
        a_var, a_scale, b_var, b_scale, c_var, c_scale = (
            sem("a_var"), sem("a_scale"), sem("b_var"), sem("b_scale"), sem("c_var"), sem("c_scale"))
        b_gt, b_gt_done, b_y, b_y_done, b_xh, b_xt, b_xt_done = (
            sem("b_gt"), sem("b_gt_done"), sem("b_y"), sem("b_y_done"), sem("b_xh"), sem("b_xt"), sem("b_xt_done"))
        b_chain, b_chain_y = sem("b_chain"), sem("b_chain_y")
        wide_act, wide_done = sem("wide_act"), sem("wide_done")
        c_prep, c_scores, c_sub, c_exp, c_rs, c_norm = (
            sem("c_prep"), sem("c_scores"), sem("c_sub"), sem("c_exp"), sem("c_rs"), sem("c_norm"))
        c_vw = [sem("c_vw0"), sem("c_vw1")]
        c_bias0 = sem("c_bias0")
        c_pt, c_pt_done = [sem(f"c_pt{i}") for i in range(3)], [sem(f"c_pt_done{i}") for i in range(3)]
        c_y, c_y_done, c_xh, c_xt, c_xt_done = sem("c_y"), sem("c_y_done"), sem("c_xh"), sem("c_xt"), sem("c_xt_done")
        c_chain, c_chain_y = sem("c_chain"), sem("c_chain_y")
        d_prep_hi, d_prep = sem("d_prep_hi"), sem("d_prep")
        d_sh, d_gu, d_tanh, d_tanh_sh, d_z, d_sh_done, d_mul = (
            sem("d_sh"), sem("d_gu"), sem("d_tanh"), sem("d_tanh_sh"), sem("d_z"), sem("d_sh_done"), sem("d_mul"))
        d_neg, d_exp, d_comb = sem("d_neg"), sem("d_exp"), sem("d_comb")
        d_it5, d_it6, d_it5_done, d_it6_done = sem("d_it5"), sem("d_it6"), sem("d_it5_done"), sem("d_it6_done")
        scores_max, d_lg_done, d_z1 = sem("scores_max"), sem("d_lg_done"), sem("d_z1")
        d_y, d_y_done, d_out, d_chain = sem("d_y"), sem("d_y_done"), [sem("d_out0"), sem("d_out1")], sem("d_chain")

        G_K, G_V, G_WQ, G_A, G_M, G_XT, G_Q, G_WG, G_B = 0, 2, 4, 6, 10, 14, 16, 18, 19
        N_B = 2 * H
        N_FIRST = G_B + N_B

        def columns(tensor, t, width):
            return tensor[:, bass.ds(t.n * width, width)]

        def tile_of(tensor, t):
            if isinstance(t.n, int):
                return tensor[:, t.n, :]
            return tensor[:, bass.ds(t.n, 1), :].rearrange("p o d -> p (o d)")

        block = stack.enter_context(nc.Block())

        @block.sync
        def _(sp):
            srcs = {"ctx": (ctx_s[:, :], ctx_t), "w0": (w0_s[:, :, :], w0), "cols": (cols_s[:, :], cols),
                    "ident": (id_s[:, :, :], ident), "wq": (wq_s[:, :], wq), "wk": (wk_s[:, :, :], wk),
                    "gate": (gate_s[:, :], gate.broadcast_to([128, 1])), "wout": (wout_s[:, :, :], wout),
                    "wv": (wv_s[:, :, :], wv),
                    "wg": (wg_s[:, :], wg), "w1": (w1_s[:, :, :], w1), "b1": (b1_s[:, :], b1)}
            for n, (dst, src) in srcs.items():
                sp.dma_start(dst, src).then_inc(load[n], 16)

            def store(t):
                sp.wait_ge(vw_act, t.n * 2 + 2)
                sp.wait_ge(vw_dve, t.n * 2 + 2)
                dst = vw_dram[bass.ds(t.n, 1), :, :].rearrange("o (h k) d -> k (o h) d", h=H)
                sp.dma_start(dst, vws[:, t.odd, :, :].rearrange("k a (h d) -> k (a h) d", h=4)).then_inc(vw_stored[t.odd], 16)

            steps(sp, 0, store)

            for stored in vw_stored:
                sp.wait_ge(stored, 16 * (B // 2))
            sp.wait_ge(w1t_ready, B)
            sp.wait_ge(w1t_done, B)
            sp.dma_start(gu_s[:, :], gu).then_inc(load["gu"], 16)
            sp.dma_start(rsh_s[:, :], rsh).then_inc(load["rsh"], 16)
            sp.dma_start(down_s[:, :, :], down).then_inc(load["down"], 16)

            def fetch(t):
                wait(sp, c_y, t.n - 1)
                src = vw_dram[bass.ds(t.n, 1), :, :]
                sp.dma_start(vw[:, t.odd, 0:KC - 1, :],
                             src[:, 0:128 * (KC - 1), :].rearrange("o (c p) d -> p (o c) d", p=128)
                             ).then_inc(c_vw[t.odd], 16)
                sp.dma_start(vw[0:KLAST, t.odd, KC - 1, :],
                             src[:, 128 * (KC - 1):HK, :].rearrange("o p d -> p (o d)")
                             ).then_inc(c_vw[t.odd], 16)

            steps(sp, 0, fetch)

            def result(t):
                sp.wait_ge(d_y_done, t.n + 1)
                sp.dma_start(out[bass.ds(t.n, 1), :, :].rearrange("o s d -> s (o d)"),
                             yb[:, t.odd, :]).then_inc(d_out[t.odd], 16)

            steps(sp, 0, result)
            for s in d_out:
                sp.wait_ge(s, 16 * (B // 2))

        @block.gpsimd
        def _(pool):
            ps = nc.gpsimd
            own = [0]

            def link(ins):
                own[0] += 1
                ins.then_inc(pool_first, 1)
                pool.wait_ge(pool_first, own[0])

            for buf in (pair_q, pair_o):
                ps.memset(buf[:, :, :, :], 0.0).then_inc(bd_zero, 1)
            link(ps.memset(root[:, :], -0.5))

            def inverse_root(t, var_sem, scale_sem):
                pool.wait_ge(var_sem, t.n + 1)
                u = slice(t.odd, t.odd + 1)
                ps.tensor_tensor(scale[:, u], var[:, u], root[:, 0:1], ALU.pow).then_inc(scale_sem, 1)

            pool.wait_ge(var8_done, 1)
            ps.tensor_tensor(scale8[:, :], var8[:, :], root[:, :], ALU.pow).then_inc(scale8_done, 1)
            loaded(pool, "wg")
            link(ps.tensor_copy(w127[:, 0:1], wg_s[:, D - 1:D]))
            link(ps.tensor_tensor(wg_s[:, 0:D - 1], wg_s[:, 0:D - 1],
                                  w127[:, 0:1].broadcast_to([E0, D - 1]), ALU.subtract))
            ps.memset(wg_s[:, D - 1:D], 0.0).then_inc(wg_done, 1)
            loaded(pool, "rows")
            pool.wait_ge(xh0_done, B)
            ps.tensor_tensor(xr[:, :, :], xr[:, :, :], rows_s[:, 0:1, :].broadcast_to([128, B, D]),
                             ALU.add).then_inc(bias0_done, 1)

            pool.wait_ge(ctx_split, 2)

            def context(t):
                wait(pool, vw_ready, (t.n - 1) * 4)
                ps.tensor_copy(cb_hi[:, t.odd, :], columns(ctx_hi, t, K))
                ps.tensor_copy(cb_lo[:, t.odd, :], columns(ctx_lo, t, K)).then_inc(cb_done, 1)
                wait(pool, w1t_ready, t.n - 1)
                rows4 = w1_s[:, bass.ds(t.n * 4, 4), :]
                ps.tensor_tensor(w1f[:, t.odd, :, 0:D - 1], rows4[:, :, 0:D - 1],
                                 rows4[:, :, D - 1:D].broadcast_to([128, 4, D - 1]), ALU.subtract)
                ps.tensor_copy(w1f[:, t.odd, :, D - 1], b1_s[:, bass.ds(t.n * 4, 4)]).then_inc(w1_done, 1)

            loaded(pool, "w1", "b1")
            steps(pool, 0, context)

            pool.wait_ge(w1t_ready, B)
            pool.wait_ge(w1t_done, B)
            for stored in vw_stored:
                pool.wait_ge(stored, 16 * (B // 2))
            pool.wait_ge(first_done[(G_Q + 1) % 8], (G_Q + 1) // 8 + 1)
            pool.wait_ge(first_done[G_Q % 8], G_Q // 8 + 1)
            loaded(pool, "hmask")

            def step_a(ahead):
                if ahead.live():
                    wait(pool, a_scores, (ahead.n - 1) * 3)
                    ps.tensor_copy(lhs[:, ahead.odd, :], columns(q_t, ahead, S))
                    ps.tensor_tensor(kbd[:, ahead.odd, :].rearrange("p (h k) -> p h k", h=H),
                                     columns(k_t, ahead, K).unsqueeze(1).broadcast_to([128, H, K]),
                                     hmask_s[:, :].unsqueeze(2).broadcast_to([128, H, K]),
                                     ALU.mult).then_inc(a_prep, 1)
                    wait(pool, a_ready[5], (ahead.n - 1) * 3)
                    ps.tensor_copy(vper[:, ahead.odd, :, :],
                                   columns(v_t, ahead, K).unsqueeze(1).broadcast_to([128, 3, K])).then_inc(a_vper, 1)
                if ahead.back(3).live():
                    inverse_root(ahead.back(3), a_var, a_scale)

            steps(pool, 3, step_a)

            def step_b(t):
                if t.back(3).live():
                    inverse_root(t.back(3), b_var, b_scale)
                if t.live():
                    pool.wait_ge(b_u, t.n * E0 + EP)
                    pool.wait_ge(b_comb, t.n + 1)
                    ps.tensor_tensor(part[:, :, :], ub[:, 0:EP, :],
                                     comb[:, t.odd, 0:EP].unsqueeze(2).broadcast_to([128, EP, F0]),
                                     ALU.mult).then_inc(b_part, 1)
                    pool.wait_ge(b_part, t.n * 2 + 1)
                    ps.tensor_tensor(part[:, 0:2, :], part[:, 0:2, :], part[:, 2:4, :], ALU.add).then_inc(b_part, 1)
                    pool.wait_ge(b_part, t.n * 2 + 2)
                    wait(pool, b_gt, t.n - 1)
                    ps.tensor_tensor(gb[:, t.odd, :], part[:, 0, :], part[:, 1, :], ALU.add).then_inc(b_acc, 1)

            steps(pool, 3, step_b)

            loaded(pool, "gu", "rsh")
            pool.wait_ge(wide_act, 2)
            ps.tensor_tensor(wide_lo[:, 0:2 * EI], gu_s[:, :], wide_hi[:, 0:2 * EI].bitcast(f32),
                             ALU.subtract)
            ps.tensor_tensor(wide_lo[:, 2 * EI:], rsh_s[:, :], wide_hi[:, 2 * EI:].bitcast(f32),
                             ALU.subtract).then_inc(wide_done, 1)
            pool.wait_ge(tanh_done, 1)
            ps.memset(one[0:1, :], 1.0)
            ps.tensor_scalar(rows_s[:, 2, :], rows_s[:, 2, :], tanh_g[:, 0:1], None, ALU.mult).then_inc(c_bias0, 1)

            def step_c(ahead):
                if ahead.live():
                    pool.wait_ge(b_xt_done, ahead.n + 1)
                    wait(pool, c_scores, (ahead.n - 1) * 3)
                    ps.tensor_copy(lhs[:, ahead.odd, :], columns(xn_t, ahead, S)).then_inc(c_prep, 1)
                if ahead.back(2).live():
                    q = ahead.back(2)
                    pool.wait_ge(c_rs, q.n + 1)
                    pq = p[:, q.odd, :].rearrange("p (h k) -> p h k", h=H)
                    ps.tensor_tensor(pq, pq, rinv[:, q.odd, :].unsqueeze(2).broadcast_to([128, H, K]),
                                     ALU.mult).then_inc(c_norm, 1)
                if ahead.back(4).live():
                    inverse_root(ahead.back(4), c_var, c_scale)

            steps(pool, 4, step_c)

            def weigh(t, half):
                pool.wait_ge(d_z, t.n * 2 + half + 1)
                pool.wait_ge(d_comb, t.n + 1)
                if half == 0:
                    wait(pool, d_it6, t.n - 1)
                    wait(pool, d_it5, (t.n - 1) * 2)
                ps.tensor_tensor(
                    inter[:, t.odd, half * 512:(half + 1) * 512].rearrange("p (e f) -> p e f", f=F1),
                    z2[:, half, :].rearrange("p (e f) -> p e f", f=F1),
                    comb[:, t.odd, half * 8:half * 8 + 8].unsqueeze(2).broadcast_to([128, 8, F1]),
                    ALU.mult).then_inc(d_mul, 1)

            def step_d(t):
                if t.back(1).live():
                    weigh(t.back(1), 1)
                if t.live():
                    weigh(t, 0)

            steps(pool, 1, step_d)

        @block.scalar
        def _(act):
            ac = nc.scalar
            srcs = {"x": (xr[:, :, :], x), "rows": (rows_s[:, :, :], rows.unsqueeze(0).broadcast_to([128, 3, D])),
                    "mask": (mask_s[:, :, :], mask), "hmask": (hmask_s[:, :], hmask),
                    "vmask": (vmask_s[:, :, :], vmask), "wo0": (wo0_s[:, :, :], wo0)}
            for n, (dst, src) in srcs.items():
                act.dma_start(dst, src).then_inc(load[n], 16)

            def group(g):
                act.wait_ge(first_ready[g % 8], g // 8 + 1)
                return bank[g % 8]

            loaded(act, "ctx")
            ac.activation(ctx_hi[:, :], ctx_s[:, :], ACT.Copy).then_inc(ctx_split, 1)
            loaded(act, "cols")
            for i in range(2):
                g = G_K + i
                ac.activation(k_t[:, i * NKH:(i + 1) * NKH], group(g)[:, 0:NKH], ACT.Identity,
                              bias=cols_s[:, 1:2]).then_inc(first_done[g % 8], 1)
            for i in range(2):
                g = G_V + i
                ac.activation(v_t[:, i * NKH:(i + 1) * NKH], group(g)[:, 0:NKH], ACT.Identity,
                              bias=cols_s[:, 2:3]).then_inc(first_done[g % 8], 1)
            loaded(act, "ident")
            ac.activation(idb[:, :], id_s[:, 0, :], ACT.Copy).then_inc(consts_done, 1)
            loaded(act, "gate", "wout")
            ac.activation(tanh_g[:, :], gate_s[:, :], ACT.Tanh).then_inc(tanh_done, 1)
            act.wait_ge(tanh_done, 1)
            act.wait_ge(bd_zero, 2)
            for h in range(2):
                half = slice(64 * h, 64 * h + 64)
                ac.activation(pair_o[half, :, h, :], wout_s[half, :, :], ACT.Copy,
                              scale=tanh_g[half, 0:1]).then_inc(outw_done, 1)

            def wq_group(i):
                g = G_WQ + i
                src = group(g)[:, :].rearrange("p (c d) -> p c d", c=4)
                for h in range(2):
                    half = slice(64 * h, 64 * h + 64)
                    last = ac.activation(pair_q[half, 4 * i:4 * i + 4, h, :], src[half, :, :], ACT.Copy)
                last.then_inc(first_done[g % 8], 1)

            for i in range(2):
                wq_group(i)
            for g0, hi in ((G_A, a_hi), (G_M, m_hi)):
                for i in range(4):
                    ac.activation(hi[:, i * 512:(i + 1) * 512], group(g0 + i)[:, :], ACT.Copy).then_inc(hi_done, 1)
            for i in range(2):
                g = G_XT + i
                ac.activation(xn_t[:, i * 512:(i + 1) * 512], group(g)[:, :], ACT.Copy).then_inc(first_done[g % 8], 1)
            for i in range(2):
                g = G_Q + i
                ac.activation(q_t[:, i * 512:(i + 1) * 512], group(g)[:, :], ACT.Identity,
                              bias=cols_s[:, 0:1]).then_inc(first_done[g % 8], 1)
            g = G_WG
            ac.activation(wgt[:, :], group(g)[:, 0:E0], ACT.Copy).then_inc(first_done[g % 8], 1)
            for i in range(0, N_B, 2):
                g = G_B + i
                ac.activation(b_all[:, 0:4, (i // 2) * K:(i // 2) * K + K],
                              group(g)[:, 0:NKH].rearrange("p (b k) -> p b k", k=K),
                              ACT.Copy).then_inc(first_done[g % 8], 1)

            def step_w(t):
                wait(act, vw_stored[t.odd], t.pairs(16))
                for c in (0, 2):
                    act.wait_ge(vw_ready, t.n * 4 + c + 1)
                    ac.activation(vws[:, t.odd, c, :], bank[c][0:K, :], ACT.Copy).then_inc(vw_act, 1)
                act.wait_ge(w1t_ready, t.n + 1)
                ac.activation(w1_hi[:, bass.ds(t.n, 1), :].rearrange("p o f -> p (o f)"), bank[4 + t.odd][:, :],
                              ACT.Copy).then_inc(w1t_hi, 1)

            act.wait_ge(first_ready[(N_FIRST - 1) % 8], (N_FIRST - 1) // 8 + 1)
            steps(act, 0, step_w)

            for stored in vw_stored:
                act.wait_ge(stored, 16 * (B // 2))

            def probs_a(q, c):
                c0, c1 = CHUNKS[c]
                if c == 0:
                    wait(act, a_ready[6], q.n - 1)
                b = 3 if c != 1 else 4
                act.wait_ge(a_ready[b], q.n * 2 + c // 2 + 1 if b == 3 else q.n + 1)
                src = bank[b][:, 0:(c1 - c0) * 128].rearrange("p (c q) -> p c q", q=128)
                if c < 2:
                    ins = ac.activation(pt[:, q.odd, c0:c1, :], src, ACT.Copy)
                else:
                    ac.activation(pt[:, q.odd, c0:c0 + 1, :], src[:, 0:1, :], ACT.Copy)
                    ins = ac.activation(pt[0:KLAST, q.odd, c0 + 1, :], src[0:KLAST, 1, :], ACT.Copy)
                ins.then_inc(a_done[b], 1)

            def exp_a(t, g):
                h0, h1 = HEADS[g]
                act.wait_ge(a_sub, t.n * 3 + g + 1)
                cut = p[:, t.odd, h0 * K:h1 * K]
                ac.activation(cut, cut, ACT.Exp, scale=HD ** -0.5).then_inc(a_exp, 1)

            def step_a(t):
                q1, q2 = t.back(1), t.back(2)
                if q2.live():
                    act.wait_ge(a_ready[7], q2.n * 3 + 1)
                    ac.activation(ot[:, q2.odd, 0:128], bank[7][:, 0:128], ACT.Copy).then_inc(a_done[7], 1)
                if t.live():
                    exp_a(t, 0)
                if q1.live():
                    probs_a(q1, 0)
                if t.live():
                    exp_a(t, 1)
                if q1.live():
                    probs_a(q1, 1)
                    probs_a(q1, 2)
                if t.live():
                    exp_a(t, 2)
                if q2.live():
                    act.wait_ge(a_ready[7], q2.n * 3 + 3)
                    ac.activation(columns(xn_t, q2, S), bank[7][:, 256:384], ACT.Copy).then_inc(a_done[7], 1)

            steps(act, 2, step_a)

            def router_exp(t, n, neg_sem, exp_sem):
                act.wait_ge(neg_sem, t.n + 1)
                ac.activation(ee[:, t.odd, 0:n], lg[:, 0:n], ACT.Exp, bias=neg[:, t.odd:t.odd + 1],
                              accum_out=ssum[:, t.odd:t.odd + 1]).then_inc(exp_sem, 1)

            def halves(t, there, n, used, m, hi_sem):
                act.wait_ge(there, n)
                wait(act, used, m)
                ac.activation(lhs_hi[:, t.odd, :], columns(xn_t, t, S), ACT.Copy).then_inc(hi_sem, 1)

            def tanh_b(t, e):
                act.wait_ge(b_h, t.n * E0 + e + 1)
                ac.activation(th[:, e % 4, :], bank[e % 4][:, F0:2 * F0], ACT.Tanh, scale=0.5).then_inc(b_tanh, 1)

            def step_b(ahead):
                t, q1, q2, q3 = ahead.back(1), ahead.back(2), ahead.back(3), ahead.back(4)
                if q1.live():
                    tanh_b(q1, 6)
                    tanh_b(q1, 7)
                if t.live():
                    tanh_b(t, 0)
                    tanh_b(t, 1)
                    router_exp(t, E0, b_neg, b_exp)
                if ahead.live():
                    halves(ahead, a_done[7], ahead.n * 3 + 3, b_h, (ahead.n - 1) * E0, b_prep_hi)
                if q2.live():
                    act.wait_ge(b_gt, q2.n + 1)
                    ac.activation(ot[:, q2.odd, :], bank[5][:, 0:256], ACT.Copy).then_inc(b_gt_done, 1)
                if t.live():
                    tanh_b(t, 2)
                    tanh_b(t, 3)
                    tanh_b(t, 4)
                    tanh_b(t, 5)
                if q3.live():
                    act.wait_ge(b_xt, q3.n + 1)
                    ac.activation(columns(xn_t, q3, S), bank[7][:, 0:128], ACT.Copy).then_inc(b_xt_done, 1)

            steps(act, 4, step_b)
            loaded(act, "gu", "rsh")
            ac.activation(wide_hi[:, 0:2 * EI], gu_s[:, :], ACT.Copy).then_inc(wide_act, 1)
            ac.activation(wide_hi[:, 2 * EI:], rsh_s[:, :], ACT.Copy).then_inc(wide_act, 1)

            def probs_c(q, c):
                c0, c1 = CHUNKS[c]
                if c == 0:
                    wait(act, c_y, q.n - 1)
                b = PT_BANKS[c]
                act.wait_ge(c_pt[c], q.n + 1)
                src = bank[b][:, 0:(c1 - c0) * 128].rearrange("p (c q) -> p c q", q=128)
                if c < 2:
                    ins = ac.activation(pt[:, q.odd, c0:c1, :], src, ACT.Copy)
                else:
                    ac.activation(pt[:, q.odd, c0:c0 + 1, :], src[:, 0:1, :], ACT.Copy)
                    ins = ac.activation(pt[0:KLAST, q.odd, c0 + 1, :], src[0:KLAST, 1, :], ACT.Copy)
                ins.then_inc(c_pt_done[c], 1)

            def exp_c(t, g):
                h0, h1 = HEADS[g]
                act.wait_ge(c_sub, t.n * 3 + g + 1)
                cut = p[:, t.odd, h0 * K:h1 * K]
                ac.activation(cut, cut, ACT.Exp, scale=64 ** -0.5).then_inc(c_exp, 1)

            def step_c(t):
                q2, q3 = t.back(2), t.back(3)
                if q2.live():
                    probs_c(q2, 0)
                    probs_c(q2, 1)
                if t.live():
                    exp_c(t, 0)
                if q2.live():
                    probs_c(q2, 2)
                if t.live():
                    exp_c(t, 1)
                    exp_c(t, 2)
                if q3.live():
                    act.wait_ge(c_xt, q3.n + 1)
                    ac.activation(columns(xn_t, q3, S), bank[6][:, 0:128], ACT.Copy).then_inc(c_xt_done, 1)

            steps(act, 3, step_c)

            def tanh_d(t, h):
                act.wait_ge(d_gu, t.n * 2 + h + 1)
                ac.activation(tg[:, h, :], bank[2 * h][:, :], ACT.Tanh, scale=0.5).then_inc(d_tanh, 1)

            def step_d(ahead):
                t, q = ahead.back(1), ahead.back(2)
                if q.live():
                    tanh_d(q, 1)
                    act.wait_ge(d_it5, q.n * 2 + 1)
                    ac.activation(it[:, q.odd, 0:4, :], bank[5][:, :].rearrange("p (c q) -> p c q", q=128),
                                  ACT.Copy).then_inc(d_it5_done, 1)
                if t.live():
                    router_exp(t, E1, d_neg, d_exp)
                    ac.activation(tg[:, 2, 0:FS], bank[4][:, 0:FS], ACT.Tanh, scale=0.5).then_inc(d_tanh_sh, 1)
                    tanh_d(t, 0)
                if ahead.live():
                    halves(ahead, c_xt_done, ahead.n + 1, d_gu, (ahead.n - 1) * 2, d_prep_hi)
                if q.live():
                    act.wait_ge(d_it6, q.n + 1)
                    ac.activation(it[:, q.odd, 4:8, :], bank[6][:, :].rearrange("p (c q) -> p c q", q=128),
                                  ACT.Copy).then_inc(d_it6_done, 1)
                    act.wait_ge(d_it5, q.n * 2 + 2)
                    ac.activation(it[:, q.odd, 8, :], bank[5][:, 0:128], ACT.Copy).then_inc(d_it5_done, 1)

            steps(act, 2, step_d)

        @block.vector
        def _(dve):
            ve = nc.vector
            own = [0]

            def link(ins):
                own[0] += 1
                ins.then_inc(dve_first, 1)
                dve.wait_ge(dve_first, own[0])

            def group(g):
                dve.wait_ge(first_ready[g % 8], g // 8 + 1)
                return bank[g % 8]

            def row_stats(chain, t):
                chain.made(ve.bn_stats(out=st[:, t.odd, :], in_=tile_of(xr, t)))

            def row_mean(chain, t):
                chain.made(ve.bn_aggr(out=ag[:, t.odd, :], in_=st[:, t.odd, :]))

            def row_var(chain, t, var_sem, twice=False):
                u = t.odd
                chain.need(t, 2)
                ve.tensor_scalar(var[:, u:u + 1], ag[:, u, 1:2], 1.0 + EPS if twice else 1.0,
                                 EPS * EPS if twice else EPS, ALU.mult, ALU.add).then_inc(var_sem, 1)

            def normed(row, t, scale_sem, xh_sem, last=None):
                u = t.odd
                dve.wait_ge(scale_sem, t.n + 1)
                n = D if last is None else D - 1
                if last is not None:
                    ve.memset(xh[:, u, D - 1:D], last)
                ve.tensor_scalar(xh[:, u, 0:n], row[:, 0:n], ag[:, u, 0:1], scale[:, u:u + 1],
                                 ALU.subtract, ALU.mult).then_inc(xh_sem, 1)

            loaded(dve, "cols", "ident")
            link(ve.tensor_scalar(tt[:, :], id_s[:, 1, :], cols_s[:, 3:4], None, ALU.mult))
            ve.tensor_copy(tt[:, D - 1:D], cols_s[:, 4:5]).then_inc(tt_done, 1)
            dve.wait_ge(ctx_split, 1)
            loaded(dve, "ctx")
            ve.tensor_tensor(ctx_lo[:, :], ctx_s[:, :], ctx_hi[:, :].bitcast(f32), ALU.subtract).then_inc(ctx_split, 1)
            loaded(dve, "x")
            for b in range(B):
                link(ve.bn_stats(out=st[:, b % 2, :], in_=xr[:, b, :]))
                link(ve.bn_aggr(out=ag8[:, b, :], in_=st[:, b % 2, :]))
            ve.tensor_scalar(var8[:, :], ag8[:, :, 1], EPS, None, ALU.add).then_inc(var8_done, 1)
            dve.wait_ge(scale8_done, 1)
            for b in range(B):
                ve.tensor_scalar(xh0[:, b, :], xr[:, b, :], ag8[:, b, 0:1], scale8[:, b:b + 1],
                                 ALU.subtract, ALU.mult).then_inc(xh0_done, 1)
            loaded(dve, "mask")
            ve.tensor_scalar(maskneg[:, :, :], mask_s[:, :, :], MASKED, None, ALU.mult).then_inc(consts_done, 1)
            link(ve.memset(mark[:, :], BIG))
            link(ve.memset(lg[:, :], BIG))
            n_hi = 0
            for g0, hi, lo in ((G_A, a_hi, a_lo), (G_M, m_hi, m_lo)):
                for i in range(4):
                    n_hi += 1
                    g, cut = g0 + i, slice(i * 512, (i + 1) * 512)
                    src = group(g)
                    dve.wait_ge(hi_done, n_hi)
                    ve.tensor_tensor(lo[:, cut], src[:, :], hi[:, cut].bitcast(f32),
                                     ALU.subtract).then_inc(first_done[g % 8], 1)
            for i in range(1, N_B, 2):
                g = G_B + i
                ve.tensor_copy(b_all[:, 4:8, (i // 2) * K:(i // 2) * K + K],
                               group(g)[:, 0:NKH].rearrange("p (b k) -> p b k", k=K)).then_inc(first_done[g % 8], 1)

            def step_w(t):
                wait(dve, vw_stored[t.odd], t.pairs(16))
                for c in (1, 3):
                    dve.wait_ge(vw_ready, t.n * 4 + c + 1)
                    ve.tensor_copy(vws[:, t.odd, c, :], bank[c][0:K, :]).then_inc(vw_dve, 1)
                dve.wait_ge(w1t_hi, t.n + 1)
                e = bass.ds(t.n, 1)
                ve.tensor_tensor(w1_lo[:, e, :].rearrange("p o f -> p (o f)"), bank[4 + t.odd][:, :],
                                 w1_hi[:, e, :].rearrange("p o f -> p (o f)").bitcast(f32),
                                 ALU.subtract).then_inc(w1t_done, 1)

            steps(dve, 0, step_w)

            for stored in vw_stored:
                dve.wait_ge(stored, 16 * (B // 2))
            dve.wait_ge(w1t_done, B)
            loaded(dve, "vmask")
            dve.wait_ge(bias0_done, 1)
            for u in range(2):
                ve.tensor_copy(vbd[:, u, :, :].rearrange("p c (h o) -> p c h o", o=OW)[:, :, :, HD],
                               vmask_s[:, :, :].rearrange("p c (h o) -> p c h o", o=HD)[:, :, :, 0]).then_inc(ones_done, 1)

            def maximum(t, g, scores):
                h0, h1 = HEADS[g]
                dve.wait_ge(scores, t.n * 3 + g + 1)
                ve.tensor_reduce(mx[:, t.odd, h0:h1], bank[g][:, 0:(h1 - h0) * K].rearrange("p (h k) -> p h k", k=K),
                                 AX.X, ALU.max).then_inc(scores_max, 1)

            def minus_max(t, g, first, sub):
                h0, h1 = HEADS[g]
                dve.wait_ge(scores_max, (first + t.n) * 3 + g + 1)
                ve.tensor_tensor(p[:, t.odd, h0 * K:h1 * K].rearrange("p (h k) -> p h k", k=K),
                                 bank[g][:, 0:(h1 - h0) * K].rearrange("p (h k) -> p h k", k=K),
                                 mx[:, t.odd, h0:h1].unsqueeze(2).broadcast_to([128, h1 - h0, K]),
                                 ALU.subtract).then_inc(sub, 1)

            chain_o, chain_y = Chain(dve, a_chain, 1), Chain(dve, a_chain_y, 2)

            def values(t, c):
                c0, c1 = CHUNKS[c]
                if c == 0:
                    wait(dve, a_ready[6], t.n - 1)
                dve.wait_ge(a_ready[5], t.n * 3 + c + 1)
                src = bank[5][:, 0:(c1 - c0) * 128].rearrange("p (c h o) -> p c h o", h=H, o=HD)
                msk = vmask_s[:, c0:c1, :].rearrange("p c (h o) -> p c h o", o=HD)
                dst = vbd[:, t.odd, c0:c1, :].rearrange("p c (h o) -> p c h o", o=OW)[:, :, :, 0:HD]
                if c < 2:
                    ins = ve.tensor_tensor(dst, src, msk, ALU.mult)
                else:
                    ve.tensor_tensor(dst[:, 0], src[:, 0], msk[:, 0], ALU.mult)
                    ins = ve.tensor_tensor(dst[0:KLAST, 1], src[0:KLAST, 1], msk[0:KLAST, 1], ALU.mult)
                ins.then_inc(a_done[5], 1)

            def step_a(t):
                q = t.back(2)
                heads = bank[6][:, 0:H * OW].rearrange("p (h o) -> p h o", o=OW)
                if q.live():
                    dve.wait_ge(a_ready[6], q.n + 1)
                    chain_o.made(ve.reciprocal(rinv[:, q.odd, :], heads[:, :, HD]))
                if t.live():
                    maximum(t, 0, a_scores)
                if q.live():
                    chain_o.need(q, 1)
                    ve.tensor_tensor(o_n[:, q.odd, :, :], heads[:, :, 0:HD],
                                     rinv[:, q.odd, :].unsqueeze(2).broadcast_to([128, H, HD]),
                                     ALU.mult).then_inc(a_done[6], 1)
                if t.live():
                    values(t, 0)
                    maximum(t, 1, a_scores)
                    wait(dve, a_ready[3], (t.n - 1) * 2)
                    minus_max(t, 0, 0, a_sub)
                    maximum(t, 2, a_scores)
                if q.live():
                    row = tile_of(xr, q)
                    dve.wait_ge(a_ready[7], q.n * 3 + 2)
                    ve.tensor_tensor(row, bank[7][:, 128:256], row, ALU.add).then_inc(a_done[7], 1)
                if t.live():
                    minus_max(t, 1, 0, a_sub)
                if q.live():
                    dve.wait_ge(a_done[7], q.n * 3 + 2)
                if t.live():
                    values(t, 1)
                if q.live():
                    row_stats(chain_y, q)
                if t.live():
                    minus_max(t, 2, 0, a_sub)
                if q.live():
                    chain_y.need(q, 1)
                if t.live():
                    values(t, 2)
                if q.live():
                    row_mean(chain_y, q)
                    row_var(chain_y, q, a_var)
                    normed(tile_of(xr, q), q, a_scale, a_xh, 1.0)

            steps(dve, 2, step_a)

            def largest(chain, t, n):
                chain.made(ve.max(out=top[:, :], in_=lg[:, 0:n]))

            def mark_top(chain, t, neg_sem):
                chain.need(t, 2)
                ve.tensor_scalar(neg[:, t.odd:t.odd + 1], top[:, 0:1], -1.0, None, ALU.mult).then_inc(neg_sem, 1)
                chain.made(ve.tensor_copy(mark[:, 0:2], top[:, 0:2]))

            def without_top(chain, t, n):
                chain.made(ve.match_replace(out=lr[:, 0:n + 6], in_to_replace=mark[:, :],
                                            in_values=lg[:, 0:n + 6], imm_value=-BIG))

            def select(t, n, logits_done):
                ve.tensor_tensor(sel[:, 0:n], lr[:, 0:n], lg[:, 0:n], ALU.is_lt).then_inc(logits_done, 1)

            def selected(chain, t, n, logits_done, exp_sem):
                dve.wait_ge(logits_done, t.n + 1)
                dve.wait_ge(exp_sem, t.n + 1)
                chain.made(ve.tensor_tensor(es[:, 0:n], ee[:, t.odd, 0:n], sel[:, 0:n], ALU.mult))

            chain_r, chain_y = Chain(dve, b_chain, 10), Chain(dve, b_chain_y, 2)

            def low_half(t, hi_sem, done_sem):
                dve.wait_ge(hi_sem, t.n + 1)
                ve.tensor_tensor(lhs_lo[:, t.odd, :], columns(xn_t, t, S), lhs_hi[:, t.odd, :].bitcast(f32),
                                 ALU.subtract).then_inc(done_sem, 1)

            def gated(t, e):
                dve.wait_ge(b_tanh, t.n * E0 + e + 1)
                if e < EP:
                    wait(dve, b_part, (t.n - 1) * 2 + 1)
                ve.scalar_tensor_tensor(out=ub[:, e, :], in0=th[:, e % 4, :], scalar=1.0,
                                        in1=bank[e % 4][:, 0:F0], op0=ALU.add, op1=ALU.mult).then_inc(b_u, 1)

            def add_expert(q, k):
                if k == 0:
                    dve.wait_ge(b_acc, q.n + 1)
                    dve.wait_ge(b_u, q.n * E0 + E0)
                wait(dve, b_sum, q.n * (E0 - EP) + k)
                ve.scalar_tensor_tensor(out=gb[:, q.odd, :], in0=ub[:, EP + k, :],
                                        scalar=comb[:, q.odd, EP + k:EP + k + 1], in1=gb[:, q.odd, :],
                                        op0=ALU.mult, op1=ALU.add).then_inc(b_sum, 1)

            def step_b(ahead):
                t, q1, q2, q3 = ahead.back(1), ahead.back(2), ahead.back(3), ahead.back(4)
                if q1.live():
                    gated(q1, 6)
                if q3.live():
                    dve.wait_ge(b_y_done, q3.n + 1)
                if q1.live():
                    gated(q1, 7)
                if q3.live():
                    row_stats(chain_y, q3)
                if t.live():
                    dve.wait_ge(b_lg, t.n + 1)
                    chain_r.made(ve.tensor_copy(lg[:, 0:E0], bank[4][:, 0:E0]))
                if q3.live():
                    chain_y.need(q3, 1)
                if t.live():
                    chain_r.need(t, 1)
                    gated(t, 0)
                    largest(chain_r, t, E0)
                if q3.live():
                    row_mean(chain_y, q3)
                if q1.live():
                    add_expert(q1, 0)
                if t.live():
                    mark_top(chain_r, t, b_neg)
                if q3.live():
                    row_var(chain_y, q3, b_var, True)
                if t.live():
                    chain_r.need(t, 3)
                    gated(t, 1)
                    without_top(chain_r, t, E0)
                if q1.live():
                    add_expert(q1, 1)
                if t.live():
                    chain_r.need(t, 4)
                    select(t, E0, b_lg_done)
                    gated(t, 2)
                    selected(chain_r, t, E0, b_lg_done, b_exp)
                if q1.live():
                    add_expert(q1, 2)
                if t.live():
                    chain_r.need(t, 5)
                    chain_r.made(ve.tensor_reduce(s2[:, 0:1], es[:, 0:E0], AX.X, ALU.add))
                    gated(t, 3)
                    chain_r.need(t, 6)
                    chain_r.made(ve.scalar_tensor_tensor(out=s2[:, 1:2], in0=ssum[:, t.odd:t.odd + 1],
                                                         scalar=EPS_TOP, in1=s2[:, 0:1],
                                                         op0=ALU.mult, op1=ALU.add))
                if q1.live():
                    add_expert(q1, 3)
                if t.live():
                    chain_r.need(t, 7)
                    chain_r.made(ve.reciprocal(s2[:, 2:3], s2[:, 1:2]))
                if ahead.live():
                    low_half(ahead, b_prep_hi, b_prep)
                if t.live():
                    chain_r.need(t, 8)
                    ve.tensor_scalar(comb[:, t.odd, 0:E0], es[:, 0:E0], s2[:, 2:3], 0.5,
                                     ALU.mult, ALU.mult).then_inc(b_comb, 1)
                    chain_r.made(ve.tensor_tensor(csum[:, t.odd:t.odd + 1], s2[:, 0:1], s2[:, 2:3], ALU.mult))
                    gated(t, 4)
                    chain_r.need(t, 9)
                    row = tile_of(xr, t)
                    chain_r.made(ve.scalar_tensor_tensor(out=row, in0=rows_s[:, 1, :],
                                                         scalar=csum[:, t.odd:t.odd + 1], in1=row,
                                                         op0=ALU.mult, op1=ALU.add))
                if q3.live():
                    normed(tile_of(xr, q3), q3, b_scale, b_xh, 1.0)
                if q2.live():
                    dve.wait_ge(b_y, q2.n + 1)
                    chain_r.need(q2, 10)
                    row = tile_of(xr, q2)
                    ve.tensor_tensor(row, bank[6][:, 0:D], row, ALU.add).then_inc(b_y_done, 1)
                if t.live():
                    gated(t, 5)

            steps(dve, 4, step_b)

            chain_y = Chain(dve, c_chain_y, 2)

            def row_sum(t, g):
                h0, h1 = HEADS[g]
                dve.wait_ge(c_exp, t.n * 3 + g + 1)
                ins = ve.tensor_reduce(rs[:, t.odd, h0:h1],
                                       p[:, t.odd, h0 * K:h1 * K].rearrange("p (h k) -> p h k", k=K),
                                       AX.X, ALU.add)
                if g == len(HEADS) - 1:
                    ins.then_inc(c_chain, 1)

            def step_c(t):
                q1, q = t.back(1), t.back(3)
                if q1.live():
                    for g in range(len(HEADS)):
                        row_sum(q1, g)
                if q.live():
                    dve.wait_ge(c_y, q.n + 1)
                    row = tile_of(xr, q)
                    ve.tensor_tensor(row, bank[5][:, 0:D], row, ALU.add).then_inc(c_y_done, 1)
                if q1.live():
                    dve.wait_ge(c_chain, q1.n + 1)
                    wait(dve, c_norm, q1.n - 1)
                    ve.reciprocal(rinv[:, q1.odd, :], rs[:, q1.odd, :]).then_inc(c_rs, 1)
                if t.live():
                    maximum(t, 0, c_scores)
                if q.live():
                    dve.wait_ge(c_y_done, q.n + 1)
                if t.live():
                    maximum(t, 1, c_scores)
                if q.live():
                    row_stats(chain_y, q)
                if t.live():
                    maximum(t, 2, c_scores)
                if q.live():
                    chain_y.need(q, 1)
                if t.live():
                    wait(dve, c_pt[2], t.n - 1)
                    minus_max(t, 0, B, c_sub)
                if q.live():
                    row_mean(chain_y, q)
                if t.live():
                    minus_max(t, 1, B, c_sub)
                if q.live():
                    row_var(chain_y, q, c_var)
                if t.live():
                    minus_max(t, 2, B, c_sub)
                if q.live():
                    normed(tile_of(xr, q), q, c_scale, c_xh)

            steps(dve, 3, step_c)

            chain_r = Chain(dve, d_chain, 7)
            dve.wait_ge(c_rs, B)
            link(ve.memset(lg[:, E1:24], BIG))

            def gate(t, h):
                dve.wait_ge(d_tanh, t.n * 2 + h + 1)
                ve.scalar_tensor_tensor(out=z1[:, h, :], in0=tg[:, h, :], scalar=1.0, in1=bank[2 * h][:, :],
                                        op0=ALU.add, op1=ALU.mult).then_inc(d_z1, 1)

            def gate_times_up(t, h):
                dve.wait_ge(d_z1, t.n * 2 + h + 1)
                wait(dve, d_mul, (t.n - 1) * 2 + h + 1)
                ve.tensor_tensor(z2[:, h, :], z1[:, h, :], bank[2 * h + 1][:, :], ALU.mult).then_inc(d_z, 1)

            def step_d(ahead):
                t, q, q2 = ahead.back(1), ahead.back(2), ahead.back(3)
                if q.live():
                    gate(q, 1)
                if t.live():
                    dve.wait_ge(d_sh, t.n + 1)
                    chain_r.made(ve.tensor_copy(lg[:, 0:E1], bank[4][:, 2 * FS:2 * FS + E1]))
                if q2.live():
                    wait(dve, d_out[q2.odd], q2.pairs(16))
                    dve.wait_ge(d_y, q2.n + 1)
                    ve.tensor_tensor(yb[:, q2.odd, :], bank[7][:, 0:D], tile_of(xr, q2), ALU.add).then_inc(d_y_done, 1)
                if t.live():
                    chain_r.need(t, 1)
                if q.live():
                    gate_times_up(q, 1)
                if t.live():
                    largest(chain_r, t, E1)
                    mark_top(chain_r, t, d_neg)
                    chain_r.need(t, 3)
                    dve.wait_ge(d_tanh_sh, t.n + 1)
                    chain_r.made(ve.scalar_tensor_tensor(out=z1[:, 2, 0:FS], in0=tg[:, 2, 0:FS], scalar=1.0,
                                                         in1=bank[4][:, 0:FS], op0=ALU.add, op1=ALU.mult))
                    without_top(chain_r, t, E1)
                    wait(dve, d_it5, (t.n - 1) * 2)
                    chain_r.need(t, 4)
                    ve.scalar_tensor_tensor(out=inter[:, t.odd, EI:EI + FS], in0=z1[:, 2, 0:FS], scalar=0.5,
                                            in1=bank[4][:, FS:2 * FS], op0=ALU.mult,
                                            op1=ALU.mult).then_inc(d_sh_done, 1)
                    chain_r.need(t, 5)
                    select(t, E1, d_lg_done)
                    gate(t, 0)
                    selected(chain_r, t, E1, d_lg_done, d_exp)
                    chain_r.made(ve.reciprocal(s2[:, 2:3], ssum[:, t.odd:t.odd + 1]))
                if ahead.live():
                    low_half(ahead, d_prep_hi, d_prep)
                if t.live():
                    gate_times_up(t, 0)
                    chain_r.need(t, 7)
                    wait(dve, d_mul, (t.n - 1) * 2)
                    ve.tensor_scalar(comb[:, t.odd, :], es[:, :], s2[:, 2:3], 0.5,
                                     ALU.mult, ALU.mult).then_inc(d_comb, 1)

            steps(dve, 3, step_d)

        @block.tensor
        def _(pe):
            te = nc.tensor

            def mm3(dst, a_hi_, a_lo_, b_hi_, b_lo_):
                te.matmul(dst, a_hi_, b_hi_, start=True, stop=False)
                te.matmul(dst, a_hi_, b_lo_, start=False, stop=False)
                return te.matmul(dst, a_lo_, b_hi_, start=False, stop=True)

            def group(g):
                if g >= 8:
                    pe.wait_ge(first_done[g % 8], g // 8)
                return bank[g % 8]

            def ready(ins, g):
                ins.then_inc(first_ready[g % 8], 1)

            loaded(pe, "ctx", "w0")
            for g0, w in ((G_K, 1), (G_V, 2)):
                for i in range(2):
                    ready(te.matmul(group(g0 + i)[:, 0:NKH], w0_s[:, w, :], ctx_s[:, i * NKH:(i + 1) * NKH],
                                    start=True, stop=True), g0 + i)
            loaded(pe, "wq")
            pe.wait_ge(tt_done, 1)
            for i in range(2):
                dst = group(G_WQ + i)
                for c in range(4):
                    j = 4 * i + c
                    last = te.matmul(dst[:, c * 128:(c + 1) * 128], wq_s[:, j * 128:(j + 1) * 128], tt[:, :],
                                     start=True, stop=True)
                ready(last, G_WQ + i)
            pe.wait_ge(bd_zero, 2)
            loaded(pe, "wk")
            for i in range(2):
                pe.wait_ge(first_done[(G_WQ + i) % 8], (G_WQ + i) // 8 + 1)
            for g0, lhs_w, rhs_w in ((G_A, wk_s, pair_q), (G_M, wv_s, pair_o)):
                if g0 == G_M:
                    loaded(pe, "wv")
                    pe.wait_ge(outw_done, 2)
                for i in range(4):
                    dst = group(g0 + i)
                    for c in range(2):
                        j = 2 * i + c
                        last = te.matmul(dst[:, c * 256:(c + 1) * 256], lhs_w[:, j, :],
                                         rhs_w[:, j, :, :].rearrange("p h d -> p (h d)"), start=True, stop=True)
                    ready(last, g0 + i)
            loaded(pe, "ident")
            for i in range(2):
                dst = group(G_XT + i)
                for c in range(4):
                    pe.wait_ge(xh0_done, 4 * i + c + 1)
                    last = te.transpose(dst[:, c * 128:(c + 1) * 128], xh0[:, 4 * i + c, :], id_s[:, 0, :])
                ready(last, G_XT + i)
            for i in range(2):
                dst = group(G_Q + i)
                pe.wait_ge(first_done[(G_XT + i) % 8], (G_XT + i) // 8 + 1)
                ready(te.matmul(dst[:, :], w0_s[:, 0, :], xn_t[:, i * 512:(i + 1) * 512], start=True, stop=True),
                      G_Q + i)
            pe.wait_ge(wg_done, 1)
            ready(te.transpose(group(G_WG)[:, 0:E0], wg_s[:, :], id_s[0:E0, 0, 0:E0]), G_WG)
            pe.wait_ge(ctx_split, 2)
            for i in range(4):
                pe.wait_ge(first_done[(G_A + i) % 8], (G_A + i) // 8 + 1)
            for h in range(H):
                for i in range(2):
                    g = G_B + 2 * h + i
                    cut = slice(h * D, h * D + D)
                    ready(mm3(group(g)[:, 0:NKH], a_hi[:, cut], a_lo[:, cut],
                              ctx_hi[:, i * NKH:(i + 1) * NKH], ctx_lo[:, i * NKH:(i + 1) * NKH]), g)
            for i in range(8):
                n = len([g for g in range(N_FIRST) if g % 8 == i])
                pe.wait_ge(first_done[i], n)

            def step_w(t):
                pe.wait_ge(cb_done, t.n + 1)
                for c in range(4):
                    wait(pe, vw_act if c % 2 == 0 else vw_dve, (t.n - 1) * 2 + c // 2 + 1)
                    cut = slice(c * 512, (c + 1) * 512)
                    mm3(bank[c][0:K, :], cb_hi[:, t.odd, :], cb_lo[:, t.odd, :], m_hi[:, cut],
                        m_lo[:, cut]).then_inc(vw_ready, 1)
                wait(pe, w1t_done, t.n - 1)
                pe.wait_ge(w1_done, t.n + 1)
                for c in range(4):
                    last = te.transpose(bank[4 + t.odd][:, c * 128:(c + 1) * 128], w1f[:, t.odd, c, :],
                                        id_s[:, 0, :])
                last.then_inc(w1t_ready, 1)

            steps(pe, 0, step_w)

            for i in range(0, 4):
                pe.wait_ge(vw_act if i % 2 == 0 else vw_dve, B * 2)
            pe.wait_ge(w1t_done, B)
            pe.wait_ge(consts_done, 2)
            pe.wait_ge(ones_done, 2)

            def scores_a(t, g):
                h0, h1 = HEADS[g]
                dst = bank[g][:, 0:(h1 - h0) * K]
                wait(pe, a_sub, (t.n - 1) * 3 + g + 1)
                te.matmul(dst, lhs[:, t.odd, :], kbd[:, t.odd, h0 * K:h1 * K], start=True, stop=False)
                te.matmul(dst.rearrange("p (h k) -> p h k", k=K), idb[:, :],
                          maskneg[:, bass.ds(t.n, 1), :].broadcast_to([128, h1 - h0, K]),
                          start=False, stop=True).then_inc(a_scores, 1)

            def probs(q, c, b, ready, done, n):
                c0, c1 = CHUNKS[c]
                wait(pe, done, n)
                for j in range(c0, c1):
                    m = rows_of(j)
                    last = te.transpose(bank[b][0:m, (j - c0) * 128:(j - c0 + 1) * 128],
                                        p[:, q.odd, j * 128:j * 128 + m], id_s[:, 0, :])
                last.then_inc(ready, 1)

            def values_a(t, c):
                c0, c1 = CHUNKS[c]
                wait(pe, a_done[5], t.n * 3 + c)
                flat = vper[:, t.odd, :, :].rearrange("p a k -> p (a k)")
                for j in range(c0, c1):
                    m, at = rows_of(j), (j * 128) % K
                    last = te.transpose(bank[5][0:m, (j - c0) * 128:(j - c0 + 1) * 128],
                                        flat[:, at:at + m], id_s[:, 0, :])
                last.then_inc(a_ready[5], 1)

            def step_a(t):
                q1, q2 = t.back(1), t.back(2)
                if t.live():
                    pe.wait_ge(a_prep, t.n + 1)
                    scores_a(t, 0)
                    pe.wait_ge(a_vper, t.n + 1)
                    values_a(t, 0)
                    scores_a(t, 1)
                if q2.live():
                    pe.wait_ge(a_done[6], q2.n + 1)
                    wait(pe, a_done[7], q2.n * 3)
                    te.transpose(bank[7][:, 0:128], o_n[:, q2.odd, :, :].rearrange("p h o -> p (h o)"),
                                 id_s[:, 0, :]).then_inc(a_ready[7], 1)
                if t.live():
                    scores_a(t, 2)
                    values_a(t, 1)
                if q2.live():
                    pe.wait_ge(a_done[7], q2.n * 3 + 1)
                    te.matmul(bank[7][:, 128:256], ot[:, q2.odd, 0:128], w0_s[:, 3, :],
                              start=True, stop=True).then_inc(a_ready[7], 1)
                if q1.live():
                    pe.wait_ge(a_exp, q1.n * 3 + 3)
                    probs(q1, 0, 3, a_ready[3], a_done[3], q1.n * 2)
                    probs(q1, 1, 4, a_ready[4], a_done[4], q1.n)
                if t.live():
                    values_a(t, 2)
                if q1.live():
                    probs(q1, 2, 3, a_ready[3], a_done[3], q1.n * 2 + 1)
                    pe.wait_ge(a_done[5], q1.n * 3 + 3)
                    wait(pe, a_done[6], q1.n)
                    for c, (sem_c, n) in enumerate(((a_done[3], q1.n * 2 + 1), (a_done[4], q1.n + 1),
                                                    (a_done[3], q1.n * 2 + 2))):
                        pe.wait_ge(sem_c, n)
                        for j in range(*CHUNKS[c]):
                            m = rows_of(j)
                            last = te.matmul(bank[6][:, 0:H * OW], pt[0:m, q1.odd, j, :], vbd[0:m, q1.odd, j, :],
                                             start=(j == 0), stop=(j == KC - 1))
                    last.then_inc(a_ready[6], 1)
                if q2.live():
                    pe.wait_ge(a_xh, q2.n + 1)
                    te.transpose(bank[7][:, 256:384], xh[:, q2.odd, :], id_s[:, 0, :]).then_inc(a_ready[7], 1)

            steps(pe, 2, step_a)
            pe.wait_ge(a_done[7], B * 3)
            pe.wait_ge(first_done[G_WG % 8], G_WG // 8 + 1)
            loaded(pe, "wo0")

            def experts(t, e0, e1):
                for e in range(e0, e1):
                    wait(pe, b_u, t.n * E0 + e - 3)
                    mm3(bank[e % 4][:, :], lhs_hi[:, t.odd, :], lhs_lo[:, t.odd, :], w1_hi[:, e, :],
                        w1_lo[:, e, :]).then_inc(b_h, 1)

            def step_b(t):
                q2, q3 = t.back(2), t.back(3)
                if t.live():
                    pe.wait_ge(b_prep, t.n + 1)
                    wait(pe, b_lg_done, t.n)
                    te.matmul(bank[4][:, 0:E0], lhs_hi[:, t.odd, :].bitcast(f32), wgt[:, :], start=True, stop=False)
                    te.matmul(bank[4][:, 0:E0], lhs_lo[:, t.odd, :].bitcast(f32), wgt[:, :], start=False,
                              stop=True).then_inc(b_lg, 1)
                    experts(t, 0, 2)
                if q2.live():
                    pe.wait_ge(b_sum, (q2.n + 1) * (E0 - EP))
                    wait(pe, b_gt_done, q2.n)
                    for c in range(2):
                        last = te.transpose(bank[5][:, c * 128:(c + 1) * 128],
                                            gb[:, q2.odd, c * 128:(c + 1) * 128], id_s[:, 0, :])
                    last.then_inc(b_gt, 1)
                if t.live():
                    experts(t, 2, 4)
                if q2.live():
                    pe.wait_ge(b_gt_done, q2.n + 1)
                    wait(pe, b_y_done, q2.n)
                    te.matmul(bank[6][:, 0:D], ot[:, q2.odd, 0:128], wo0_s[:, 0, :], start=True, stop=False)
                    te.matmul(bank[6][:, 0:D], ot[:, q2.odd, 128:256], wo0_s[:, 1, :], start=False,
                              stop=True).then_inc(b_y, 1)
                if t.live():
                    experts(t, 4, 7)
                if q3.live():
                    pe.wait_ge(b_xh, q3.n + 1)
                    wait(pe, b_xt_done, q3.n)
                    te.transpose(bank[7][:, 0:128], xh[:, q3.odd, :], id_s[:, 0, :]).then_inc(b_xt, 1)
                if t.live():
                    experts(t, 7, E0)

            steps(pe, 3, step_b)

            pe.wait_ge(b_u, B * E0)
            pe.wait_ge(b_xt_done, B)
            pe.wait_ge(c_bias0, 1)

            def step_c(t):
                q2, q3 = t.back(2), t.back(3)
                if t.live():
                    pe.wait_ge(c_prep, t.n + 1)
                    for g, (h0, h1) in enumerate(HEADS):
                        wait(pe, c_sub, (t.n - 1) * 3 + g + 1)
                        te.matmul(bank[g][:, 0:(h1 - h0) * K], lhs[:, t.odd, :],
                                  b_all[:, bass.ds(t.n, 1), h0 * K:h1 * K].rearrange("p o k -> p (o k)"),
                                  start=True, stop=True).then_inc(c_scores, 1)
                if q2.live():
                    pe.wait_ge(c_norm, q2.n + 1)
                    for c in range(len(CHUNKS)):
                        probs(q2, c, PT_BANKS[c], c_pt[c], c_pt_done[c], q2.n)
                    pe.wait_ge(c_vw[q2.odd], q2.pairs(32) + 32)
                    wait(pe, c_y_done, q2.n)
                    te.matmul(bank[5][:, 0:D], one[0:1, :], rows_s[0:1, 2, :], start=True, stop=False)
                    for c in range(len(CHUNKS)):
                        pe.wait_ge(c_pt_done[c], q2.n + 1)
                        for j in range(*CHUNKS[c]):
                            m = rows_of(j)
                            last = te.matmul(bank[5][:, 0:D], pt[0:m, q2.odd, j, :], vw[0:m, q2.odd, j, :],
                                             start=False, stop=(j == KC - 1))
                    last.then_inc(c_y, 1)
                if q3.live():
                    pe.wait_ge(c_xh, q3.n + 1)
                    wait(pe, c_xt_done, q3.n)
                    te.transpose(bank[6][:, 0:128], xh[:, q3.odd, :], id_s[:, 0, :]).then_inc(c_xt, 1)

            steps(pe, 3, step_c)

            pe.wait_ge(wide_done, 1)
            pe.wait_ge(wide_act, 2)
            pe.wait_ge(c_xt_done, B)
            loaded(pe, "down")

            def wide(t, dst, at, n):
                return mm3(dst, lhs_hi[:, t.odd, :], lhs_lo[:, t.odd, :], wide_hi[:, at:at + n], wide_lo[:, at:at + n])

            def step_d(t):
                q = t.back(1)

                def inner(c, b, ready, done, n):
                    c0, c1 = ICHUNKS[c]
                    wait(pe, done, n)
                    for j in range(c0, c1):
                        last = te.transpose(bank[b][:, (j - c0) * 128:(j - c0 + 1) * 128],
                                            inter[:, q.odd, j * 128:(j + 1) * 128], id_s[:, 0, :])
                    last.then_inc(ready, 1)

                def gate_up(h, up):
                    if not up:
                        wait(pe, d_z, (t.n - 1) * 2 + h + 1)
                    last = wide(t, bank[2 * h + up][:, :], up * EI + h * 512, 512)
                    if up:
                        last.then_inc(d_gu, 1)

                if t.live():
                    pe.wait_ge(d_prep, t.n + 1)
                    wait(pe, d_lg_done, t.n)
                    wait(pe, d_sh_done, t.n)
                    wide(t, bank[4][:, 0:2 * FS + E1], 2 * EI, 2 * FS + E1).then_inc(d_sh, 1)
                if q.live():
                    pe.wait_ge(d_mul, q.n * 2 + 1)
                    inner(0, 5, d_it5, d_it5_done, q.n * 2)
                if t.live():
                    gate_up(0, 0)
                    gate_up(0, 1)
                    gate_up(1, 0)
                if q.live():
                    pe.wait_ge(d_mul, q.n * 2 + 2)
                    pe.wait_ge(d_sh_done, q.n + 1)
                    inner(1, 6, d_it6, d_it6_done, q.n)
                    inner(2, 5, d_it5, d_it5_done, q.n * 2 + 1)
                if t.live():
                    gate_up(1, 1)
                if q.live():
                    pe.wait_ge(d_it5_done, q.n * 2 + 2)
                    pe.wait_ge(d_it6_done, q.n + 1)
                    wait(pe, d_y_done, q.n)
                    for j in range(IC):
                        last = te.matmul(bank[7][:, 0:D], it[:, q.odd, j, :], down_s[:, j, :],
                                         start=(j == 0), stop=(j == IC - 1))
                    last.then_inc(d_y, 1)

            steps(pe, 1, step_d)


def kernel(x, ctx_1024, mask_Bx1xSxS2_bk1, L0_xattn_Wq, L0_xattn_bq, L0_xattn_Wk, L0_xattn_bk, L0_xattn_Wv,
           L0_xattn_bv, L0_xattn_Wo, L0_xattn_bo, L0_ffn_Wg, L0_ffn_W1, L0_ffn_b1, L0_ffn_Wo, L0_ffn_bo,
           L1_xattn_ln_gamma, L1_xattn_ln_beta, L1_xattn_w_q, L1_xattn_w_kv, L1_xattn_w_out, L1_xattn_b_out,
           L1_xattn_gate, L1_ffn_router_w, L1_ffn_gate_w, L1_ffn_up_w, L1_ffn_down_w, L1_ffn_shared_gate_w,
           L1_ffn_shared_up_w, L1_ffn_shared_down_w):
    import concourse.bacc as bacc
    import numpy as np
    from concourse.bass_utils import run_bass_kernel_spmd

    inner = H * 64
    pairs = lambda w: w.reshape(8, 128, D).transpose(1, 0, 2)
    eye = np.eye(128, dtype=np.float32)
    less_last = eye.copy()
    less_last[127, :] -= 1.0
    row_head = np.arange(KC * 128) // K
    arrays = {
        "x": x.transpose(1, 0, 2),
        "ctx_t": ctx_1024.reshape(NK, D).T,
        "mask": mask_Bx1xSxS2_bk1[:, 0].transpose(1, 0, 2),
        "w0": np.stack([L0_xattn_Wq, L0_xattn_Wk, L0_xattn_Wv, L0_xattn_Wo], axis=1),
        "cols": np.stack([L0_xattn_bq, L0_xattn_bk, L0_xattn_bv, L1_xattn_ln_gamma, L1_xattn_ln_beta], axis=1),
        "rows": np.stack([L0_xattn_bo, L0_ffn_bo, L1_xattn_b_out]),
        "w1": L0_ffn_W1.reshape(32, 128, D).transpose(1, 0, 2),
        "b1": L0_ffn_b1.reshape(32, 128).T,
        "wg": L0_ffn_Wg,
        "wo0": L0_ffn_Wo.T.reshape(2, 128, D).transpose(1, 0, 2),
        "wq": L1_xattn_w_q,
        "wk": pairs(L1_xattn_w_kv[:, :inner].T),
        "wv": pairs(L1_xattn_w_kv[:, inner:].T),
        "wout": pairs(L1_xattn_w_out),
        "gate": L1_xattn_gate.reshape(1, 1),
        "gu": np.concatenate([L1_ffn_gate_w.transpose(1, 0, 2).reshape(D, EI),
                              L1_ffn_up_w.transpose(1, 0, 2).reshape(D, EI)], axis=1),
        "rsh": np.concatenate([L1_ffn_shared_gate_w, L1_ffn_shared_up_w, L1_ffn_router_w], axis=1),
        "down": np.concatenate([L1_ffn_down_w.reshape(EI, D), L1_ffn_shared_down_w]).reshape(IC, 128, D)
                .transpose(1, 0, 2),
        "ident": np.stack([eye, less_last], axis=1),
        "hmask": (np.arange(D)[:, None] // HD == np.arange(H)[None, :]).astype(np.float32),
        "vmask": row_head.reshape(KC, 128).T[:, :, None] == np.arange(D)[None, None, :] // HD,
    }
    nc = bacc.Bacc("TRN2", target_bir_lowering=False, num_devices=1)
    feeds, args = {}, {}
    for name, a in arrays.items():
        a = np.ascontiguousarray(a)
        feeds[name + "_in"] = a
        args[name] = nc.dram_tensor(name + "_in", a.shape, mybir.dt.from_np(a.dtype), kind="ExternalInput").ap()
    args["out"] = nc.dram_tensor("out_0", (B, S, D), mybir.dt.float32, kind="ExternalOutput").ap()
    build(nc, **args)
    return run_bass_kernel_spmd(nc, [feeds], core_ids=[0]).results[0]["out_0"]
```

```python
from contextlib import ExitStack

import concourse.bass as bass
from concourse import mybir

B, S, D, K, H = 8, 128, 128, 77, 16
HK = H * K
KC = (HK + 127) // 128
KLAST = HK - 128 * (KC - 1)
HD = D // H
KEYS = 128 // H
OW = HD + 1
NK = B * K
NKH = NK // 2
E0, F0 = 8, 256
EP = 4
E1, F1, FS = 16, 64, 128
EI = E1 * F1
IC = (EI + FS) // 128
HEADS = [(0, 5), (5, 10), (10, 16)]
CHUNKS = [(0, 4), (4, 8), (8, 10)]
PT_BANKS_A, PT_BANKS = (3, 4, 3), (3, 4, 7)
START_A, START_B, START_C, START_D = 0, B + .5, 2 * B + 1.1, 3 * B + 2.8
ICHUNKS = [(0, 4), (4, 8), (8, 9)]
WIDE = 2 * EI + 2 * FS + E1
WPIECE = WIDE // B
EPS, EPS_TOP = 1e-5, 1e-9
MASKED = -1e15
BIG = 3.0e38
RC = (NK + 127) // 128


def context_rows(c):
    return min(128, NK - 128 * c)


def segments(c):
    out, row = [], 0
    while row < context_rows(c):
        tile, key = divmod(128 * c + row, K)
        n = min(K - key, context_rows(c) - row)
        out.append((tile, key, row, n))
        row += n
    return out


def rows_of(c):
    return 128 if c < KC - 1 else KLAST


class Tile:

    def __init__(self, n, odd):
        self.n, self.odd = n, odd

    def back(self, k):
        return Tile(self.n - k, (self.odd + k) % 2)

    def pairs(self, per):
        return (self.n - self.odd) * (per // 2)

    def live(self):
        return not isinstance(self.n, int) or 0 <= self.n < B


def steps(eng, lag, step):
    first = max(2, lag + lag % 2)
    for n in range(first):
        step(Tile(n, n % 2))
    with eng.Fori(0, (B - first) // 2) as i:
        for odd in range(2):
            step(Tile(i * 2 + (first + odd), odd))
    for n in range(B, B + lag):
        step(Tile(n, n % 2))


class Phase:

    def __init__(self, start, ahead, lag, step, before=None):
        self.start, self.ahead, self.lag, self.step, self.before = start, ahead, lag, step, before
        self.first = max(2, lag + lag % 2)

    def slot(self, n):
        return self.start + n - self.ahead

    def part(self, numbers):
        for n in numbers:
            for at in self.step(Tile(n, n % 2)):
                yield self.slot(n) + at

    def loop(self, eng):
        with eng.Fori(0, (B - self.first) // 2) as i:
            for odd in range(2):
                for _ in self.step(Tile(i * 2 + (self.first + odd), odd)):
                    pass


def beside(tail, head):
    a, b = next(tail, None), next(head, None)
    while a is not None or b is not None:
        if b is None or (a is not None and a <= b):
            a = next(tail, None)
        else:
            b = next(head, None)


def joined(eng, phases):
    tail, end = iter(()), 0
    for phase in phases:
        while phase.slot(phase.first) < end:
            phase.first += 2
        if phase.before:
            phase.before()
        beside(tail, phase.part(range(phase.first)))
        phase.loop(eng)
        tail, end = phase.part(range(B, B + phase.lag)), phase.slot(B + phase.lag)
    beside(tail, iter(()))


def wait(eng, sem, value):
    if not isinstance(value, int) or value > 0:
        eng.wait_ge(sem, value)


class Chain:

    def __init__(self, eng, sem, per):
        self.eng, self.sem, self.per = eng, sem, per

    def made(self, ins):
        ins.then_inc(self.sem, 1)

    def need(self, t, k):
        self.eng.wait_ge(self.sem, t.n * self.per + k)


def build(nc, x, ctx_t, mask, w0, bv, cols, rows, w1, b1, wg, wo0, wq, wk, wv, wout, gate, gu, rsh, down,
          ident, hmask, vmask, out):
    f32, f32r, bf16, u8 = mybir.dt.float32, mybir.dt.float32r, mybir.dt.bfloat16, mybir.dt.uint8
    ALU, ACT, AX = mybir.AluOpType, mybir.ActivationFunctionType, mybir.AxisListType
    vw_dram = nc.dram_tensor("vw_scratch", [B, HK, D], f32, kind="Internal").ap()
    v_dram = nc.dram_tensor("v_scratch", [B, K, D], f32, kind="Internal").ap()

    with ExitStack() as stack:
        def sb(name, shape, dt=f32, on=stack):
            return on.enter_context(nc.sbuf_tensor(name, shape, dt))

        def sem(name):
            return stack.enter_context(nc.semaphore(name))

        bank = [stack.enter_context(nc.psum_tensor(f"bank{i}", [128, 512], f32)) for i in range(8)]

        xr = sb("xr", [128, B, D])
        rows_s = sb("rows_s", [128, 3, D])
        w0_s = sb("w0_s", [128, 4, D])
        wo0_s = sb("wo0_s", [128, 2, D])
        id_s = sb("id_s", [128, 2, 128])
        idb = sb("idb", [128, 128], bf16)
        hmask_s = sb("hmask_s", [128, H])
        vmask_s = sb("vmask_s", [128, D], u8)
        bv_s = sb("bv_s", [1, D])
        maskneg = sb("maskneg", [128, B, K], bf16)
        k_t = sb("k_t", [128, NK])
        v_rows = sb("v_rows", [128, RC, D])
        q_t = sb("q_t", [128, B * S])
        xn_t = sb("xn_t", [128, B * S])
        wgt = sb("wgt", [128, E0])
        tanh_g = sb("tanh_g", [128, 1])
        b_all = sb("b_all", [128, B, HK])
        w1_hi, w1_lo = sb("w1_hi", [128, E0, 512], f32r), sb("w1_lo", [128, E0, 512], f32r)
        lhs = sb("lhs", [128, 2, 128])
        lhs_hi, lhs_lo = sb("lhs_hi", [128, 2, 128], f32r), sb("lhs_lo", [128, 2, 128], f32r)
        mx, rs = sb("mx", [128, 2, H]), sb("rs", [128, 2, H])
        rinv = sb("rinv", [128, 2, H])
        o_n = sb("o_n", [128, 2, H, HD])
        ot = sb("ot", [128, 2, 256])
        xh = sb("xh", [128, 2, D])
        st, ag = sb("st", [128, 2, 6]), sb("ag", [128, 2, 2])
        var, scale = sb("var", [128, 2]), sb("scale", [128, 2])
        ag8, var8, scale8 = sb("ag8", [128, B, 2]), sb("var8", [128, B]), sb("scale8", [128, B])
        one = sb("one", [1, 128])
        root = sb("root", [128, B])
        lg, lr = sb("lg", [128, 24]), sb("lr", [128, 24])
        top, mark = sb("top", [128, 8]), sb("mark", [128, 8])
        ee, es, sel = sb("ee", [128, 2, E1]), sb("es", [128, E1]), sb("sel", [128, E1])
        neg, ssum, s2 = sb("neg", [128, 2]), sb("ssum", [128, 2]), sb("s2", [128, 4])
        comb, csum = sb("comb", [128, 2, E1]), sb("csum", [128, 2])
        yb = sb("yb", [128, 2, D])

        with ExitStack() as early:
            ctx_s = sb("ctx_s", [128, NK], on=early)
            mask_s = sb("mask_s", [128, B, K], u8, on=early)
            cols_s = sb("cols_s", [128, 4], on=early)
            w127 = sb("w127", [E0, 1], on=early)
            wg_s = sb("wg_s", [E0, D], on=early)
            wq_s = sb("wq_s", [128, H * 64], on=early)
            wk_s = sb("wk_s", [128, 8, D], on=early)
            wv_s = sb("wv_s", [128, 8, D], on=early)
            wout_s = sb("wout_s", [128, 8, D], on=early)
            gate_s = sb("gate_s", [128, 1], on=early)
            tt = sb("tt", [128, D], on=early)
            ctx_hi, ctx_lo = sb("ctx_hi", [128, NK], f32r, early), sb("ctx_lo", [128, NK], f32r, early)
            m_hi, m_lo = sb("m_hi", [128, H * D], f32r, early), sb("m_lo", [128, H * D], f32r, early)
        p = sb("p", [128, 2, HK])
        pt = sb("pt", [128, 2, KC, 128])
        vw = sb("vw", [128, 2, KC, D])
        wide_s = sb("wide_s", [128, WIDE])
        down_s = sb("down_s", [128, IC, D])
        with ExitStack() as rows_w1:
            w1_s = sb("w1_s", [128, 32, D], on=rows_w1)
            w1f = sb("w1f", [128, 4, D], on=rows_w1)
            b1_s = sb("b1_s", [128, 32], on=rows_w1)
        wide_hi = sb("wide_hi", [128, WIDE], f32r)
        wide_lo = sb("wide_lo", [128, WIDE], f32r)
        with ExitStack() as first:
            pair_q = sb("pair_q", [128, 8, 2, D], on=first)
            pair_o = sb("pair_o", [128, 8, 2, D], on=first)
            xh0 = sb("xh0", [128, B, D], on=first)
            a_hi, a_lo = sb("a_hi", [128, H * D], f32r, first), sb("a_lo", [128, H * D], f32r, first)
        with ExitStack() as phase_a:
            vws = sb("vws", [128, 2, 4, 512], on=phase_a)
            vbd = sb("vbd", [128, 2, KC, H * OW], on=phase_a)
            kbd = sb("kbd", [128, 2, HK], on=phase_a)
        with ExitStack() as phase_b:
            th = sb("th", [128, 4, F0], on=phase_b)
            ub = sb("ub", [128, E0, F0], on=phase_b)
            gb = sb("gb", [128, 2, F0], on=phase_b)
            part = sb("part", [128, EP, F0], on=phase_b)
        tg = sb("tg", [128, 3, 512])
        z1 = sb("z1", [128, 3, 512])
        z2 = sb("z2", [128, 2, 512])
        inter = sb("inter", [128, 2, EI + FS])
        it = pt

        names = ("ctx", "w0", "cols", "x", "ident", "wq", "wout", "gate", "wk", "wv", "wg", "rows", "mask",
                 "hmask", "w1", "b1", "vmask", "wo0", "gu", "rsh", "down", "bv")
        load = {n: sem("load_" + n) for n in names}

        def loaded(eng, *which):
            for n in which:
                eng.wait_ge(load[n], 16)

        first_ready = [sem(f"first_ready{i}") for i in range(8)]
        first_done = [sem(f"first_done{i}") for i in range(8)]
        hi_done = sem("hi_done")
        dve_first, pool_first = sem("dve_first"), sem("pool_first")
        tt_done, ctx_split, xh0_done, wg_done = sem("tt_done"), sem("ctx_split"), sem("xh0_done"), sem("wg_done")
        bd_zero, w1_done, consts_done, tanh_done = sem("bd_zero"), sem("w1_done"), sem("consts_done"), sem("tanh_done")
        outw_done, bias0_done = sem("outw_done"), sem("bias0_done")
        vw_act, vw_dve = sem("vw_act"), sem("vw_dve")
        vw_stored = [sem("vw_stored0"), sem("vw_stored1")]
        w1t_ready, w1t_hi, w1t_done = sem("w1t_ready"), sem("w1t_hi"), sem("w1t_done")
        one_done, ones_done = sem("one_done"), sem("ones_done")
        v_stored, a_values = sem("v_stored"), [sem("a_values0"), sem("a_values1")]
        a_pt, a_pt_done = sem("a_pt"), sem("a_pt_done")
        a_prep, a_masked = sem("a_prep"), sem("a_masked")
        a_sub, a_exp, a_scores = sem("a_sub"), sem("a_exp"), sem("a_scores")
        a_ready = {i: sem(f"a_ready{i}") for i in (6, 7)}
        a_done = {i: sem(f"a_done{i}") for i in (6, 7)}
        a_xh = sem("a_xh")
        a_chain, a_chain_y = sem("a_chain"), sem("a_chain_y")
        b_prep_hi, b_prep = sem("b_prep_hi"), sem("b_prep")
        b_lg, b_lg_done, b_h, b_tanh, b_u, b_acc = (
            sem("b_lg"), sem("b_lg_done"), sem("b_h"), sem("b_tanh"), sem("b_u"), sem("b_acc"))
        b_neg, b_exp, b_comb = sem("b_neg"), sem("b_exp"), sem("b_comb")
        b_part, b_sum = sem("b_part"), sem("b_sum")
        var8_done, scale8_done = sem("var8_done"), sem("scale8_done")
        a_var, a_scale, b_var, b_scale, c_var, c_scale = (
            sem("a_var"), sem("a_scale"), sem("b_var"), sem("b_scale"), sem("c_var"), sem("c_scale"))
        b_gt, b_gt_done, b_y, b_y_done, b_xh, b_xt, b_xt_done = (
            sem("b_gt"), sem("b_gt_done"), sem("b_y"), sem("b_y_done"), sem("b_xh"), sem("b_xt"), sem("b_xt_done"))
        b_chain, b_chain_y = sem("b_chain"), sem("b_chain_y")
        wide_act, wide_done = sem("wide_act"), sem("wide_done")
        c_prep, c_scores, c_sub, c_exp, c_rs, c_norm = (
            sem("c_prep"), sem("c_scores"), sem("c_sub"), sem("c_exp"), sem("c_rs"), sem("c_norm"))
        c_vw = [sem("c_vw0"), sem("c_vw1")]
        c_bias0 = sem("c_bias0")
        c_pt, c_pt_done = sem("c_pt"), sem("c_pt_done")
        c_y, c_y_done, c_xh, c_xt, c_xt_done = sem("c_y"), sem("c_y_done"), sem("c_xh"), sem("c_xt"), sem("c_xt_done")
        c_chain, c_chain_y = sem("c_chain"), sem("c_chain_y")
        d_prep_hi, d_prep = sem("d_prep_hi"), sem("d_prep")
        d_sh, d_gu, d_tanh, d_tanh_sh, d_z, d_sh_done, d_mul = (
            sem("d_sh"), sem("d_gu"), sem("d_tanh"), sem("d_tanh_sh"), sem("d_z"), sem("d_sh_done"), sem("d_mul"))
        d_neg, d_exp, d_comb = sem("d_neg"), sem("d_exp"), sem("d_comb")
        d_it5, d_it6, d_it5_done, d_it6_done = sem("d_it5"), sem("d_it6"), sem("d_it5_done"), sem("d_it6_done")
        scores_max, d_lg_done, d_z1 = sem("scores_max"), sem("d_lg_done"), sem("d_z1")
        d_y, d_y_done, d_out, d_chain = sem("d_y"), sem("d_y_done"), [sem("d_out0"), sem("d_out1")], sem("d_chain")

        G_K, G_V, G_WQ, G_A, G_M, G_XT, G_Q, G_WG, G_B = 0, 2, 4, 6, 10, 14, 16, 18, 19
        N_B = 2 * H
        G_VW = G_B + N_B

        def stored_by(c):
            return 16 * sum(len(segments(i)) for i in range(c % 2, c + 1, 2))

        def columns(tensor, t, width):
            return tensor[:, bass.ds(t.n * width, width)]

        def tile_of(tensor, t):
            if isinstance(t.n, int):
                return tensor[:, t.n, :]
            return tensor[:, bass.ds(t.n, 1), :].rearrange("p o d -> p (o d)")

        block = stack.enter_context(nc.Block())

        @block.sync
        def _(sp):
            srcs = {"ctx": (ctx_s[:, :], ctx_t), "w0": (w0_s[:, :, :], w0), "wq": (wq_s[:, :], wq),
                    "wk": (wk_s[:, :, :], wk),
                    "gate": (gate_s[:, :], gate.broadcast_to([128, 1])), "wout": (wout_s[:, :, :], wout),
                    "wv": (wv_s[:, :, :], wv),
                    "wg": (wg_s[:, :], wg), "w1": (w1_s[:, :, :], w1), "b1": (b1_s[:, :], b1)}
            for n, (dst, src) in srcs.items():
                sp.dma_start(dst, src).then_inc(load[n], 16)

            whole = RC - 1
            for i in range(2):
                sp.wait_ge(first_done[(G_V + i) % 8], (G_V + i) // 8 + 1)
            v_flat = v_dram.rearrange("b k d -> (b k) d")
            sp.dma_start(v_flat[0:128 * whole].rearrange("(c p) d -> p c d", p=128),
                         v_rows[:, 0:whole, :]).then_inc(v_stored, 16)
            sp.dma_start(v_flat[128 * whole:NK], v_rows[0:context_rows(whole), whole, :]).then_inc(v_stored, 16)

            for c in range(RC):
                sp.wait_ge(vw_act, 2 * c + 2)
                sp.wait_ge(vw_dve, 2 * c + 2)
                for tile, key, row, n in segments(c):
                    dst = vw_dram[tile].rearrange("(h k) d -> k h d", h=H)[key:key + n]
                    sp.dma_start(dst, vws[row:row + n, c % 2, :, :].rearrange("k a (h d) -> k (a h) d", h=4)
                                 ).then_inc(vw_stored[c % 2], 16)

            def fetch_values(t):
                wait(sp, a_masked, (t.n - 1) * len(CHUNKS))
                for k in range(KEYS):
                    n = len(range(k, K, KEYS))
                    src = v_dram[bass.ds(t.n, 1), k:k + (n - 1) * KEYS + 1:KEYS, :]
                    sp.dma_start(vw[k * H:(k + 1) * H, t.odd, 0:n, :],
                                 src.broadcast_to([H, n, D])).then_inc(a_values[t.odd], 16)

            sp.wait_ge(v_stored, 32)
            steps(sp, 0, fetch_values)
            for c in (RC - 2, RC - 1):
                sp.wait_ge(vw_stored[c % 2], stored_by(c))
            sp.dma_start(wide_s[:, 0:2 * EI], gu).then_inc(load["gu"], 16)
            sp.dma_start(wide_s[:, 2 * EI:], rsh).then_inc(load["rsh"], 16)
            sp.dma_start(down_s[:, :, :], down).then_inc(load["down"], 16)

            def fetch(t):
                if isinstance(t.n, int):
                    sp.wait_ge(a_masked, B * len(CHUNKS))
                wait(sp, c_y, t.n - 1)
                src = vw_dram[bass.ds(t.n, 1), :, :]
                sp.dma_start(vw[:, t.odd, 0:KC - 1, :],
                             src[:, 0:128 * (KC - 1), :].rearrange("o (c p) d -> p (o c) d", p=128)
                             ).then_inc(c_vw[t.odd], 16)
                sp.dma_start(vw[0:KLAST, t.odd, KC - 1, :],
                             src[:, 128 * (KC - 1):HK, :].rearrange("o p d -> p (o d)")
                             ).then_inc(c_vw[t.odd], 16)

            steps(sp, 0, fetch)

            def result(t):
                sp.wait_ge(d_y_done, t.n + 1)
                sp.dma_start(out[bass.ds(t.n, 1), :, :].rearrange("o s d -> s (o d)"),
                             yb[:, t.odd, :]).then_inc(d_out[t.odd], 16)

            steps(sp, 0, result)
            for s in d_out:
                sp.wait_ge(s, 16 * (B // 2))

        @block.gpsimd
        def _(pool):
            ps = nc.gpsimd
            own = [0]

            def link(ins):
                own[0] += 1
                ins.then_inc(pool_first, 1)
                pool.wait_ge(pool_first, own[0])

            for buf in (pair_q, pair_o):
                ps.memset(buf[:, :, :, :], 0.0).then_inc(bd_zero, 1)
            ps.memset(one[0:1, :], 1.0).then_inc(one_done, 1)
            link(ps.memset(root[:, :], -0.5))

            def inverse_root(t, var_sem, scale_sem):
                pool.wait_ge(var_sem, t.n + 1)
                u = slice(t.odd, t.odd + 1)
                ps.tensor_tensor(scale[:, u], var[:, u], root[:, 0:1], ALU.pow).then_inc(scale_sem, 1)

            pool.wait_ge(var8_done, 1)
            ps.tensor_tensor(scale8[:, :], var8[:, :], root[:, :], ALU.pow).then_inc(scale8_done, 1)
            loaded(pool, "wg")
            link(ps.tensor_copy(w127[:, 0:1], wg_s[:, D - 1:D]))
            link(ps.tensor_tensor(wg_s[:, 0:D - 1], wg_s[:, 0:D - 1],
                                  w127[:, 0:1].broadcast_to([E0, D - 1]), ALU.subtract))
            ps.memset(wg_s[:, D - 1:D], 0.0).then_inc(wg_done, 1)
            loaded(pool, "rows")
            pool.wait_ge(xh0_done, B)
            ps.tensor_tensor(xr[:, :, :], xr[:, :, :], rows_s[:, 0:1, :].broadcast_to([128, B, D]),
                             ALU.add).then_inc(bias0_done, 1)

            g = G_VW - 1
            pool.wait_ge(first_ready[g % 8], g // 8 + 1)
            pool.wait_ge(first_done[(G_Q + 1) % 8], (G_Q + 1) // 8 + 1)
            pool.wait_ge(first_done[G_Q % 8], G_Q // 8 + 1)
            loaded(pool, "hmask", "w1", "b1", "vmask")
            for u in range(2):
                ps.tensor_copy(vbd[:, u, :, :].rearrange("p c (h o) -> p c h o", o=OW)[:, :, :, HD],
                               vmask_s[:, :].rearrange("p (h o) -> p h o", o=HD)[:, :, 0].unsqueeze(1)
                               .broadcast_to([128, KC, H])).then_inc(ones_done, 1)

            def step_a(ahead):
                yield 0
                if ahead.live():
                    wait(pool, a_scores, (ahead.n - 1) * 3)
                    ps.tensor_copy(lhs[:, ahead.odd, :], columns(q_t, ahead, S))
                    ps.tensor_tensor(kbd[:, ahead.odd, :].rearrange("p (h k) -> p h k", h=H),
                                     columns(k_t, ahead, K).unsqueeze(1).broadcast_to([128, H, K]),
                                     hmask_s[:, :].unsqueeze(2).broadcast_to([128, H, K]),
                                     ALU.mult).then_inc(a_prep, 1)
                yield 0.85
                if ahead.back(3).live():
                    inverse_root(ahead.back(3), a_var, a_scale)
                yield .9
                if ahead.live():
                    wait(pool, w1t_ready, ahead.n)
                    rows4 = w1_s[:, bass.ds(ahead.n * 4, 4), :]
                    ps.tensor_tensor(w1f[:, :, 0:D - 1], rows4[:, :, 0:D - 1],
                                     rows4[:, :, D - 1:D].broadcast_to([128, 4, D - 1]), ALU.subtract)
                    ps.tensor_copy(w1f[:, :, D - 1], b1_s[:, bass.ds(ahead.n * 4, 4)]).then_inc(w1_done, 1)

            def step_b(t):
                yield .4
                if t.back(3).live():
                    inverse_root(t.back(3), b_var, b_scale)
                yield .7
                if t.live():
                    pool.wait_ge(b_u, t.n * E0 + EP)
                    pool.wait_ge(b_comb, t.n + 1)
                    ps.tensor_tensor(part[:, :, :], ub[:, 0:EP, :],
                                     comb[:, t.odd, 0:EP].unsqueeze(2).broadcast_to([128, EP, F0]),
                                     ALU.mult).then_inc(b_part, 1)
                    pool.wait_ge(b_part, t.n * 2 + 1)
                    ps.tensor_tensor(part[:, 0:2, :], part[:, 0:2, :], part[:, 2:4, :], ALU.add).then_inc(b_part, 1)
                    pool.wait_ge(b_part, t.n * 2 + 2)
                    wait(pool, b_gt, t.n - 1)
                    ps.tensor_tensor(gb[:, t.odd, :], part[:, 0, :], part[:, 1, :], ALU.add).then_inc(b_acc, 1)

            def before_b():
                for c in (RC - 2, RC - 1):
                    pool.wait_ge(vw_stored[c % 2], stored_by(c))
                pool.wait_ge(tanh_done, 1)
                ps.tensor_scalar(rows_s[:, 2, :], rows_s[:, 2, :], tanh_g[:, 0:1], None, ALU.mult).then_inc(c_bias0, 1)

            def before_c():
                loaded(pool, "gu", "rsh")

            def step_c(ahead):
                yield 0.0
                if ahead.live():
                    pool.wait_ge(b_xt_done, ahead.n + 1)
                    wait(pool, c_scores, (ahead.n - 1) * 3)
                    ps.tensor_copy(lhs[:, ahead.odd, :], columns(xn_t, ahead, S)).then_inc(c_prep, 1)
                yield 0.3
                if ahead.back(2).live():
                    q = ahead.back(2)
                    pool.wait_ge(c_rs, q.n + 1)
                    pq = p[:, q.odd, :].rearrange("p (h k) -> p h k", h=H)
                    ps.tensor_tensor(pq, pq, rinv[:, q.odd, :].unsqueeze(2).broadcast_to([128, H, K]),
                                     ALU.mult).then_inc(c_norm, 1)
                yield 0.7
                if ahead.back(4).live():
                    inverse_root(ahead.back(4), c_var, c_scale)
                yield 0.95
                if ahead.live():
                    pool.wait_ge(wide_act, ahead.n + 1)
                    ps.tensor_tensor(columns(wide_lo, ahead, WPIECE), columns(wide_s, ahead, WPIECE),
                                     columns(wide_hi, ahead, WPIECE).bitcast(f32), ALU.subtract).then_inc(wide_done, 1)

            def weigh(t, half):
                pool.wait_ge(d_z, t.n * 2 + half + 1)
                pool.wait_ge(d_comb, t.n + 1)
                if half == 0:
                    wait(pool, d_it6, t.n - 1)
                    wait(pool, d_it5, (t.n - 1) * 2)
                ps.tensor_tensor(
                    inter[:, t.odd, half * 512:(half + 1) * 512].rearrange("p (e f) -> p e f", f=F1),
                    z2[:, half, :].rearrange("p (e f) -> p e f", f=F1),
                    comb[:, t.odd, half * 8:half * 8 + 8].unsqueeze(2).broadcast_to([128, 8, F1]),
                    ALU.mult).then_inc(d_mul, 1)

            def step_d(t):
                yield 0.3
                if t.back(1).live():
                    weigh(t.back(1), 1)
                yield 0.7
                if t.live():
                    weigh(t, 0)

            joined(pool, [Phase(START_A, 1, 3, step_a), Phase(START_B, 0, 3, step_b, before_b),
                          Phase(START_C, 1, 4, step_c, before_c), Phase(START_D, 0, 1, step_d)])

        @block.scalar
        def _(act):
            ac = nc.scalar
            srcs = {"cols": (cols_s[:, :], cols), "bv": (bv_s[:, :], bv), "ident": (id_s[:, :, :], ident), "x": (xr[:, :, :], x),
                    "rows": (rows_s[:, :, :], rows.unsqueeze(0).broadcast_to([128, 3, D])),
                    "mask": (mask_s[:, :, :], mask), "hmask": (hmask_s[:, :], hmask),
                    "vmask": (vmask_s[:, :], vmask), "wo0": (wo0_s[:, :, :], wo0)}
            for n, (dst, src) in srcs.items():
                act.dma_start(dst, src).then_inc(load[n], 16)

            def group(g):
                act.wait_ge(first_ready[g % 8], g // 8 + 1)
                return bank[g % 8]

            loaded(act, "ctx")
            ac.activation(ctx_hi[:, :], ctx_s[:, :], ACT.Copy).then_inc(ctx_split, 1)
            loaded(act, "cols")
            for i in range(2):
                g = G_K + i
                ac.activation(k_t[:, i * NKH:(i + 1) * NKH], group(g)[:, 0:NKH], ACT.Identity,
                              bias=cols_s[:, 1:2]).then_inc(first_done[g % 8], 1)
            for i in range(2):
                g = G_V + i
                c0, c1, n = (0, RC - 1, 128) if i == 0 else (RC - 1, RC, context_rows(RC - 1))
                ac.activation(v_rows[0:n, c0:c1, :],
                              group(g)[0:n, 0:(c1 - c0) * D].rearrange("p (c d) -> p c d", d=D),
                              ACT.Copy).then_inc(first_done[g % 8], 1)
            loaded(act, "ident")
            ac.activation(idb[:, :], id_s[:, 0, :], ACT.Copy).then_inc(consts_done, 1)
            def wq_group(i):
                g = G_WQ + i
                src = group(g)[:, :].rearrange("p (c d) -> p c d", c=4)
                for h in range(2):
                    half = slice(64 * h, 64 * h + 64)
                    last = ac.activation(pair_q[half, 4 * i:4 * i + 4, h, :], src[half, :, :], ACT.Copy)
                last.then_inc(first_done[g % 8], 1)

            act.wait_ge(bd_zero, 1)
            for i in range(2):
                wq_group(i)
            loaded(act, "gate", "wout")
            ac.activation(tanh_g[:, :], gate_s[:, :], ACT.Tanh).then_inc(tanh_done, 1)
            act.wait_ge(tanh_done, 1)
            act.wait_ge(bd_zero, 2)
            for h in range(2):
                half = slice(64 * h, 64 * h + 64)
                ac.activation(pair_o[half, :, h, :], wout_s[half, :, :], ACT.Copy,
                              scale=tanh_g[half, 0:1]).then_inc(outw_done, 1)

            def high(g0, hi, i):
                ac.activation(hi[:, i * 512:(i + 1) * 512], group(g0 + i)[:, :], ACT.Copy).then_inc(hi_done, 1)

            for i in range(4):
                high(G_A, a_hi, i)
            for i in range(4):
                high(G_M, m_hi, i)
            for i in range(2):
                g = G_XT + i
                ac.activation(xn_t[:, i * 512:(i + 1) * 512], group(g)[:, :], ACT.Copy).then_inc(first_done[g % 8], 1)
            for i in range(2):
                g = G_Q + i
                ac.activation(q_t[:, i * 512:(i + 1) * 512], group(g)[:, :], ACT.Identity,
                              bias=cols_s[:, 0:1]).then_inc(first_done[g % 8], 1)
            g = G_WG
            ac.activation(wgt[:, :], group(g)[:, 0:E0], ACT.Copy).then_inc(first_done[g % 8], 1)
            for i in range(0, N_B, 2):
                g = G_B + i
                ac.activation(b_all[:, 0:4, (i // 2) * K:(i // 2) * K + K],
                              group(g)[:, 0:NKH].rearrange("p (b k) -> p b k", k=K),
                              ACT.Copy).then_inc(first_done[g % 8], 1)

            def value_rows(c, i):
                g, n = G_VW + 4 * c + i, context_rows(c)
                if i < 2 and c >= 2:
                    act.wait_ge(vw_stored[c % 2], stored_by(c - 2))
                ac.activation(vws[0:n, c % 2, i, :], group(g)[0:n, :], ACT.Copy).then_inc(vw_act, 1)

            for c in range(RC):
                value_rows(c, 0)
                value_rows(c, 2)

            def copy_probs(q, c, src, used, ready, done):
                c0, c1 = CHUNKS[c]
                if c == 0:
                    wait(act, used, q.n - 1)
                act.wait_ge(ready, q.n * 3 + c + 1)
                src = src[:, 0:(c1 - c0) * 128].rearrange("p (c q) -> p c q", q=128)
                if c < 2:
                    ins = ac.activation(pt[:, q.odd, c0:c1, :], src, ACT.Copy)
                else:
                    ac.activation(pt[:, q.odd, c0:c0 + 1, :], src[:, 0:1, :], ACT.Copy)
                    ins = ac.activation(pt[0:KLAST, q.odd, c0 + 1, :], src[0:KLAST, 1, :], ACT.Copy)
                ins.then_inc(done, 1)

            def probs_a(q, c):
                copy_probs(q, c, bank[PT_BANKS_A[c]], a_ready[6], a_pt, a_pt_done)

            def exp_a(t, g):
                h0, h1 = HEADS[g]
                act.wait_ge(a_sub, t.n * 3 + g + 1)
                cut = p[:, t.odd, :].rearrange("p (k h) -> p k h", h=H)[:, :, h0:h1]
                ac.activation(cut, cut, ACT.Exp, scale=HD ** -0.5).then_inc(a_exp, 1)

            def step_a(t):
                q1, q2 = t.back(1), t.back(2)
                q3 = t.back(3)
                late = 0 if t.live() else .4
                yield .1 + late
                if q3.live():
                    act.wait_ge(a_ready[7], q3.n * 3 + 3)
                    ac.activation(columns(xn_t, q3, S), bank[7][:, 256:384], ACT.Copy).then_inc(a_done[7], 1)
                for c in range(2):
                    yield .15
                    if q1.live():
                        probs_a(q1, c)
                yield 0.2 + late
                if q2.live():
                    act.wait_ge(a_ready[7], q2.n * 3 + 1)
                    ac.activation(ot[:, q2.odd, 0:128], bank[7][:, 0:128], ACT.Copy).then_inc(a_done[7], 1)
                yield .3
                if q1.live():
                    probs_a(q1, 2)
                yield 0.4
                if t.live():
                    exp_a(t, 0)
                yield .5
                if t.live():
                    act.wait_ge(w1t_ready, t.n + 1)
                    ac.activation(w1_hi[:, bass.ds(t.n, 1), :].rearrange("p o f -> p (o f)"), bank[5][:, :],
                                  ACT.Copy).then_inc(w1t_hi, 1)
                yield 0.6
                if t.live():
                    exp_a(t, 1)
                yield 0.7
                if t.live():
                    exp_a(t, 2)

            def router_exp(t, n, neg_sem, exp_sem):
                act.wait_ge(neg_sem, t.n + 1)
                ac.activation(ee[:, t.odd, 0:n], lg[:, 0:n], ACT.Exp, bias=neg[:, t.odd:t.odd + 1],
                              accum_out=ssum[:, t.odd:t.odd + 1]).then_inc(exp_sem, 1)

            def halves(t, there, n, used, m, hi_sem):
                act.wait_ge(there, n)
                wait(act, used, m)
                ac.activation(lhs_hi[:, t.odd, :], columns(xn_t, t, S), ACT.Copy).then_inc(hi_sem, 1)

            def tanh_b(t, e):
                act.wait_ge(b_h, t.n * E0 + e + 1)
                ac.activation(th[:, e % 4, :], bank[e % 4][:, F0:2 * F0], ACT.Tanh, scale=0.5).then_inc(b_tanh, 1)

            def step_b(ahead):
                t, q1, q2, q3 = ahead.back(1), ahead.back(2), ahead.back(3), ahead.back(4)
                yield 0
                if q1.live():
                    tanh_b(q1, 6)
                    tanh_b(q1, 7)
                yield .15
                if t.live():
                    tanh_b(t, 0)
                yield .25
                if t.live():
                    tanh_b(t, 1)
                yield .25 if t.live() else 0
                if q2.live():
                    act.wait_ge(b_gt, q2.n + 1)
                    ac.activation(ot[:, q2.odd, :], bank[5][:, 0:256], ACT.Copy).then_inc(b_gt_done, 1)
                yield .35
                if t.live():
                    router_exp(t, E0, b_neg, b_exp)
                if ahead.live():
                    halves(ahead, a_done[7], ahead.n * 3 + 3, b_h, (ahead.n - 1) * E0, b_prep_hi)
                yield .45
                if t.live():
                    tanh_b(t, 2)
                yield .55
                if t.live():
                    tanh_b(t, 3)
                    ac.activation(columns(wide_hi, t, WPIECE), columns(wide_s, t, WPIECE), ACT.Copy).then_inc(wide_act, 1)
                yield .65
                if t.live():
                    tanh_b(t, 4)
                yield .8
                if t.live():
                    tanh_b(t, 5)
                if q3.live():
                    act.wait_ge(b_xt, q3.n + 1)
                    ac.activation(columns(xn_t, q3, S), bank[7][:, 0:128], ACT.Copy).then_inc(b_xt_done, 1)

            def before_b():
                for c in (RC - 2, RC - 1):
                    act.wait_ge(vw_stored[c % 2], stored_by(c))
                loaded(act, "gu", "rsh")

            def probs_c(q, c):
                copy_probs(q, c, bank[PT_BANKS[c]], c_y, c_pt, c_pt_done)

            def exp_c(t, g):
                h0, h1 = HEADS[g]
                act.wait_ge(c_sub, t.n * 3 + g + 1)
                cut = p[:, t.odd, h0 * K:h1 * K]
                ac.activation(cut, cut, ACT.Exp, scale=64 ** -0.5).then_inc(c_exp, 1)

            def step_c(t):
                q2, q3 = t.back(2), t.back(3)
                yield 0.3
                if q2.live():
                    probs_c(q2, 0)
                    probs_c(q2, 1)
                yield 0.5
                if t.live():
                    exp_c(t, 0)
                yield 0.55
                if q2.live():
                    probs_c(q2, 2)
                yield 0.6
                if t.live():
                    exp_c(t, 1)
                    exp_c(t, 2)
                yield 0.97
                if q3.live():
                    act.wait_ge(c_xt, q3.n + 1)
                    ac.activation(columns(xn_t, q3, S), bank[6][:, 0:128], ACT.Copy).then_inc(c_xt_done, 1)

            def tanh_d(t, h):
                act.wait_ge(d_gu, t.n * 2 + h + 1)
                ac.activation(tg[:, h, :], bank[2 * h][:, :], ACT.Tanh, scale=0.5).then_inc(d_tanh, 1)

            def step_d(ahead):
                t, q = ahead.back(1), ahead.back(2)
                yield 0
                if q.live():
                    tanh_d(q, 1)
                yield 0.2
                if t.live():
                    router_exp(t, E1, d_neg, d_exp)
                    ac.activation(tg[:, 2, 0:FS], bank[4][:, 0:FS], ACT.Tanh, scale=0.5).then_inc(d_tanh_sh, 1)
                    tanh_d(t, 0)
                yield .4
                if q.live():
                    act.wait_ge(d_it5, q.n * 2 + 1)
                    ac.activation(it[:, q.odd, 0:4, :], bank[5][:, :].rearrange("p (c q) -> p c q", q=128),
                                  ACT.Copy).then_inc(d_it5_done, 1)
                yield 0.5
                if ahead.live():
                    halves(ahead, c_xt_done, ahead.n + 1, d_gu, (ahead.n - 1) * 2, d_prep_hi)
                yield 0.6
                if q.live():
                    act.wait_ge(d_it6, q.n + 1)
                    ac.activation(it[:, q.odd, 4:8, :], bank[6][:, :].rearrange("p (c q) -> p c q", q=128),
                                  ACT.Copy).then_inc(d_it6_done, 1)
                    act.wait_ge(d_it5, q.n * 2 + 2)
                    ac.activation(it[:, q.odd, 8, :], bank[5][:, 0:128], ACT.Copy).then_inc(d_it5_done, 1)

            joined(act, [Phase(START_A, 0, 3, step_a), Phase(START_B, 1, 4, step_b, before_b),
                         Phase(START_C, 0, 3, step_c), Phase(START_D, 1, 2, step_d)])

        @block.vector
        def _(dve):
            ve = nc.vector
            own = [0]

            def link(ins):
                own[0] += 1
                ins.then_inc(dve_first, 1)
                dve.wait_ge(dve_first, own[0])

            def group(g):
                dve.wait_ge(first_ready[g % 8], g // 8 + 1)
                return bank[g % 8]

            def row_stats(chain, t):
                chain.made(ve.bn_stats(out=st[:, t.odd, :], in_=tile_of(xr, t)))

            def row_mean(chain, t):
                chain.made(ve.bn_aggr(out=ag[:, t.odd, :], in_=st[:, t.odd, :]))

            def row_var(chain, t, var_sem, twice=False):
                u = t.odd
                chain.need(t, 2)
                ve.tensor_scalar(var[:, u:u + 1], ag[:, u, 1:2], 1.0 + EPS if twice else 1.0,
                                 EPS * EPS if twice else EPS, ALU.mult, ALU.add).then_inc(var_sem, 1)

            def normed(row, t, scale_sem, xh_sem, last=None):
                u = t.odd
                dve.wait_ge(scale_sem, t.n + 1)
                n = D if last is None else D - 1
                if last is not None:
                    ve.memset(xh[:, u, D - 1:D], last)
                ve.tensor_scalar(xh[:, u, 0:n], row[:, 0:n], ag[:, u, 0:1], scale[:, u:u + 1],
                                 ALU.subtract, ALU.mult).then_inc(xh_sem, 1)

            loaded(dve, "cols", "ident")
            link(ve.tensor_scalar(tt[:, :], id_s[:, 1, :], cols_s[:, 2:3], None, ALU.mult))
            ve.tensor_copy(tt[:, D - 1:D], cols_s[:, 3:4]).then_inc(tt_done, 1)
            dve.wait_ge(ctx_split, 1)
            loaded(dve, "ctx")
            ve.tensor_tensor(ctx_lo[:, :], ctx_s[:, :], ctx_hi[:, :].bitcast(f32), ALU.subtract).then_inc(ctx_split, 1)
            loaded(dve, "x")
            for b in range(B):
                link(ve.bn_stats(out=st[:, b % 2, :], in_=xr[:, b, :]))
                link(ve.bn_aggr(out=ag8[:, b, :], in_=st[:, b % 2, :]))
            ve.tensor_scalar(var8[:, :], ag8[:, :, 1], EPS, None, ALU.add).then_inc(var8_done, 1)
            dve.wait_ge(scale8_done, 1)
            for b in range(B):
                ve.tensor_scalar(xh0[:, b, :], xr[:, b, :], ag8[:, b, 0:1], scale8[:, b:b + 1],
                                 ALU.subtract, ALU.mult).then_inc(xh0_done, 1)
            loaded(dve, "mask")
            ve.tensor_scalar(maskneg[:, :, :], mask_s[:, :, :], MASKED, None, ALU.mult).then_inc(consts_done, 1)
            link(ve.memset(mark[:, :], BIG))
            link(ve.memset(lg[:, :], BIG))
            n_hi = 0
            for g0, hi, lo in ((G_A, a_hi, a_lo), (G_M, m_hi, m_lo)):
                for i in range(4):
                    n_hi += 1
                    g, cut = g0 + i, slice(i * 512, (i + 1) * 512)
                    src = group(g)
                    dve.wait_ge(hi_done, n_hi)
                    ve.tensor_tensor(lo[:, cut], src[:, :], hi[:, cut].bitcast(f32),
                                     ALU.subtract).then_inc(first_done[g % 8], 1)
            for i in range(1, N_B, 2):
                g = G_B + i
                ve.tensor_copy(b_all[:, 4:8, (i // 2) * K:(i // 2) * K + K],
                               group(g)[:, 0:NKH].rearrange("p (b k) -> p b k", k=K)).then_inc(first_done[g % 8], 1)

            dve.wait_ge(bias0_done, 1)
            for c in range(RC):
                for i in (1, 3):
                    g, n = G_VW + 4 * c + i, context_rows(c)
                    if i == 1 and c >= 2:
                        dve.wait_ge(vw_stored[c % 2], stored_by(c - 2))
                    ve.tensor_copy(vws[0:n, c % 2, i, :], group(g)[0:n, :]).then_inc(vw_dve, 1)

            def maximum(t, g, scores):
                h0, h1 = HEADS[g]
                dve.wait_ge(scores, t.n * 3 + g + 1)
                ve.tensor_reduce(mx[:, t.odd, h0:h1], bank[g][:, 0:(h1 - h0) * K].rearrange("p (h k) -> p h k", k=K),
                                 AX.X, ALU.max).then_inc(scores_max, 1)

            def minus_max(t, g, first, sub, heads):
                h0, h1 = HEADS[g]
                dve.wait_ge(scores_max, (first + t.n) * 3 + g + 1)
                ve.tensor_tensor(heads[:, h0:h1, :],
                                 bank[g][:, 0:(h1 - h0) * K].rearrange("p (h k) -> p h k", k=K),
                                 mx[:, t.odd, h0:h1].unsqueeze(2).broadcast_to([128, h1 - h0, K]),
                                 ALU.subtract).then_inc(sub, 1)

            chain_o, chain_ya = Chain(dve, a_chain, 1), Chain(dve, a_chain_y, 2)

            def by_key(t):
                return p[:, t.odd, :].rearrange("p (k h) -> p h k", h=H)

            def by_head(t):
                return p[:, t.odd, :].rearrange("p (h k) -> p h k", h=H)

            def mask_values(t, c):
                c0, c1 = CHUNKS[c]
                if c == 0:
                    wait(dve, a_ready[6], t.n - 1)
                    dve.wait_ge(a_values[t.odd], t.pairs(16 * KEYS) + 16 * KEYS)
                last = c == len(CHUNKS) - 1
                for j0, j1, n in ((c0, c1, 128),) if not last else ((c0, c1 - 1, 128), (c1 - 1, c1, KLAST)):
                    ins = ve.tensor_tensor(
                        vbd[0:n, t.odd, j0:j1, :].rearrange("p c (h o) -> p c h o", o=OW)[:, :, :, 0:HD],
                        vw[0:n, t.odd, j0:j1, :].rearrange("p c (h o) -> p c h o", o=HD),
                        vmask_s[0:n, :].rearrange("p (h o) -> p h o", o=HD).unsqueeze(1)
                        .broadcast_to([n, j1 - j0, H, HD]), ALU.mult)
                ins.then_inc(a_masked, 1)

            def step_a(t):
                q = t.back(2)
                heads = bank[6][:, 0:H * OW].rearrange("p (h o) -> p h o", o=OW)
                q1, last = t.back(1), t.back(3)
                yield 0
                if q.live():
                    dve.wait_ge(a_ready[6], q.n + 1)
                    chain_o.made(ve.reciprocal(rinv[:, q.odd, :], heads[:, :, HD]))
                yield .05
                if q1.live():
                    mask_values(q1, 0)
                yield .1
                if q.live():
                    chain_o.need(q, 1)
                    ve.tensor_tensor(o_n[:, q.odd, :, :], heads[:, :, 0:HD],
                                     rinv[:, q.odd, :].unsqueeze(2).broadcast_to([128, H, HD]),
                                     ALU.mult).then_inc(a_done[6], 1)
                yield .12
                if last.live():
                    normed(tile_of(xr, last), last, a_scale, a_xh, 1.0)
                yield 0.15
                if t.live():
                    maximum(t, 0, a_scores)
                if q1.live():
                    mask_values(q1, 1)
                yield 0.2
                if t.live():
                    maximum(t, 1, a_scores)
                    wait(dve, a_pt, (t.n - 1) * 3)
                    minus_max(t, 0, 0, a_sub, by_key(t))
                yield .3
                if q1.live():
                    mask_values(q1, 2)
                if t.live():
                    maximum(t, 2, a_scores)
                late = 0 if t.live() else .1
                yield 0.45 + late
                if q.live():
                    row = tile_of(xr, q)
                    dve.wait_ge(a_ready[7], q.n * 3 + 2)
                    ve.tensor_tensor(row, bank[7][:, 128:256], row, ALU.add).then_inc(a_done[7], 1)
                    dve.wait_ge(a_done[7], q.n * 3 + 2)
                yield .5 + late
                if t.live():
                    minus_max(t, 1, 0, a_sub, by_key(t))
                if q.live():
                    row_stats(chain_ya, q)
                yield 0.65
                if q.live():
                    chain_ya.need(q, 1)
                if t.live():
                    minus_max(t, 2, 0, a_sub, by_key(t))
                if q.live():
                    row_mean(chain_ya, q)
                yield .7
                if t.live():
                    dve.wait_ge(w1t_hi, t.n + 1)
                    e = bass.ds(t.n, 1)
                    ve.tensor_tensor(w1_lo[:, e, :].rearrange("p o f -> p (o f)"), bank[5][:, :],
                                     w1_hi[:, e, :].rearrange("p o f -> p (o f)").bitcast(f32),
                                     ALU.subtract).then_inc(w1t_done, 1)
                yield 0.8
                if q.live():
                    row_var(chain_ya, q, a_var)

            def before_b():
                for c in (RC - 2, RC - 1):
                    dve.wait_ge(vw_stored[c % 2], stored_by(c))

            def largest(chain, t, n):
                chain.made(ve.max(out=top[:, :], in_=lg[:, 0:n]))

            def mark_top(chain, t, neg_sem):
                chain.need(t, 2)
                ve.tensor_scalar(neg[:, t.odd:t.odd + 1], top[:, 0:1], -1.0, None, ALU.mult).then_inc(neg_sem, 1)
                chain.made(ve.tensor_copy(mark[:, 0:2], top[:, 0:2]))

            def without_top(chain, t, n):
                chain.made(ve.match_replace(out=lr[:, 0:n + 6], in_to_replace=mark[:, :],
                                            in_values=lg[:, 0:n + 6], imm_value=-BIG))

            def select(t, n, logits_done):
                ve.tensor_tensor(sel[:, 0:n], lr[:, 0:n], lg[:, 0:n], ALU.is_lt).then_inc(logits_done, 1)

            def selected(chain, t, n, logits_done, exp_sem):
                dve.wait_ge(logits_done, t.n + 1)
                dve.wait_ge(exp_sem, t.n + 1)
                chain.made(ve.tensor_tensor(es[:, 0:n], ee[:, t.odd, 0:n], sel[:, 0:n], ALU.mult))

            chain_rb, chain_yb = Chain(dve, b_chain, 10), Chain(dve, b_chain_y, 2)

            def low_half(t, hi_sem, done_sem):
                dve.wait_ge(hi_sem, t.n + 1)
                ve.tensor_tensor(lhs_lo[:, t.odd, :], columns(xn_t, t, S), lhs_hi[:, t.odd, :].bitcast(f32),
                                 ALU.subtract).then_inc(done_sem, 1)

            def gated(t, e):
                dve.wait_ge(b_tanh, t.n * E0 + e + 1)
                if e < EP:
                    wait(dve, b_part, (t.n - 1) * 2 + 1)
                else:
                    wait(dve, b_sum, (t.n - 1) * (E0 - EP) + e - EP + 1)
                ve.scalar_tensor_tensor(out=ub[:, e, :], in0=th[:, e % 4, :], scalar=1.0,
                                        in1=bank[e % 4][:, 0:F0], op0=ALU.add, op1=ALU.mult).then_inc(b_u, 1)

            def add_expert(q, k):
                if k == 0:
                    dve.wait_ge(b_acc, q.n + 1)
                    dve.wait_ge(b_u, q.n * E0 + E0)
                wait(dve, b_sum, q.n * (E0 - EP) + k)
                ve.scalar_tensor_tensor(out=gb[:, q.odd, :], in0=ub[:, EP + k, :],
                                        scalar=comb[:, q.odd, EP + k:EP + k + 1], in1=gb[:, q.odd, :],
                                        op0=ALU.mult, op1=ALU.add).then_inc(b_sum, 1)

            def step_b(ahead):
                t, q1, q2, q3 = ahead.back(1), ahead.back(2), ahead.back(3), ahead.back(4)
                yield 0
                if q1.live():
                    gated(q1, 6)
                if q3.live():
                    dve.wait_ge(b_y_done, q3.n + 1)
                if q1.live():
                    gated(q1, 7)
                if q3.live():
                    row_stats(chain_yb, q3)
                yield .15
                if t.live():
                    dve.wait_ge(b_lg, t.n + 1)
                    chain_rb.made(ve.tensor_copy(lg[:, 0:E0], bank[4][:, 0:E0]))
                if q3.live():
                    chain_yb.need(q3, 1)
                yield .2
                if t.live():
                    chain_rb.need(t, 1)
                    gated(t, 0)
                    largest(chain_rb, t, E0)
                if q3.live():
                    row_mean(chain_yb, q3)
                yield .3
                if t.live():
                    mark_top(chain_rb, t, b_neg)
                if q3.live():
                    row_var(chain_yb, q3, b_var, True)
                if t.live():
                    chain_rb.need(t, 3)
                    gated(t, 1)
                    without_top(chain_rb, t, E0)
                yield .45
                if t.live():
                    chain_rb.need(t, 4)
                    select(t, E0, b_lg_done)
                    gated(t, 2)
                    selected(chain_rb, t, E0, b_lg_done, b_exp)
                if q3.live():
                    normed(tile_of(xr, q3), q3, b_scale, b_xh, 1.0)
                yield .6
                if t.live():
                    chain_rb.need(t, 5)
                    chain_rb.made(ve.tensor_reduce(s2[:, 0:1], es[:, 0:E0], AX.X, ALU.add))
                    gated(t, 3)
                    chain_rb.need(t, 6)
                    chain_rb.made(ve.scalar_tensor_tensor(out=s2[:, 1:2], in0=ssum[:, t.odd:t.odd + 1],
                                                          scalar=EPS_TOP, in1=s2[:, 0:1],
                                                          op0=ALU.mult, op1=ALU.add))
                yield .75
                if t.live():
                    chain_rb.need(t, 7)
                    chain_rb.made(ve.reciprocal(s2[:, 2:3], s2[:, 1:2]))
                if ahead.live():
                    low_half(ahead, b_prep_hi, b_prep)
                if q1.live():
                    add_expert(q1, 0)
                if t.live():
                    chain_rb.need(t, 8)
                    ve.tensor_scalar(comb[:, t.odd, 0:E0], es[:, 0:E0], s2[:, 2:3], 0.5,
                                     ALU.mult, ALU.mult).then_inc(b_comb, 1)
                    chain_rb.made(ve.tensor_tensor(csum[:, t.odd:t.odd + 1], s2[:, 0:1], s2[:, 2:3], ALU.mult))
                    gated(t, 4)
                if q1.live():
                    add_expert(q1, 1)
                if t.live():
                    chain_rb.need(t, 9)
                    row = tile_of(xr, t)
                    chain_rb.made(ve.scalar_tensor_tensor(out=row, in0=rows_s[:, 1, :],
                                                          scalar=csum[:, t.odd:t.odd + 1], in1=row,
                                                          op0=ALU.mult, op1=ALU.add))
                if q1.live():
                    add_expert(q1, 2)
                yield .9
                if q2.live():
                    dve.wait_ge(b_y, q2.n + 1)
                    chain_rb.need(q2, 10)
                    row = tile_of(xr, q2)
                    ve.tensor_tensor(row, bank[6][:, 0:D], row, ALU.add).then_inc(b_y_done, 1)
                if t.live():
                    gated(t, 5)
                if q1.live():
                    add_expert(q1, 3)

            chain_yc = Chain(dve, c_chain_y, 2)

            def row_sum(t, g):
                h0, h1 = HEADS[g]
                dve.wait_ge(c_exp, t.n * 3 + g + 1)
                ins = ve.tensor_reduce(rs[:, t.odd, h0:h1],
                                       p[:, t.odd, h0 * K:h1 * K].rearrange("p (h k) -> p h k", k=K),
                                       AX.X, ALU.add)
                if g == len(HEADS) - 1:
                    ins.then_inc(c_chain, 1)

            def step_c(t):
                q1, q = t.back(1), t.back(3)
                yield 0
                if q1.live():
                    for g in range(len(HEADS)):
                        row_sum(q1, g)
                yield .15
                if q.live():
                    dve.wait_ge(c_y, q.n + 1)
                    row = tile_of(xr, q)
                    ve.tensor_tensor(row, bank[5][:, 0:D], row, ALU.add).then_inc(c_y_done, 1)
                yield .2
                if q1.live():
                    dve.wait_ge(c_chain, q1.n + 1)
                    wait(dve, c_norm, q1.n - 1)
                    ve.reciprocal(rinv[:, q1.odd, :], rs[:, q1.odd, :]).then_inc(c_rs, 1)
                yield .25
                if t.live():
                    maximum(t, 0, c_scores)
                if q.live():
                    dve.wait_ge(c_y_done, q.n + 1)
                yield .35
                if t.live():
                    maximum(t, 1, c_scores)
                if q.live():
                    row_stats(chain_yc, q)
                yield .45
                if t.live():
                    maximum(t, 2, c_scores)
                if q.live():
                    chain_yc.need(q, 1)
                yield .5
                if t.live():
                    wait(dve, c_pt, (t.n - 1) * 3)
                    minus_max(t, 0, B, c_sub, by_head(t))
                if q.live():
                    row_mean(chain_yc, q)
                yield .6
                if t.live():
                    minus_max(t, 1, B, c_sub, by_head(t))
                if q.live():
                    row_var(chain_yc, q, c_var)
                yield .7
                if t.live():
                    minus_max(t, 2, B, c_sub, by_head(t))
                yield .85
                if q.live():
                    normed(tile_of(xr, q), q, c_scale, c_xh)

            chain_rd = Chain(dve, d_chain, 7)

            def before_d():
                link(ve.memset(lg[:, E1:24], BIG))

            def gate(t, h):
                dve.wait_ge(d_tanh, t.n * 2 + h + 1)
                ve.scalar_tensor_tensor(out=z1[:, h, :], in0=tg[:, h, :], scalar=1.0, in1=bank[2 * h][:, :],
                                        op0=ALU.add, op1=ALU.mult).then_inc(d_z1, 1)

            def gate_times_up(t, h):
                dve.wait_ge(d_z1, t.n * 2 + h + 1)
                wait(dve, d_mul, (t.n - 1) * 2 + h + 1)
                ve.tensor_tensor(z2[:, h, :], z1[:, h, :], bank[2 * h + 1][:, :], ALU.mult).then_inc(d_z, 1)

            def step_d(ahead):
                t, q, q2 = ahead.back(1), ahead.back(2), ahead.back(3)
                yield 0.1
                if q.live():
                    gate(q, 1)
                yield 0.15
                if t.live():
                    dve.wait_ge(d_sh, t.n + 1)
                    chain_rd.made(ve.tensor_copy(lg[:, 0:E1], bank[4][:, 2 * FS:2 * FS + E1]))
                yield 0.2
                if q2.live():
                    wait(dve, d_out[q2.odd], q2.pairs(16))
                    dve.wait_ge(d_y, q2.n + 1)
                    ve.tensor_tensor(yb[:, q2.odd, :], bank[7][:, 0:D], tile_of(xr, q2), ALU.add).then_inc(d_y_done, 1)
                yield 0.25
                if t.live():
                    chain_rd.need(t, 1)
                if q.live():
                    gate_times_up(q, 1)
                yield 0.4
                if t.live():
                    largest(chain_rd, t, E1)
                    mark_top(chain_rd, t, d_neg)
                    chain_rd.need(t, 3)
                    dve.wait_ge(d_tanh_sh, t.n + 1)
                    chain_rd.made(ve.scalar_tensor_tensor(out=z1[:, 2, 0:FS], in0=tg[:, 2, 0:FS], scalar=1.0,
                                                         in1=bank[4][:, 0:FS], op0=ALU.add, op1=ALU.mult))
                    without_top(chain_rd, t, E1)
                    wait(dve, d_it5, (t.n - 1) * 2)
                    chain_rd.need(t, 4)
                    ve.scalar_tensor_tensor(out=inter[:, t.odd, EI:EI + FS], in0=z1[:, 2, 0:FS], scalar=0.5,
                                            in1=bank[4][:, FS:2 * FS], op0=ALU.mult,
                                            op1=ALU.mult).then_inc(d_sh_done, 1)
                    chain_rd.need(t, 5)
                    select(t, E1, d_lg_done)
                    gate(t, 0)
                    selected(chain_rd, t, E1, d_lg_done, d_exp)
                    chain_rd.made(ve.reciprocal(s2[:, 2:3], ssum[:, t.odd:t.odd + 1]))
                yield 0.75
                if ahead.live():
                    low_half(ahead, d_prep_hi, d_prep)
                yield 0.8
                if t.live():
                    chain_rd.need(t, 7)
                    wait(dve, d_mul, (t.n - 1) * 2)
                    ve.tensor_scalar(comb[:, t.odd, :], es[:, :], s2[:, 2:3], 0.5,
                                     ALU.mult, ALU.mult).then_inc(d_comb, 1)
                    gate_times_up(t, 0)

            joined(dve, [Phase(START_A, 0, 3, step_a), Phase(START_B, 1, 4, step_b, before_b),
                         Phase(START_C, 0, 3, step_c), Phase(START_D, 1, 3, step_d, before_d)])

        @block.tensor
        def _(pe):
            te = nc.tensor

            def mm3(dst, a_hi_, a_lo_, b_hi_, b_lo_):
                te.matmul(dst, a_hi_, b_hi_, start=True, stop=False)
                te.matmul(dst, a_hi_, b_lo_, start=False, stop=False)
                return te.matmul(dst, a_lo_, b_hi_, start=False, stop=True)

            taken_by = {}

            def group(g):
                if g - 8 in taken_by:
                    pe.wait_ge(*taken_by[g - 8])
                elif g >= 8:
                    pe.wait_ge(first_done[g % 8], g // 8)
                return bank[g % 8]

            def ready(ins, g):
                ins.then_inc(first_ready[g % 8], 1)

            loaded(pe, "ctx", "w0")
            for i in range(2):
                ready(te.matmul(group(G_K + i)[:, 0:NKH], w0_s[:, 1, :], ctx_s[:, i * NKH:(i + 1) * NKH],
                                start=True, stop=True), G_K + i)
            loaded(pe, "bv")
            pe.wait_ge(one_done, 1)
            for i, chunks in enumerate((range(RC - 1), (RC - 1,))):
                dst = group(G_V + i)
                for c in chunks:
                    n = context_rows(c)
                    cut = dst[0:n, (c - chunks[0]) * D:(c - chunks[0] + 1) * D]
                    te.matmul(cut, one[0:1, 0:n], bv_s[0:1, :], start=True, stop=False)
                    last = te.matmul(cut, ctx_s[:, 128 * c:128 * c + n], w0_s[:, 2, :], start=False, stop=True)
                ready(last, G_V + i)
            loaded(pe, "wq")
            pe.wait_ge(tt_done, 1)
            for i in range(2):
                dst = group(G_WQ + i)
                for c in range(4):
                    j = 4 * i + c
                    last = te.matmul(dst[:, c * 128:(c + 1) * 128], wq_s[:, j * 128:(j + 1) * 128], tt[:, :],
                                     start=True, stop=True)
                ready(last, G_WQ + i)
            pe.wait_ge(bd_zero, 2)
            loaded(pe, "wk")
            for i in range(2):
                pe.wait_ge(first_done[(G_WQ + i) % 8], (G_WQ + i) // 8 + 1)
            for g0, lhs_w, rhs_w in ((G_A, wk_s, pair_q), (G_M, wv_s, pair_o)):
                if g0 == G_M:
                    loaded(pe, "wv")
                    pe.wait_ge(outw_done, 2)
                for i in range(4):
                    dst = group(g0 + i)
                    for c in range(2):
                        j = 2 * i + c
                        last = te.matmul(dst[:, c * 256:(c + 1) * 256], lhs_w[:, j, :],
                                         rhs_w[:, j, :, :].rearrange("p h d -> p (h d)"), start=True, stop=True)
                    ready(last, g0 + i)
            loaded(pe, "ident")
            for i in range(2):
                dst = group(G_XT + i)
                for c in range(4):
                    pe.wait_ge(xh0_done, 4 * i + c + 1)
                    last = te.transpose(dst[:, c * 128:(c + 1) * 128], xh0[:, 4 * i + c, :], id_s[:, 0, :])
                ready(last, G_XT + i)
            for i in range(2):
                dst = group(G_Q + i)
                pe.wait_ge(first_done[(G_XT + i) % 8], (G_XT + i) // 8 + 1)
                ready(te.matmul(dst[:, :], w0_s[:, 0, :], xn_t[:, i * 512:(i + 1) * 512], start=True, stop=True),
                      G_Q + i)
            pe.wait_ge(wg_done, 1)
            ready(te.transpose(group(G_WG)[:, 0:E0], wg_s[:, :], id_s[0:E0, 0, 0:E0]), G_WG)
            pe.wait_ge(ctx_split, 2)
            for i in range(4):
                pe.wait_ge(first_done[(G_A + i) % 8], (G_A + i) // 8 + 1)
            for h in range(H):
                for i in range(2):
                    g = G_B + 2 * h + i
                    cut = slice(h * D, h * D + D)
                    ready(mm3(group(g)[:, 0:NKH], a_hi[:, cut], a_lo[:, cut],
                              ctx_hi[:, i * NKH:(i + 1) * NKH], ctx_lo[:, i * NKH:(i + 1) * NKH]), g)
            for i in range(4):
                pe.wait_ge(first_done[(G_M + i) % 8], (G_M + i) // 8 + 1)
            for c in range(RC):
                n = context_rows(c)
                lines = slice(128 * c, 128 * c + n)
                for i in range(4):
                    g, cut = G_VW + 4 * c + i, slice(i * 512, (i + 1) * 512)
                    dst = group(g)[0:n, :]
                    if i % 2:
                        taken_by[g] = vw_dve, 2 * c + i // 2 + 1
                    else:
                        taken_by[g] = vw_act, 2 * c + i // 2 + 1
                    ready(mm3(dst, ctx_hi[:, lines], ctx_lo[:, lines], m_hi[:, cut], m_lo[:, cut]), g)

            pe.wait_ge(consts_done, 2)
            pe.wait_ge(ones_done, 2)

            def empty(t, i):
                taken(t, *taken_by[max(g for g in taken_by if g % 8 == i)])

            def taken(t, sem, value):
                if isinstance(t.n, int) and t.n == 0:
                    pe.wait_ge(sem, value)

            def scores_a(t, g):
                h0, h1 = HEADS[g]
                dst = bank[g][:, 0:(h1 - h0) * K]
                wait(pe, a_sub, (t.n - 1) * 3 + g + 1)
                empty(t, g)
                te.matmul(dst, lhs[:, t.odd, :], kbd[:, t.odd, h0 * K:h1 * K], start=True, stop=False)
                te.matmul(dst.rearrange("p (h k) -> p h k", k=K), idb[:, :],
                          maskneg[:, bass.ds(t.n, 1), :].broadcast_to([128, h1 - h0, K]),
                          start=False, stop=True).then_inc(a_scores, 1)

            def probs(q, c, b, ready, done, free):
                c0, c1 = CHUNKS[c]
                wait(pe, done, free)
                dst = bank[b]
                for j in range(c0, c1):
                    m = rows_of(j)
                    last = te.transpose(dst[0:m, (j - c0) * 128:(j - c0 + 1) * 128],
                                        p[:, q.odd, j * 128:j * 128 + m], id_s[:, 0, :])
                last.then_inc(ready, 1)

            def step_a(t):
                q1, q2, q3 = t.back(1), t.back(2), t.back(3)

                def probs_a(c):
                    if q1.live():
                        if c == 0:
                            pe.wait_ge(a_exp, q1.n * 3 + 3)
                        empty(q1, PT_BANKS_A[c])
                        free = q1.n * 3 + 1 if c == 2 else (q1.n - 1) * 3 + (3, 2)[c]
                        probs(q1, c, PT_BANKS_A[c], a_pt, a_pt_done, free)

                yield 0
                if t.live():
                    pe.wait_ge(a_prep, t.n + 1)
                    scores_a(t, 0)
                yield .05
                probs_a(0)
                yield .08
                if t.live():
                    scores_a(t, 1)
                late = 0 if t.live() else .4
                yield .1 + late
                if q3.live():
                    pe.wait_ge(a_xh, q3.n + 1)
                    te.transpose(bank[7][:, 256:384], xh[:, q3.odd, :], id_s[:, 0, :]).then_inc(a_ready[7], 1)
                yield .12
                probs_a(1)
                yield .15 + late
                if q2.live():
                    pe.wait_ge(a_done[6], q2.n + 1)
                    wait(pe, a_done[7], q2.n * 3)
                    empty(q2, 7)
                    te.transpose(bank[7][:, 0:128], o_n[:, q2.odd, :, :].rearrange("p h o -> p (h o)"),
                                 id_s[:, 0, :]).then_inc(a_ready[7], 1)
                yield .25
                if t.live():
                    scores_a(t, 2)
                yield .27
                probs_a(2)
                yield .3
                if t.live():
                    pe.wait_ge(w1_done, t.n + 1)
                    wait(pe, w1t_done, t.n)
                    empty(t, 5)
                    for j in range(4):
                        last = te.transpose(bank[5][:, j * 128:(j + 1) * 128], w1f[:, j, :], id_s[:, 0, :])
                    last.then_inc(w1t_ready, 1)
                yield .32 + late
                if q2.live():
                    pe.wait_ge(a_done[7], q2.n * 3 + 1)
                    te.matmul(bank[7][:, 128:256], ot[:, q2.odd, 0:128], w0_s[:, 3, :],
                              start=True, stop=True).then_inc(a_ready[7], 1)
                for c in range(len(CHUNKS)):
                    yield .55 + .1 * c
                    if q1.live():
                        if c == 0:
                            pe.wait_ge(a_masked, (q1.n + 1) * len(CHUNKS))
                            wait(pe, a_done[6], q1.n)
                        pe.wait_ge(a_pt_done, q1.n * 3 + c + 1)
                        for j in range(*CHUNKS[c]):
                            m = rows_of(j)
                            last = te.matmul(bank[6][:, 0:H * OW], pt[0:m, q1.odd, j, :], vbd[0:m, q1.odd, j, :],
                                             start=(j == 0), stop=(j == KC - 1))
                        if c == len(CHUNKS) - 1:
                            last.then_inc(a_ready[6], 1)

            def before_b():
                pe.wait_ge(first_done[G_WG % 8], G_WG // 8 + 1)
                pe.wait_ge(w1t_done, B)
                loaded(pe, "wo0")

            def experts(t, e0, e1):
                for e in range(e0, e1):
                    if e < 3:
                        taken(t, a_sub, (B - 1) * 3 + e + 1)
                    elif e == 3:
                        taken(t, a_pt_done, B * 3)
                    wait(pe, b_u, t.n * E0 + e - 3)
                    mm3(bank[e % 4][:, :], lhs_hi[:, t.odd, :], lhs_lo[:, t.odd, :], w1_hi[:, e, :],
                        w1_lo[:, e, :]).then_inc(b_h, 1)

            def step_b(t):
                q2, q3 = t.back(2), t.back(3)
                yield .05
                if t.live():
                    pe.wait_ge(b_prep, t.n + 1)
                    taken(t, a_pt_done, (B - 1) * 3 + 2)
                    wait(pe, b_lg_done, t.n)
                    te.matmul(bank[4][:, 0:E0], lhs_hi[:, t.odd, :].bitcast(f32), wgt[:, :], start=True, stop=False)
                    te.matmul(bank[4][:, 0:E0], lhs_lo[:, t.odd, :].bitcast(f32), wgt[:, :], start=False,
                              stop=True).then_inc(b_lg, 1)
                    experts(t, 0, 1)
                yield .2
                if t.live():
                    experts(t, 1, 2)
                if q2.live():
                    pe.wait_ge(b_sum, (q2.n + 1) * (E0 - EP))
                    wait(pe, b_gt_done, q2.n)
                    for c in range(2):
                        last = te.transpose(bank[5][:, c * 128:(c + 1) * 128],
                                            gb[:, q2.odd, c * 128:(c + 1) * 128], id_s[:, 0, :])
                    last.then_inc(b_gt, 1)
                yield .35
                if t.live():
                    experts(t, 2, 3)
                yield .5
                if t.live():
                    experts(t, 3, 4)
                yield .5 if t.live() else .5
                if q2.live():
                    pe.wait_ge(b_gt_done, q2.n + 1)
                    wait(pe, b_y_done, q2.n)
                    taken(q2, a_done[6], B)
                    te.matmul(bank[6][:, 0:D], ot[:, q2.odd, 0:128], wo0_s[:, 0, :], start=True, stop=False)
                    te.matmul(bank[6][:, 0:D], ot[:, q2.odd, 128:256], wo0_s[:, 1, :], start=False,
                              stop=True).then_inc(b_y, 1)
                yield .6
                if t.live():
                    experts(t, 4, 5)
                yield .7
                if t.live():
                    experts(t, 5, 6)
                if q3.live():
                    pe.wait_ge(b_xh, q3.n + 1)
                    wait(pe, b_xt_done, q3.n)
                    taken(q3, a_done[7], B * 3)
                    te.transpose(bank[7][:, 0:128], xh[:, q3.odd, :], id_s[:, 0, :]).then_inc(b_xt, 1)
                yield .8
                if t.live():
                    experts(t, 6, 7)
                yield .9
                if t.live():
                    experts(t, 7, E0)

            def step_c(t):
                q2, q3 = t.back(2), t.back(3)
                for g, (h0, h1) in enumerate(HEADS):
                    yield .1 * g
                    if t.live():
                        if g == 0:
                            pe.wait_ge(c_prep, t.n + 1)
                        wait(pe, c_sub, (t.n - 1) * 3 + g + 1)
                        taken(t, b_u, (B - 1) * E0 + 5 + g)
                        te.matmul(bank[g][:, 0:(h1 - h0) * K], lhs[:, t.odd, :],
                                  b_all[:, bass.ds(t.n, 1), h0 * K:h1 * K].rearrange("p o k -> p (o k)"),
                                  start=True, stop=True).then_inc(c_scores, 1)
                for c in range(len(CHUNKS)):
                    yield .3 + .08 * c
                    if q2.live():
                        if c == 0:
                            pe.wait_ge(c_norm, q2.n + 1)
                            taken(q2, b_u, B * E0)
                            taken(q2, b_lg_done, B)
                        if c == 2:
                            taken(q2, b_xt_done, B)
                        probs(q2, c, PT_BANKS[c], c_pt, c_pt_done, (q2.n - 1) * 3 + c + 1)
                for c in range(len(CHUNKS)):
                    yield .6 + .1 * c
                    if q2.live():
                        if c == 0:
                            pe.wait_ge(c_vw[q2.odd], q2.pairs(32) + 32)
                            wait(pe, c_y_done, q2.n)
                            taken(q2, b_gt_done, B)
                            taken(q2, c_bias0, 1)
                            te.matmul(bank[5][:, 0:D], one[0:1, :], rows_s[0:1, 2, :], start=True, stop=False)
                        pe.wait_ge(c_pt_done, q2.n * 3 + c + 1)
                        for j in range(*CHUNKS[c]):
                            m = rows_of(j)
                            last = te.matmul(bank[5][:, 0:D], pt[0:m, q2.odd, j, :], vw[0:m, q2.odd, j, :],
                                             start=False, stop=(j == KC - 1))
                        if c == len(CHUNKS) - 1:
                            last.then_inc(c_y, 1)
                yield .95
                if q3.live():
                    pe.wait_ge(c_xh, q3.n + 1)
                    wait(pe, c_xt_done, q3.n)
                    taken(q3, b_y_done, B)
                    te.transpose(bank[6][:, 0:128], xh[:, q3.odd, :], id_s[:, 0, :]).then_inc(c_xt, 1)

            def before_d():
                pe.wait_ge(wide_done, B)
                loaded(pe, "down")

            def wide(t, dst, at, n):
                return mm3(dst, lhs_hi[:, t.odd, :], lhs_lo[:, t.odd, :], wide_hi[:, at:at + n], wide_lo[:, at:at + n])

            def step_d(t):
                q = t.back(1)

                def inner(c, b, ready, done, n):
                    c0, c1 = ICHUNKS[c]
                    wait(pe, done, n)
                    for j in range(c0, c1):
                        last = te.transpose(bank[b][:, (j - c0) * 128:(j - c0 + 1) * 128],
                                            inter[:, q.odd, j * 128:(j + 1) * 128], id_s[:, 0, :])
                    last.then_inc(ready, 1)

                def gate_up(h, up):
                    if not up:
                        wait(pe, d_z, (t.n - 1) * 2 + h + 1)
                    last = wide(t, bank[2 * h + up][:, :], up * EI + h * 512, 512)
                    if up:
                        last.then_inc(d_gu, 1)

                yield 0
                if t.live():
                    pe.wait_ge(d_prep, t.n + 1)
                    taken(t, c_sub, B * 3)
                    taken(t, c_pt_done, (B - 1) * 3 + 2)
                    wait(pe, d_lg_done, t.n)
                    wait(pe, d_sh_done, t.n)
                    wide(t, bank[4][:, 0:2 * FS + E1], 2 * EI, 2 * FS + E1).then_inc(d_sh, 1)
                yield 0.15
                if t.live():
                    gate_up(0, 0)
                    gate_up(0, 1)
                yield .35
                if q.live():
                    pe.wait_ge(d_mul, q.n * 2 + 1)
                    taken(q, c_y_done, B)
                    inner(0, 5, d_it5, d_it5_done, q.n * 2)
                yield .4
                if t.live():
                    gate_up(1, 0)
                yield 0.5
                if q.live():
                    pe.wait_ge(d_mul, q.n * 2 + 2)
                    taken(q, c_xt_done, B)
                    pe.wait_ge(d_sh_done, q.n + 1)
                    inner(1, 6, d_it6, d_it6_done, q.n)
                    inner(2, 5, d_it5, d_it5_done, q.n * 2 + 1)
                yield 0.6
                if t.live():
                    gate_up(1, 1)
                yield 0.8
                if q.live():
                    pe.wait_ge(d_it5_done, q.n * 2 + 2)
                    pe.wait_ge(d_it6_done, q.n + 1)
                    wait(pe, d_y_done, q.n)
                    taken(q, c_pt_done, B * 3)
                    for j in range(IC):
                        last = te.matmul(bank[7][:, 0:D], it[:, q.odd, j, :], down_s[:, j, :],
                                         start=(j == 0), stop=(j == IC - 1))
                    last.then_inc(d_y, 1)

            joined(pe, [Phase(START_A, 0, 3, step_a), Phase(START_B, 0, 3, step_b, before_b),
                        Phase(START_C, 0, 3, step_c), Phase(START_D, 0, 1, step_d, before_d)])


def kernel(x, ctx_1024, mask_Bx1xSxS2_bk1, L0_xattn_Wq, L0_xattn_bq, L0_xattn_Wk, L0_xattn_bk, L0_xattn_Wv,
           L0_xattn_bv, L0_xattn_Wo, L0_xattn_bo, L0_ffn_Wg, L0_ffn_W1, L0_ffn_b1, L0_ffn_Wo, L0_ffn_bo,
           L1_xattn_ln_gamma, L1_xattn_ln_beta, L1_xattn_w_q, L1_xattn_w_kv, L1_xattn_w_out, L1_xattn_b_out,
           L1_xattn_gate, L1_ffn_router_w, L1_ffn_gate_w, L1_ffn_up_w, L1_ffn_down_w, L1_ffn_shared_gate_w,
           L1_ffn_shared_up_w, L1_ffn_shared_down_w):
    import concourse.bacc as bacc
    import numpy as np
    from concourse.bass_utils import run_bass_kernel_spmd

    inner = H * 64
    pairs = lambda w: w.reshape(8, 128, D).transpose(1, 0, 2)
    eye = np.eye(128, dtype=np.float32)
    less_last = eye.copy()
    less_last[127, :] -= 1.0
    arrays = {
        "x": x.transpose(1, 0, 2),
        "ctx_t": ctx_1024.reshape(NK, D).T,
        "mask": mask_Bx1xSxS2_bk1[:, 0].transpose(1, 0, 2),
        "w0": np.stack([L0_xattn_Wq, L0_xattn_Wk, L0_xattn_Wv, L0_xattn_Wo], axis=1),
        "cols": np.stack([L0_xattn_bq, L0_xattn_bk, L1_xattn_ln_gamma, L1_xattn_ln_beta], axis=1),
        "bv": L0_xattn_bv.reshape(1, D),
        "rows": np.stack([L0_xattn_bo, L0_ffn_bo, L1_xattn_b_out]),
        "w1": L0_ffn_W1.reshape(32, 128, D).transpose(1, 0, 2),
        "b1": L0_ffn_b1.reshape(32, 128).T,
        "wg": L0_ffn_Wg,
        "wo0": L0_ffn_Wo.T.reshape(2, 128, D).transpose(1, 0, 2),
        "wq": L1_xattn_w_q,
        "wk": pairs(L1_xattn_w_kv[:, :inner].T),
        "wv": pairs(L1_xattn_w_kv[:, inner:].T),
        "wout": pairs(L1_xattn_w_out),
        "gate": L1_xattn_gate.reshape(1, 1),
        "gu": np.concatenate([L1_ffn_gate_w.transpose(1, 0, 2).reshape(D, EI),
                              L1_ffn_up_w.transpose(1, 0, 2).reshape(D, EI)], axis=1),
        "rsh": np.concatenate([L1_ffn_shared_gate_w, L1_ffn_shared_up_w, L1_ffn_router_w], axis=1),
        "down": np.concatenate([L1_ffn_down_w.reshape(EI, D), L1_ffn_shared_down_w]).reshape(IC, 128, D)
                .transpose(1, 0, 2),
        "ident": np.stack([eye, less_last], axis=1),
        "hmask": (np.arange(D)[:, None] // HD == np.arange(H)[None, :]).astype(np.float32),
        "vmask": np.arange(128)[:, None] % H == np.arange(D)[None, :] // HD,
    }
    nc = bacc.Bacc("TRN2", target_bir_lowering=False, num_devices=1)
    feeds, args = {}, {}
    for name, a in arrays.items():
        a = np.ascontiguousarray(a)
        feeds[name + "_in"] = a
        args[name] = nc.dram_tensor(name + "_in", a.shape, mybir.dt.from_np(a.dtype), kind="ExternalInput").ap()
    args["out"] = nc.dram_tensor("out_0", (B, S, D), mybir.dt.float32, kind="ExternalOutput").ap()
    build(nc, **args)
    return run_bass_kernel_spmd(nc, [feeds], core_ids=[0]).results[0]["out_0"]
```
